# Optimizing a Trainium2 kernel written in Bass

```python
import numpy as np
import jax
import jax.numpy as jnp

def _softmax(x, axis=-1):
    return jax.nn.softmax(x, axis=axis)

def _gelu(x):
    return jax.nn.gelu(x, approximate=True)

def _silu(x):
    return jax.nn.silu(x)

def _sigmoid(x):
    return jax.nn.sigmoid(x)

def _layernorm(x, axis=-1, eps=1e-05):
    m = jnp.mean(x, axis=axis, keepdims=True)
    v = jnp.var(x, axis=axis, keepdims=True)
    return (x - m) / jnp.sqrt(v + eps)

def _scatter_add(tgt, idx, src, axis=0):
    return tgt.at[idx].add(src)

def _segment_sum(src, seg, n):
    return jax.ops.segment_sum(src, seg, n)
kernel_name = 'mk_gnn_ffn_d4_gnn_r32_37ecf8'

def setup_inputs(seed: int=0):
    np.random.seed(seed)
    _w = jnp.asarray

    def _rec_inputs():
        import jax
        import jax.numpy as jnp
        _gk = jax.random.key(seed)
        x = -0.0002117 + 1 * jax.random.normal(jax.random.fold_in(_gk, 1), (3125, 256), jnp.float32)
        src = jax.random.randint(jax.random.fold_in(_gk, 2), (50000,), 0, 3125, jnp.int32)
        dst = jax.random.randint(jax.random.fold_in(_gk, 3), (50000,), 0, 3125, jnp.int32)
        _o = jnp.argsort(dst, stable=True)
        src = src[_o]
        dst = dst[_o]
        edge_attr_64 = -9.77346e-05 + 0.999888 * jax.random.normal(jax.random.fold_in(_gk, 12), (50000, 64), jnp.float32)
        return (x, src, dst, edge_attr_64)
    x, src, dst, edge_attr_64 = _rec_inputs()

    def _L0_gnn_setup():
        import jax, jax.numpy as jnp
        import numpy as np
        ALPHA = 0.2
        N_NODES = 3125
        N_EDGES = 50000
        NFEAT = 256
        HID = 64
        NHEADS = 4

        def _gat_head(x, src, dst, Wh, ah, n_nodes):
            hid = Wh.shape[1]
            h = x @ Wh
            h = jnp.where(jnp.isnan(h), 0.0, h)
            a1, a2 = (ah[0, :hid], ah[0, hid:])
            alpha_src = h @ a1
            alpha_dst = h @ a2
            s = alpha_src[src] + alpha_dst[dst]
            e = jnp.exp(-jax.nn.leaky_relu(s, ALPHA))
            e = jnp.where(jnp.isnan(e), 0.0, e)
            rowsum = jax.ops.segment_sum(e, src, num_segments=n_nodes)
            hp = jax.ops.segment_sum(e[:, None] * h[dst], src, num_segments=n_nodes)
            hp = jnp.where(jnp.isnan(hp), 0.0, hp)
            hp = hp / rowsum[:, None]
            hp = jnp.where(jnp.isnan(hp), 0.0, hp)
            return jax.nn.elu(hp)
        key = jax.random.key(seed)
        k1, k2, k3, k4 = jax.random.split(key, 4)
        x = jax.random.normal(k1, (N_NODES, NFEAT), dtype=jnp.float32)
        edge_index = jax.random.randint(k2, (2, N_EDGES), 0, N_NODES, dtype=jnp.int64)
        W = jax.random.normal(k3, (NHEADS, NFEAT, HID), dtype=jnp.float32) * (1.414 * np.sqrt(2.0 / (NFEAT + HID)))
        a = jax.random.normal(k4, (NHEADS, 1, 2 * HID), dtype=jnp.float32) * (1.414 * np.sqrt(2.0 / (1 + 2 * HID)))
        return {'x': x, 'edge_index': edge_index, 'W': W, 'a': a}
    _L0_gnn_all = _L0_gnn_setup()
    _L0_gnn_in = {k: v for k, v in _L0_gnn_all.items() if k in ('W', 'a')}
    del _L0_gnn_all

    def _L0_ffn_setup():
        import jax, jax.numpy as jnp
        import numpy as np
        E, D, H, TOP_K = (6, 256, 256, 2)
        ROUTER_H = D // 2
        key = jax.random.key(seed)
        ks = jax.random.split(key, 12)
        s = 1.0 / np.sqrt(D)
        sh = 1.0 / np.sqrt(H)
        sr = 1.0 / np.sqrt(ROUTER_H)
        return {'features': jax.random.normal(ks[0], (8, 128, D), dtype=jnp.float32), 'router_w1': jax.random.uniform(ks[1], (D, ROUTER_H), jnp.float32, -s, s), 'router_b1': jnp.zeros((ROUTER_H,), jnp.float32), 'router_w2': jax.random.uniform(ks[2], (ROUTER_H, E), jnp.float32, -sr, sr), 'router_b2': jnp.zeros((E,), jnp.float32), 'expert_w1': jax.random.uniform(ks[3], (E, D, H), jnp.float32, -s, s), 'expert_b1': jnp.zeros((E, H), jnp.float32), 'expert_w2': jax.random.uniform(ks[4], (E, H, H), jnp.float32, -sh, sh), 'expert_b2': jnp.zeros((E, H), jnp.float32), 'expert_w3': jax.random.uniform(ks[5], (E, H, D), jnp.float32, -sh, sh), 'expert_b3': jnp.zeros((E, D), jnp.float32)}
    _L0_ffn_all = _L0_ffn_setup()
    _L0_ffn_in = {k: v for k, v in _L0_ffn_all.items() if k in ('router_w1', 'router_b1', 'router_w2', 'router_b2', 'expert_w1', 'expert_b1', 'expert_w2', 'expert_b2', 'expert_w3', 'expert_b3')}
    del _L0_ffn_all

    def _L1_gnn_setup():
        import jax, jax.numpy as jnp
        import numpy as np
        N = 3125
        E = 50000
        C_IN = 256
        H = 2
        D = 128
        ALPHA = 0.2
        key = jax.random.key(seed)
        ks = jax.random.split(key, 5)
        x = jax.random.normal(ks[0], (N, C_IN), dtype=jnp.float32)
        edge_index = jax.random.randint(ks[1], (2, E), 0, N, dtype=jnp.int64)
        W = jax.random.normal(ks[2], (H, D, C_IN), dtype=jnp.float32) * 0.05
        b = jax.random.normal(ks[3], (H, D), dtype=jnp.float32) * 0.05
        a = jax.random.normal(ks[4], (H, 2 * D), dtype=jnp.float32) * 0.05
        return {'x': x, 'edge_index': edge_index, 'W': W, 'b': b, 'a': a, 'n': N}
    _L1_gnn_all = _L1_gnn_setup()
    _L1_gnn_in = {k: v for k, v in _L1_gnn_all.items() if k in ('W', 'b', 'a')}
    del _L1_gnn_all

    def _L1_ffn_setup():
        import jax, jax.numpy as jnp
        import numpy as np
        TOP_K = 2
        LN_EPS = 1e-05
        key = jax.random.key(seed)
        ks = jax.random.split(key, 8)
        B, S, D, E, H = (16, 1024, 256, 8, 1024)
        x = jax.random.normal(ks[0], (B, S, D), dtype=jnp.float32)
        Wr = jax.random.normal(ks[1], (D, E), dtype=jnp.float32) * 0.1
        br = jnp.zeros((E,), dtype=jnp.float32)
        ln_g = jnp.ones((E, D), dtype=jnp.float32)
        ln_b = jnp.zeros((E, D), dtype=jnp.float32)
        W1 = jax.random.normal(ks[2], (E, D, H), dtype=jnp.float32) * (1.0 / np.sqrt(D))
        b1 = jnp.zeros((E, H), dtype=jnp.float32)
        W2 = jax.random.normal(ks[3], (E, H, D), dtype=jnp.float32) * (1.0 / np.sqrt(H))
        b2 = jnp.zeros((E, D), dtype=jnp.float32)
        return {'x': x, 'Wr': Wr, 'br': br, 'ln_g': ln_g, 'ln_b': ln_b, 'W1': W1, 'b1': b1, 'W2': W2, 'b2': b2}
    _L1_ffn_all = _L1_ffn_setup()
    _L1_ffn_in = {k: v for k, v in _L1_ffn_all.items() if k in ('Wr', 'br', 'ln_g', 'ln_b', 'W1', 'b1', 'W2', 'b2')}
    del _L1_ffn_all

    def _L2_gnn_setup():
        import jax, jax.numpy as jnp
        import numpy as np
        N_NODES = 50000
        D = 256
        L = 2
        N_EDGES = 25000
        NEG_SLOPE = 0.2

        def _gat_conv(h, W_l, al, ar, b, src, dst, n):
            hp = h @ W_l
            el = hp @ al
            er = hp @ ar
            e = jax.nn.leaky_relu(el[src] + er[dst], NEG_SLOPE)
            emax = jax.ops.segment_max(e, dst, num_segments=n)
            ex = jnp.exp(e - emax[dst])
            denom = jax.ops.segment_sum(ex, dst, num_segments=n)
            alpha = ex / denom[dst]
            out = jax.ops.segment_sum(hp[src] * alpha[:, None], dst, num_segments=n)
            return out + b
        key = jax.random.key(seed)
        ks = jax.random.split(key, 8)
        x = jax.random.normal(ks[0], (N_NODES, D), dtype=jnp.float32)
        W = jax.random.normal(ks[1], (L, D, D), dtype=jnp.float32) * (1.0 / np.sqrt(D))
        attn_l = jax.random.normal(ks[2], (L, D), dtype=jnp.float32) * (1.0 / np.sqrt(D))
        attn_r = jax.random.normal(ks[3], (L, D), dtype=jnp.float32) * (1.0 / np.sqrt(D))
        bias = jnp.zeros((L, D), dtype=jnp.float32)
        src = jax.random.randint(ks[4], (N_EDGES,), 0, N_NODES, dtype=jnp.int32)
        dst = jax.random.randint(ks[5], (N_EDGES,), 0, N_NODES, dtype=jnp.int32)
        return {'x': x, 'W': W, 'attn_l': attn_l, 'attn_r': attn_r, 'bias': bias, 'src': src, 'dst': dst}
    _L2_gnn_all = _L2_gnn_setup()
    _L2_gnn_in = {k: v for k, v in _L2_gnn_all.items() if k in ('W', 'attn_l', 'attn_r', 'bias')}
    del _L2_gnn_all

    def _L2_ffn_setup():
        import jax, jax.numpy as jnp
        import numpy as np
        B, S, D = (8, 128, 256)
        H = 4 * D
        CAPACITY = 0.5
        key = jax.random.key(seed)
        ks = jax.random.split(key, 6)
        x = jax.random.normal(ks[0], (B, S, D), dtype=jnp.float32)
        attention_mask = jnp.zeros((B, 1, 1, S), dtype=jnp.float32)
        wr = jax.random.normal(ks[1], (D, 1), dtype=jnp.float32) * 0.02
        br = jnp.zeros((1,), dtype=jnp.float32)
        w1 = jax.random.normal(ks[2], (D, H), dtype=jnp.float32) * 0.02
        b1 = jnp.zeros((H,), dtype=jnp.float32)
        w2 = jax.random.normal(ks[3], (H, D), dtype=jnp.float32) * 0.02
        b2 = jnp.zeros((D,), dtype=jnp.float32)
        return {'x': x, 'attention_mask': attention_mask, 'wr': wr, 'br': br, 'w1': w1, 'b1': b1, 'w2': w2, 'b2': b2}
    _L2_ffn_all = _L2_ffn_setup()
    _L2_ffn_in = {k: v for k, v in _L2_ffn_all.items() if k in ('attention_mask', 'wr', 'br', 'w1', 'b1', 'w2', 'b2')}
    del _L2_ffn_all

    def _L3_gnn_setup():
        import jax, jax.numpy as jnp
        import numpy as np
        LN2 = 0.6931471805599453
        N_ATOMS = 50000
        N_PAIRS = 25000
        F = 256
        RBF = 64
        N_RES = 3
        key = jax.random.key(seed)
        ks = jax.random.split(key, 16)
        inp = {'atomic_embedding': jax.random.normal(ks[0], (N_ATOMS, F), dtype=jnp.float32), 'f_ij': jax.random.normal(ks[1], (N_PAIRS, RBF), dtype=jnp.float32), 'idx_i': jax.random.randint(ks[2], (N_PAIRS,), 0, N_ATOMS, dtype=jnp.int32), 'idx_j': jax.random.randint(ks[3], (N_PAIRS,), 0, N_ATOMS, dtype=jnp.int32), 'G': jax.random.normal(ks[4], (F, RBF), dtype=jnp.float32), 'Wi': jax.random.normal(ks[5], (F, F), dtype=jnp.float32) * 0.05, 'bi': jax.random.normal(ks[6], (F,), dtype=jnp.float32) * 0.05, 'Wj': jax.random.normal(ks[7], (F, F), dtype=jnp.float32) * 0.05, 'bj': jax.random.normal(ks[8], (F,), dtype=jnp.float32) * 0.05, 'res_w1': jax.random.normal(ks[9], (N_RES, F, F), dtype=jnp.float32) * 0.05, 'res_b1': jax.random.normal(ks[10], (N_RES, F), dtype=jnp.float32) * 0.05, 'res_w2': jax.random.normal(ks[11], (N_RES, F, F), dtype=jnp.float32) * 0.05, 'res_b2': jax.random.normal(ks[12], (N_RES, F), dtype=jnp.float32) * 0.05, 'Wv': jax.random.normal(ks[13], (F, F), dtype=jnp.float32) * 0.05, 'bv': jax.random.normal(ks[14], (F,), dtype=jnp.float32) * 0.05}
        return inp
    _L3_gnn_all = _L3_gnn_setup()
    _L3_gnn_in = {k: v for k, v in _L3_gnn_all.items() if k in ('G', 'Wi', 'bi', 'Wj', 'bj', 'res_w1', 'res_b1', 'res_w2', 'res_b2', 'Wv', 'bv')}
    del _L3_gnn_all

    def _L3_ffn_setup():
        import jax, jax.numpy as jnp
        import numpy as np
        B, N, D = (16, 128, 256)
        NUM_EXPERTS, TOP_K, HEADS = (4, 2, 4)
        N_EDGES = 32768
        LN_EPS = 1e-05

        def _layernorm(x, g, b):
            mu = x.mean(-1, keepdims=True)
            var = ((x - mu) ** 2).mean(-1, keepdims=True)
            return (x - mu) * jax.lax.rsqrt(var + LN_EPS) * g + b

        def _forward(x, edge_index, W_gat, att_src, att_dst, b_gat, ln_gamma, ln_beta, W1, b1, W2, b2):
            Bc, Nc, Dc = x.shape
            M = Bc * Nc
            x_flat = x.reshape(M, Dc)
            h = (x_flat @ W_gat).reshape(M, HEADS, NUM_EXPERTS)
            loops = jnp.arange(M, dtype=edge_index.dtype)
            src = jnp.concatenate([edge_index[0], loops])
            dst = jnp.concatenate([edge_index[1], loops])
            a_src = (h * att_src).sum(-1)
            a_dst = (h * att_dst).sum(-1)
            e = jax.nn.leaky_relu(a_src[src] + a_dst[dst], negative_slope=0.2)
            e_max = jax.ops.segment_max(e, dst, num_segments=M)
            ee = jnp.exp(e - e_max[dst])
            denom = jax.ops.segment_sum(ee, dst, num_segments=M)
            alpha = ee / (denom[dst] + 1e-16)
            msg = h[src] * alpha[:, :, None]
            agg = jax.ops.segment_sum(msg, dst, num_segments=M).reshape(M, HEADS * NUM_EXPERTS) + b_gat
            scores = _layernorm(agg, ln_gamma, ln_beta).reshape(M, HEADS, NUM_EXPERTS).mean(1)
            scores = scores.reshape(Bc, Nc, NUM_EXPERTS)
            topk_s, topk_i = jax.lax.top_k(scores, TOP_K)
            w = jax.nn.softmax(topk_s, axis=-1)
            out = jnp.zeros_like(x)
            for ei in range(NUM_EXPERTS):
                g = jnp.where(topk_i == ei, w, 0.0).sum(-1)
                hh = jax.nn.gelu(x @ W1[ei] + b1[ei], approximate=False)
                out = out + g[..., None] * (hh @ W2[ei] + b2[ei])
            return out
        key = jax.random.key(seed)
        ks = jax.random.split(key, 8)
        s = 0.05
        return {'x': jax.random.normal(ks[0], (B, N, D), jnp.float32), 'W_gat': jax.random.normal(ks[1], (D, HEADS * NUM_EXPERTS), jnp.float32) * s, 'att_src': jax.random.normal(ks[2], (HEADS, NUM_EXPERTS), jnp.float32) * s, 'att_dst': jax.random.normal(ks[3], (HEADS, NUM_EXPERTS), jnp.float32) * s, 'b_gat': jnp.zeros((HEADS * NUM_EXPERTS,), jnp.float32), 'ln_gamma': jnp.ones((HEADS * NUM_EXPERTS,), jnp.float32), 'ln_beta': jnp.zeros((HEADS * NUM_EXPERTS,), jnp.float32), 'W1': jax.random.normal(ks[4], (NUM_EXPERTS, D, 2 * D), jnp.float32) * s, 'b1': jnp.zeros((NUM_EXPERTS, 2 * D), jnp.float32), 'W2': jax.random.normal(ks[5], (NUM_EXPERTS, 2 * D, D), jnp.float32) * s, 'b2': jnp.zeros((NUM_EXPERTS, D), jnp.float32), 'edge_index': jax.random.randint(ks[6], (2, N_EDGES), 0, B * N, jnp.int32)}
    _L3_ffn_all = _L3_ffn_setup()
    _L3_ffn_in = {k: v for k, v in _L3_ffn_all.items() if k in ('W_gat', 'att_src', 'att_dst', 'b_gat', 'ln_gamma', 'ln_beta', 'W1', 'b1', 'W2', 'b2', 'edge_index')}
    del _L3_ffn_all
    return {'x': x, 'src': src, 'dst': dst, 'edge_attr_64': edge_attr_64, 'L0_gnn_W': _L0_gnn_in['W'], 'L0_gnn_a': _L0_gnn_in['a'], 'L0_ffn_router_w1': _L0_ffn_in['router_w1'], 'L0_ffn_router_b1': _L0_ffn_in['router_b1'], 'L0_ffn_router_w2': _L0_ffn_in['router_w2'], 'L0_ffn_router_b2': _L0_ffn_in['router_b2'], 'L0_ffn_expert_w1': _L0_ffn_in['expert_w1'], 'L0_ffn_expert_b1': _L0_ffn_in['expert_b1'], 'L0_ffn_expert_w2': _L0_ffn_in['expert_w2'], 'L0_ffn_expert_b2': _L0_ffn_in['expert_b2'], 'L0_ffn_expert_w3': _L0_ffn_in['expert_w3'], 'L0_ffn_expert_b3': _L0_ffn_in['expert_b3'], 'L1_gnn_W': _L1_gnn_in['W'], 'L1_gnn_b': _L1_gnn_in['b'], 'L1_gnn_a': _L1_gnn_in['a'], 'L1_ffn_Wr': _L1_ffn_in['Wr'], 'L1_ffn_br': _L1_ffn_in['br'], 'L1_ffn_ln_g': _L1_ffn_in['ln_g'], 'L1_ffn_ln_b': _L1_ffn_in['ln_b'], 'L1_ffn_W1': _L1_ffn_in['W1'], 'L1_ffn_b1': _L1_ffn_in['b1'], 'L1_ffn_W2': _L1_ffn_in['W2'], 'L1_ffn_b2': _L1_ffn_in['b2'], 'L2_gnn_W': _L2_gnn_in['W'], 'L2_gnn_attn_l': _L2_gnn_in['attn_l'], 'L2_gnn_attn_r': _L2_gnn_in['attn_r'], 'L2_gnn_bias': _L2_gnn_in['bias'], 'L2_ffn_attention_mask': _L2_ffn_in['attention_mask'], 'L2_ffn_wr': _L2_ffn_in['wr'], 'L2_ffn_br': _L2_ffn_in['br'], 'L2_ffn_w1': _L2_ffn_in['w1'], 'L2_ffn_b1': _L2_ffn_in['b1'], 'L2_ffn_w2': _L2_ffn_in['w2'], 'L2_ffn_b2': _L2_ffn_in['b2'], 'L3_gnn_G': _L3_gnn_in['G'], 'L3_gnn_Wi': _L3_gnn_in['Wi'], 'L3_gnn_bi': _L3_gnn_in['bi'], 'L3_gnn_Wj': _L3_gnn_in['Wj'], 'L3_gnn_bj': _L3_gnn_in['bj'], 'L3_gnn_res_w1': _L3_gnn_in['res_w1'], 'L3_gnn_res_b1': _L3_gnn_in['res_b1'], 'L3_gnn_res_w2': _L3_gnn_in['res_w2'], 'L3_gnn_res_b2': _L3_gnn_in['res_b2'], 'L3_gnn_Wv': _L3_gnn_in['Wv'], 'L3_gnn_bv': _L3_gnn_in['bv'], 'L3_ffn_W_gat': _L3_ffn_in['W_gat'], 'L3_ffn_att_src': _L3_ffn_in['att_src'], 'L3_ffn_att_dst': _L3_ffn_in['att_dst'], 'L3_ffn_b_gat': _L3_ffn_in['b_gat'], 'L3_ffn_ln_gamma': _L3_ffn_in['ln_gamma'], 'L3_ffn_ln_beta': _L3_ffn_in['ln_beta'], 'L3_ffn_W1': _L3_ffn_in['W1'], 'L3_ffn_b1': _L3_ffn_in['b1'], 'L3_ffn_W2': _L3_ffn_in['W2'], 'L3_ffn_b2': _L3_ffn_in['b2'], 'L3_ffn_edge_index': _L3_ffn_in['edge_index']}

def reference(x, src, dst, edge_attr_64, L0_gnn_W, L0_gnn_a, L0_ffn_router_w1, L0_ffn_router_b1, L0_ffn_router_w2, L0_ffn_router_b2, L0_ffn_expert_w1, L0_ffn_expert_b1, L0_ffn_expert_w2, L0_ffn_expert_b2, L0_ffn_expert_w3, L0_ffn_expert_b3, L1_gnn_W, L1_gnn_b, L1_gnn_a, L1_ffn_Wr, L1_ffn_br, L1_ffn_ln_g, L1_ffn_ln_b, L1_ffn_W1, L1_ffn_b1, L1_ffn_W2, L1_ffn_b2, L2_gnn_W, L2_gnn_attn_l, L2_gnn_attn_r, L2_gnn_bias, L2_ffn_attention_mask, L2_ffn_wr, L2_ffn_br, L2_ffn_w1, L2_ffn_b1, L2_ffn_w2, L2_ffn_b2, L3_gnn_G, L3_gnn_Wi, L3_gnn_bi, L3_gnn_Wj, L3_gnn_bj, L3_gnn_res_w1, L3_gnn_res_b1, L3_gnn_res_w2, L3_gnn_res_b2, L3_gnn_Wv, L3_gnn_bv, L3_ffn_W_gat, L3_ffn_att_src, L3_ffn_att_dst, L3_ffn_b_gat, L3_ffn_ln_gamma, L3_ffn_ln_beta, L3_ffn_W1, L3_ffn_b1, L3_ffn_W2, L3_ffn_b2, L3_ffn_edge_index):
    import jax
    import jax.numpy as jnp

    def _L0_gnn_ref(x, edge_index, W, a):
        import jax, jax.numpy as jnp
        import numpy as np
        ALPHA = 0.2
        N_NODES = 3125
        N_EDGES = 50000
        NFEAT = 256
        HID = 64
        NHEADS = 4

        def _gat_head(x, src, dst, Wh, ah, n_nodes):
            hid = Wh.shape[1]
            h = x @ Wh
            h = jnp.where(jnp.isnan(h), 0.0, h)
            a1, a2 = (ah[0, :hid], ah[0, hid:])
            alpha_src = h @ a1
            alpha_dst = h @ a2
            s = alpha_src[src] + alpha_dst[dst]
            e = jnp.exp(-jax.nn.leaky_relu(s, ALPHA))
            e = jnp.where(jnp.isnan(e), 0.0, e)
            rowsum = jax.ops.segment_sum(e, src, num_segments=n_nodes)
            hp = jax.ops.segment_sum(e[:, None] * h[dst], src, num_segments=n_nodes)
            hp = jnp.where(jnp.isnan(hp), 0.0, hp)
            hp = hp / rowsum[:, None]
            hp = jnp.where(jnp.isnan(hp), 0.0, hp)
            return jax.nn.elu(hp)
        n_nodes = x.shape[0]
        src, dst = (edge_index[0], edge_index[1])
        outs = [_gat_head(x, src, dst, W[h], a[h], n_nodes) for h in range(W.shape[0])]
        out = jnp.concatenate(outs, axis=1)
        return jax.nn.elu(out)

    def _L0_ffn_ref(features, router_w1, router_b1, router_w2, router_b2, expert_w1, expert_b1, expert_w2, expert_b2, expert_w3, expert_b3):
        import jax, jax.numpy as jnp
        import numpy as np
        E, D, H, TOP_K = (6, 256, 256, 2)
        ROUTER_H = D // 2
        rh = jax.nn.relu(features @ router_w1 + router_b1)
        expert_logits = jax.nn.softmax(rh @ router_w2 + router_b2, axis=-1)
        top_w, top_i = jax.lax.top_k(expert_logits, TOP_K)
        routing_weights = jax.nn.softmax(top_w, axis=-1)
        h1 = jax.nn.relu(jnp.einsum('bsd,edh->bseh', features, expert_w1) + expert_b1)
        h2 = jax.nn.relu(jnp.einsum('bseh,ehf->bsef', h1, expert_w2) + expert_b2)
        expert_out = jnp.einsum('bsef,efo->bseo', h2, expert_w3) + expert_b3
        sel = jnp.take_along_axis(expert_out, top_i[:, :, :, None], axis=2)
        combined = jnp.sum(sel * routing_weights[..., None], axis=2)
        return combined

    def _L1_gnn_ref(x, edge_index, W, b, a, n):
        import jax, jax.numpy as jnp
        import numpy as np
        N = 3125
        E = 50000
        C_IN = 256
        H = 2
        D = 128
        ALPHA = 0.2
        src = edge_index[0]
        dst = edge_index[1]

        def head(Wh, bh, ah):
            h = x @ Wh.T + bh
            s_src = h @ ah[:D]
            s_dst = h @ ah[D:]
            score = s_src[src] + s_dst[dst]
            lrelu = jnp.where(score > 0, score, ALPHA * score)
            e = jnp.exp(-lrelu)
            row_sum = jax.ops.segment_sum(e, src, num_segments=n)
            num = jax.ops.segment_sum(e[:, None] * h[dst], src, num_segments=n)
            h_prime = num / row_sum[:, None]
            return jax.nn.elu(h_prime)
        outs = jax.vmap(head)(W, b, a)
        return jnp.moveaxis(outs, 0, 1).reshape(x.shape[0], H * D)

    def _L1_ffn_ref(x, Wr, br, ln_g, ln_b, W1, b1, W2, b2):
        import jax, jax.numpy as jnp
        import numpy as np
        TOP_K = 2
        LN_EPS = 1e-05
        B, S, D = x.shape
        N = B * S
        xt = x.reshape(N, D)
        logits = xt @ Wr + br
        probs = jax.nn.softmax(logits, axis=-1)
        top_p, top_idx = jax.lax.top_k(probs, TOP_K)
        weights = top_p / top_p.sum(axis=-1, keepdims=True)
        mu = xt.mean(axis=-1, keepdims=True)
        var = ((xt - mu) ** 2).mean(axis=-1, keepdims=True)
        xn = (xt - mu) * jax.lax.rsqrt(var + LN_EPS)
        xe = xn[None, :, :] * ln_g[:, None, :] + ln_b[:, None, :]
        h = jax.nn.gelu(jnp.einsum('end,edh->enh', xe, W1) + b1[:, None, :], approximate=False)
        y = jnp.einsum('enh,ehd->end', h, W2) + b2[:, None, :]
        y_tok = jnp.transpose(y, (1, 0, 2))
        sel = jnp.take_along_axis(y_tok, top_idx[:, :, None], axis=1)
        out = (weights[:, :, None] * sel).sum(axis=1)
        return out.reshape(B, S, D)

    def _L2_gnn_ref(x, W, attn_l, attn_r, bias, src, dst):
        import jax, jax.numpy as jnp
        import numpy as np
        N_NODES = 50000
        D = 256
        L = 2
        N_EDGES = 25000
        NEG_SLOPE = 0.2

        def _gat_conv(h, W_l, al, ar, b, src, dst, n):
            hp = h @ W_l
            el = hp @ al
            er = hp @ ar
            e = jax.nn.leaky_relu(el[src] + er[dst], NEG_SLOPE)
            emax = jax.ops.segment_max(e, dst, num_segments=n)
            ex = jnp.exp(e - emax[dst])
            denom = jax.ops.segment_sum(ex, dst, num_segments=n)
            alpha = ex / denom[dst]
            out = jax.ops.segment_sum(hp[src] * alpha[:, None], dst, num_segments=n)
            return out + b
        n = x.shape[0]
        loops = jnp.arange(n, dtype=src.dtype)
        src_sl = jnp.concatenate([src, loops])
        dst_sl = jnp.concatenate([dst, loops])
        h = x
        n_layers = W.shape[0]
        for i in range(n_layers):
            h = _gat_conv(h, W[i], attn_l[i], attn_r[i], bias[i], src_sl, dst_sl, n)
            if i < n_layers - 1:
                h = jax.nn.relu(h)
        return h

    def _L2_ffn_ref(x, attention_mask, wr, br, w1, b1, w2, b2):
        import jax, jax.numpy as jnp
        import numpy as np
        B, S, D = (8, 128, 256)
        H = 4 * D
        CAPACITY = 0.5
        b, s, d = x.shape
        weights = (jnp.einsum('bsd,do->bso', x, wr) + br)[..., 0]
        k = max(1, int(CAPACITY * s))
        kk = k - 1 if k > 1 else 1
        _, idx = jax.lax.top_k(weights, k)
        sel_idx = idx[:, :kk]
        sel = jnp.take_along_axis(x, sel_idx[:, :, None], axis=1)
        h = jax.nn.gelu(jnp.einsum('bkd,dh->bkh', sel, w1) + b1)
        y = jnp.einsum('bkh,hd->bkd', h, w2) + b2
        w_sel = jnp.take_along_axis(weights, sel_idx, axis=1)
        y = y * w_sel[..., None]
        batch_idx = jnp.arange(b)[:, None]
        processed = jnp.zeros_like(x).at[batch_idx, sel_idx].set(y)
        return processed + x

    def _L3_gnn_ref(atomic_embedding, f_ij, idx_i, idx_j, G, Wi, bi, Wj, bj, res_w1, res_b1, res_w2, res_b2, Wv, bv):
        import jax, jax.numpy as jnp
        import numpy as np
        LN2 = 0.6931471805599453
        N_ATOMS = 50000
        N_PAIRS = 25000
        F = 256
        RBF = 64
        N_RES = 3
        sp = jax.nn.softplus
        x = sp(atomic_embedding) - LN2
        x_i_prime = sp(x @ Wi.T + bi)
        x_j_all = sp(x @ Wj.T + bj)
        x_j_prime = x_j_all[idx_j]
        f_ij_prime = f_ij @ G.T
        msg = x_j_prime * f_ij_prime
        summed = jax.ops.segment_sum(msg, idx_i, num_segments=atomic_embedding.shape[0])
        v = x_i_prime + summed
        for k in range(res_w1.shape[0]):
            h = sp(v @ res_w1[k].T + res_b1[k])
            v = v + h @ res_w2[k].T + res_b2[k]
        return sp(v) @ Wv.T + bv

    def _L3_ffn_ref(x, W_gat, att_src, att_dst, b_gat, ln_gamma, ln_beta, W1, b1, W2, b2, edge_index):
        import jax, jax.numpy as jnp
        import numpy as np
        B, N, D = (16, 128, 256)
        NUM_EXPERTS, TOP_K, HEADS = (4, 2, 4)
        N_EDGES = 32768
        LN_EPS = 1e-05

        def _layernorm(x, g, b):
            mu = x.mean(-1, keepdims=True)
            var = ((x - mu) ** 2).mean(-1, keepdims=True)
            return (x - mu) * jax.lax.rsqrt(var + LN_EPS) * g + b

        def _forward(x, edge_index, W_gat, att_src, att_dst, b_gat, ln_gamma, ln_beta, W1, b1, W2, b2):
            Bc, Nc, Dc = x.shape
            M = Bc * Nc
            x_flat = x.reshape(M, Dc)
            h = (x_flat @ W_gat).reshape(M, HEADS, NUM_EXPERTS)
            loops = jnp.arange(M, dtype=edge_index.dtype)
            src = jnp.concatenate([edge_index[0], loops])
            dst = jnp.concatenate([edge_index[1], loops])
            a_src = (h * att_src).sum(-1)
            a_dst = (h * att_dst).sum(-1)
            e = jax.nn.leaky_relu(a_src[src] + a_dst[dst], negative_slope=0.2)
            e_max = jax.ops.segment_max(e, dst, num_segments=M)
            ee = jnp.exp(e - e_max[dst])
            denom = jax.ops.segment_sum(ee, dst, num_segments=M)
            alpha = ee / (denom[dst] + 1e-16)
            msg = h[src] * alpha[:, :, None]
            agg = jax.ops.segment_sum(msg, dst, num_segments=M).reshape(M, HEADS * NUM_EXPERTS) + b_gat
            scores = _layernorm(agg, ln_gamma, ln_beta).reshape(M, HEADS, NUM_EXPERTS).mean(1)
            scores = scores.reshape(Bc, Nc, NUM_EXPERTS)
            topk_s, topk_i = jax.lax.top_k(scores, TOP_K)
            w = jax.nn.softmax(topk_s, axis=-1)
            out = jnp.zeros_like(x)
            for ei in range(NUM_EXPERTS):
                g = jnp.where(topk_i == ei, w, 0.0).sum(-1)
                hh = jax.nn.gelu(x @ W1[ei] + b1[ei], approximate=False)
                out = out + g[..., None] * (hh @ W2[ei] + b2[ei])
            return out
        return _forward(x, edge_index, W_gat, att_src, att_dst, b_gat, ln_gamma, ln_beta, W1, b1, W2, b2)
    edge_index = jnp.stack([src, dst])
    x = x + _L0_gnn_ref(_layernorm(x, axis=-1), edge_index, L0_gnn_W, L0_gnn_a)
    x = x + _L0_ffn_ref(_layernorm(x, axis=-1)[None], L0_ffn_router_w1, L0_ffn_router_b1, L0_ffn_router_w2, L0_ffn_router_b2, L0_ffn_expert_w1, L0_ffn_expert_b1, L0_ffn_expert_w2, L0_ffn_expert_b2, L0_ffn_expert_w3, L0_ffn_expert_b3)[0]
    x = x + _L1_gnn_ref(_layernorm(x, axis=-1), edge_index, L1_gnn_W, L1_gnn_b, L1_gnn_a, 3125)
    x = x + _L1_ffn_ref(_layernorm(x, axis=-1)[None], L1_ffn_Wr, L1_ffn_br, L1_ffn_ln_g, L1_ffn_ln_b, L1_ffn_W1, L1_ffn_b1, L1_ffn_W2, L1_ffn_b2)[0]
    x = x + _L2_gnn_ref(_layernorm(x, axis=-1), L2_gnn_W, L2_gnn_attn_l, L2_gnn_attn_r, L2_gnn_bias, src, dst)
    x = x + _L2_ffn_ref(_layernorm(x, axis=-1)[None], L2_ffn_attention_mask, L2_ffn_wr, L2_ffn_br, L2_ffn_w1, L2_ffn_b1, L2_ffn_w2, L2_ffn_b2)[0]
    x = x + _L3_gnn_ref(_layernorm(x, axis=-1), edge_attr_64, src, dst, L3_gnn_G, L3_gnn_Wi, L3_gnn_bi, L3_gnn_Wj, L3_gnn_bj, L3_gnn_res_w1, L3_gnn_res_b1, L3_gnn_res_w2, L3_gnn_res_b2, L3_gnn_Wv, L3_gnn_bv)
    x = x + _L3_ffn_ref(_layernorm(x, axis=-1)[None], L3_ffn_W_gat, L3_ffn_att_src, L3_ffn_att_dst, L3_ffn_b_gat, L3_ffn_ln_gamma, L3_ffn_ln_beta, L3_ffn_W1, L3_ffn_b1, L3_ffn_W2, L3_ffn_b2, L3_ffn_edge_index)[0]
    return x

_drawn_inputs = setup_inputs


def setup_inputs(seed=0):
    import zlib

    import numpy as np

    out = dict(_drawn_inputs(seed))
    spreads = {'L0_ffn_router_b1': (0.0, 0.474),
     'L0_ffn_router_b2': (0.0, 0.316),
     'L0_ffn_expert_b1': (0.0, 0.759),
     'L0_ffn_expert_b2': (0.0, 0.487),
     'L0_ffn_expert_b3': (0.0, 0.1),
     'L1_ffn_br': (0.0, 0.407),
     'L1_ffn_ln_g': (1.0, 0.568),
     'L1_ffn_ln_b': (0.0, 0.561),
     'L1_ffn_b1': (0.0, 0.58),
     'L1_ffn_b2': (0.0, 0.393),
     'L2_gnn_bias': (0.0, 0.288),
     'L2_ffn_b1': (0.0, 0.8),
     'L2_ffn_b2': (0.0, 0.8),
     'L3_ffn_b_gat': (0.0, 2.0),
     'L3_ffn_ln_gamma': (1.0, 0.6),
     'L3_ffn_ln_beta': (0.0, 2.0),
     'L3_ffn_b1': (0.0, 2.0),
     'L3_ffn_b2': (0.0, 2.0)}
    factors = {'L1_gnn_b': 3.316,
     'L2_gnn_attn_l': 5.396,
     'L2_gnn_attn_r': 8.0,
     'L2_ffn_wr': 8.0,
     'L2_ffn_w1': 8.0,
     'L2_ffn_w2': 8.0,
     'L3_gnn_Wi': 6.157,
     'L3_gnn_bi': 53.297,
     'L3_gnn_res_b1': 42.928,
     'L3_gnn_res_b2': 25.675,
     'L3_gnn_bv': 26.484,
     'L3_ffn_W_gat': 14.73,
     'L3_ffn_att_src': 28.106,
     'L3_ffn_att_dst': 64.0,
     'L3_ffn_W1': 3.14}
    for name, (base, spread) in spreads.items():
        noise = np.random.default_rng([zlib.crc32(name.encode()), seed]).standard_normal(out[name].shape)
        drawn = base * np.exp(spread * noise) if base else spread * noise
        out[name] = jnp.asarray(drawn.astype(out[name].dtype))
    for name, factor in factors.items():
        out[name] = (out[name] * factor).astype(out[name].dtype)
    return out
```

```python
from contextlib import ExitStack, contextmanager

import concourse.bass as bass
from concourse import mybir

P = 128
N = 3125
D = 256
NT = -(-N // P)
NP = NT * P
REST = N - (NT - 1) * P
G = 2
SLOTS = G * P
U = 8
TG = 5
TOK = TG * P
HALF = TOK // 2
NTG = NT // TG
SB = 8
LN_EPS = 1e-5
LN2 = 0.6931471805599453
BIG = 1e30

F32 = mybir.dt.float32
I32 = mybir.dt.int32
ALU = mybir.AluOpType
ACT = mybir.ActivationFunctionType
AX = mybir.AxisListType
RED = bass.bass_isa.ReduceOp
ds = bass.ds


class Stage:

    def __init__(self, nc, ctx, tag):
        self.nc, self.ctx, self.tag, self.sems, self.from_zero = nc, ctx, tag, [], []

    def sb(self, name, shape, dt=F32):
        return self.ctx.enter_context(self.nc.sbuf_tensor(f"{self.tag}_{name}", shape, dt))

    def ps(self, name, shape, dt=F32):
        return self.ctx.enter_context(self.nc.psum_tensor(f"{self.tag}_{name}", shape, dt))

    def sem(self, name):
        self.sems.append(self.nc.alloc_semaphore(f"{self.tag}_{name}"))
        return self.sems[-1]

    def gather_sem(self, name):
        self.from_zero.append(self.sem(name))
        return self.from_zero[-1]

    def block(self):
        for sem in self.sems:
            if not any(sem is z for z in self.from_zero):
                self.nc.gpsimd.sem_inc(sem, 1)
        self.nc.all_engine_barrier()
        return self.ctx.enter_context(self.nc.Block())


@contextmanager
def stage(nc, tag):
    with ExitStack() as ctx:
        st = Stage(nc, ctx, tag)
        yield st
    nc.clear_and_free_semaphores(st.sems)


def need(eng, sem, it, back):
    if isinstance(it, int):
        if it * U + back > 0:
            eng.wait_ge(sem, 1 + it * U + back)
    else:
        eng.wait_ge(sem, 1 + it * U + max(back, 0))


def ahead(part, it, j, *more):
    if not isinstance(it, int) or j >= 0:
        part(it, j, *more)


class Consts:
    pass


def groups_of(edges):
    most = (edges + NT * (SLOTS - 1)) // SLOTS
    return -(-most // U) * U + U


def setup(nc, k, x):
    with stage(nc, "set") as st:
        iota_i = st.sb("iota_i", [P, P], I32)
        zeroed, cast, made, loaded = (st.sem(s) for s in ("zeroed", "cast", "made", "loaded"))
        block = st.block()

        @block.gpsimd
        def _(pool):
            pool.memset(k.ident[:], 0.0).then_inc(zeroed, 1)
            pool.memset(k.tri[:], 0.0).then_inc(zeroed, 1)
            pool.memset(k.ones[:], 1.0).then_inc(zeroed, 1)
            pool.memset(k.X[:, NT - 1, :], 0.0).then_inc(zeroed, 1)
            pool.memset(k.past_end[:], 0.0).then_inc(zeroed, 1)
            pool.iota(iota_i[:], pattern=[[1, P]], base=0, channel_multiplier=0).then_inc(zeroed, 1)
            pool.wait_ge(zeroed, 1 + 6)
            pool.affine_select(out=k.ident[:], in_=k.ident[:], compare_op=ALU.not_equal, fill=1.0, base=0,
                               pattern=[[-1, P]], channel_multiplier=1).then_inc(made, 1)
            pool.affine_select(out=k.tri[:], in_=k.tri[:], compare_op=ALU.is_ge, fill=1.0, base=0,
                               pattern=[[-1, P]], channel_multiplier=1).then_inc(made, 1)
            pool.affine_select(out=k.past_end[:], in_=k.past_end[:], compare_op=ALU.is_ge, fill=1.0,
                               base=REST - 1, pattern=[[0, 1]], channel_multiplier=-1).then_inc(made, 1)
            pool.wait_ge(made, 1 + 3)

        @block.vector
        def _(dve):
            dve.wait_ge(zeroed, 1 + 6)
            dve.tensor_copy(k.iota[:], iota_i[:]).then_inc(cast, 1)
            dve.wait_ge(cast, 1 + 1)

        @block.sync
        def _(sp):
            full = (NT - 1) * P
            sp.dma_start(k.X[:, 0:NT - 1, :], x[0:full, :].rearrange("(t p) d -> p t d", p=P)).then_inc(loaded, 16)
            sp.wait_ge(zeroed, 1 + 6)
            sp.dma_start(k.X[0:REST, NT - 1, :], x[full:N, :]).then_inc(loaded, 16)
            sp.wait_ge(loaded, 1 + 32)


class Scatter:

    def __init__(self, st, name, row, rec, table, start, end):
        self.row, self.rec, self.table, self.start = row, rec, table, start
        self.batches = (end - start) // (2 * SB)
        self.idx = [st.sb(f"{name}_idx{s}", [row.shape[0], SB], I32) for s in range(2)]
        self.out = [st.sb(f"{name}_out{s}", [row.shape[0], SB, rec.shape[2]], I32) for s in range(2)]
        self.copied = st.sem(f"{name}_copied")
        self.scattered = [st.gather_sem(f"{name}_scattered{s}") for s in range(2)]

    def run(self, pool):
        def batch(it, s):
            c = it * (2 * SB) + (self.start + s * SB)
            if not isinstance(it, int):
                pool.wait_ge(self.scattered[s], it * (16 * SB))
                pool.nop(nofuse=True)
            pool.tensor_copy(self.idx[s][:], self.row[:, ds(c, SB)]).then_inc(self.copied, 1)
            pool.tensor_copy(self.out[s][:], self.rec[:, ds(c, SB), :]).then_inc(self.copied, 1)
            pool.wait_ge(self.copied, 1 + it * 4 + s * 2 + 2)
            pool.nop(nofuse=True)
            for j in range(SB):
                pool.indirect_dma_start(
                    out=self.table, out_offset=bass.IndirectOffsetOnAxis(ap=self.idx[s][:, j:j + 1], axis=0),
                    in_=self.out[s][:, j, :], in_offset=None).then_inc(self.scattered[s], 16)

        batch(0, 0)
        batch(0, 1)
        with pool.Fori(1, self.batches) as it:
            batch(it, 0)
            batch(it, 1)
        for s in range(2):
            pool.wait_ge(self.scattered[s], 16 * SB * self.batches)


def scatter_edges(nc, tag, jobs):
    with stage(nc, tag) as st:
        scatters = [Scatter(st, f"job{n}", *job) for n, job in enumerate(jobs)]
        block = st.block()

        @block.gpsimd
        def _(pool):
            for scatter in scatters:
                scatter.run(pool)


def place_edges(nc, k, tag, seg, oth, attr, table, row, rec, tile_of, jobs=()):
    pb, m = seg.shape
    rows, rw = table.shape
    c_all = rows // P
    n_groups = tile_of.shape[1]
    fill_cols = c_all // (U * G)
    batches = m // (2 * SB)
    with stage(nc, tag) as st:
        seg_i = st.sb("seg_i", [pb, m], I32)
        oth_i = st.sb("oth_i", [pb, m], I32)
        seg_f = st.sb("seg_f", [pb, m])
        tile_i = st.sb("tile_i", [pb, m], I32)
        tile_f = st.sb("tile_f", [pb, m])
        loc = st.sb("loc", [pb, m])
        ones_m = st.sb("ones_m", [pb, m])
        hit = st.sb("hit", [pb, 2, m])
        rank = st.sb("rank", [pb, 2, m])
        slot_f = st.sb("slot_f", [pb, m])
        slot_i = st.sb("slot_i", [pb, m], I32)
        part_i = st.sb("part_i", [pb, m], I32)
        col_i = st.sb("col_i", [pb, m], I32)
        count = st.sb("count", [pb, NT])
        tot_i = st.sb("tot_i", [P, NT], I32)
        tot_j = st.sb("tot_j", [P, NT], I32)
        n_grp = st.sb("n_grp", [P, NT])
        ones_t = st.sb("ones_t", [P, NT])
        end_g = st.sb("end_g", [P, NT])
        start = st.sb("start", [P, NT])
        g_i = st.sb("g_i", [1, n_groups], I32)
        g_f = st.sb("g_f", [1, n_groups])
        past = st.sb("past", [1, n_groups, NT])
        tile_r = st.sb("tile_r", [1, n_groups])
        fill = st.sb("fill", [P, fill_cols, rw], I32)
        psum = st.ps("psum", [P, 2, 512])

        loaded = st.sem("loaded")
        iota_made = st.sem("iota_made")
        v = st.sem("dve_order")
        counted = st.sem("counted")
        summed = st.sem("summed")
        hits = st.sem("hits")
        ranks = st.sem("ranks")
        placed = st.sem("placed")
        noted = st.sem("noted")
        fill_made = st.sem("fill_made")
        filled = st.sem("filled")
        attr_in = st.sem("attr_in")
        scatters = [Scatter(st, f"job{n}", *job) for n, job in enumerate(jobs)]
        block = st.block()

        @block.gpsimd
        def _(pool):
            pool.iota(g_i[:], pattern=[[1, n_groups]], base=0, channel_multiplier=0).then_inc(iota_made, 1)
            pool.memset(fill[:], 0).then_inc(fill_made, 1)
            pool.wait_ge(fill_made, 1 + 1)
            pool.memset(fill[:, :, 0:1], N).then_inc(fill_made, 1)
            pool.memset(fill[:, :, 1:2].bitcast(F32), -1.0).then_inc(fill_made, 1)
            for scatter in scatters:
                scatter.run(pool)

        @block.sync
        def _(sp):
            sp.dma_start(seg_i[:], seg).then_inc(loaded, 16)
            sp.dma_start(oth_i[:], oth).then_inc(loaded, 16)
            sp.wait_ge(fill_made, 1 + 3)
            by_part = table.rearrange("(p c) w -> p c w", p=P)
            for q in range(U * G):
                sp.dma_start(by_part[:, q * fill_cols:(q + 1) * fill_cols, :], fill[:]).then_inc(filled, 16)
            if attr is not None:
                for q in range(4):
                    w = m // 4
                    sp.dma_start(rec[:, q * w:(q + 1) * w, 2:rw], attr[:, q * w:(q + 1) * w, :]).then_inc(attr_in, 16)
                sp.wait_ge(attr_in, 1 + 64)
            sp.wait_ge(filled, 1 + 16 * U * G)

        @block.vector
        def _(dve):
            at = [0]

            def then(ins):
                at[0] += 1
                ins.then_inc(v, 1)
                dve.wait_ge(v, 1 + at[0])

            dve.wait_ge(loaded, 1 + 32)
            dve.tensor_copy(seg_f[:], seg_i[:]).then_inc(v, 1)
            dve.memset(ones_m[:], 1.0).then_inc(v, 1)
            dve.memset(ones_t[:], 1.0).then_inc(v, 1)
            dve.memset(slot_f[:], 0.0).then_inc(v, 1)
            at[0] = 4
            then(dve.tensor_scalar(tile_i[:], seg_i[:], 7, None, ALU.arith_shift_right))
            then(dve.tensor_copy(tile_f[:], tile_i[:]))
            then(dve.scalar_tensor_tensor(out=loc[:], in0=tile_f[:], scalar=-float(P), in1=seg_f[:],
                                          op0=ALU.mult, op1=ALU.add))
            with dve.Fori(0, NT) as b:
                dve.wait_ge(counted, 1 + b)
                dve.tensor_scalar(hit[:, 0, :], tile_f[:], k.iota[0:pb, ds(b, 1)], 0.0, ALU.is_equal, ALU.add,
                                  accum_out=count[:, ds(b, 1)]).then_inc(counted, 1)
            dve.wait_ge(summed, 1 + 2)
            then(dve.tensor_scalar(tot_i[:], psum[:, 1, 0:NT], float(SLOTS - 1), None, ALU.add))
            then(dve.tensor_scalar(tot_j[:], tot_i[:], SLOTS.bit_length() - 1, None, ALU.arith_shift_right))
            then(dve.tensor_copy(n_grp[:], tot_j[:]))
            then(dve.tensor_tensor_scan(end_g[:], ones_t[:], n_grp[:], 0.0, ALU.mult, ALU.add))
            then(dve.tensor_tensor(start[:], end_g[:], n_grp[:], ALU.subtract))
            then(dve.tensor_scalar(start[:], start[:], float(SLOTS), -1.0, ALU.mult, ALU.add))
            then(dve.tensor_tensor(start[0:pb, :], psum[0:pb, 0, 0:NT], start[0:pb, :], ALU.add))
            dve.wait_ge(iota_made, 1 + 1)
            then(dve.tensor_copy(g_f[:], g_i[:]))
            then(dve.tensor_tensor(past[:], g_f[:].unsqueeze(2).broadcast_to([1, n_groups, NT]),
                                   end_g[0:1, :].unsqueeze(1).broadcast_to([1, n_groups, NT]), ALU.is_ge))
            then(dve.tensor_reduce(tile_r[:], past[:], AX.X, ALU.add))
            then(dve.tensor_scalar(tile_of, tile_r[:], float(NT - 1), None, ALU.min))

            def place(b, h, first):
                if not first:
                    dve.wait_ge(placed, 1 + b - 1)
                dve.tensor_scalar(hit[:, h, :], tile_f[:], k.iota[0:pb, ds(b, 1)], None, ALU.is_equal)\
                   .then_inc(hits, 1)
                dve.wait_ge(hits, 1 + b + 1)
                dve.tensor_tensor_scan(rank[:, h, :], ones_m[:], hit[:, h, :], start[0:pb, ds(b, 1)],
                                       ALU.mult, ALU.add).then_inc(ranks, 1)
                dve.wait_ge(ranks, 1 + b + 1)
                dve.wait_ge(placed, 1 + b)
                dve.nop(nofuse=True)
                dve.copy_predicated(slot_f[:], hit[:, h, :].bitcast(I32), rank[:, h, :]).then_inc(placed, 1)

            place(0, 0, True)
            with dve.Fori(0, (NT - 1) // 2) as i:
                place(i * 2 + 1, 1, False)
                place(i * 2 + 2, 0, False)
            dve.wait_ge(placed, 1 + NT)
            then(dve.tensor_copy(slot_i[:], slot_f[:]))
            then(dve.tensor_scalar(part_i[:], slot_i[:], P - 1, None, ALU.bitwise_and))
            then(dve.tensor_scalar(col_i[:], slot_i[:], 7, None, ALU.arith_shift_right))
            then(dve.scalar_tensor_tensor(out=row, in0=part_i[:], scalar=float(c_all), in1=col_i[:],
                                          op0=ALU.mult, op1=ALU.add))
            dve.tensor_scalar(rec[:, :, 0:1], oth_i[:].unsqueeze(2), 0, None, ALU.add).then_inc(noted, 1)
            dve.tensor_scalar(rec[:, :, 1:2].bitcast(F32), loc[:].unsqueeze(2), 0.0, None, ALU.add).then_inc(noted, 1)
            dve.wait_ge(noted, 1 + 2)

        @block.tensor
        def _(pe):
            pe.wait_ge(counted, 1 + NT)
            pe.matmul(psum[0:pb, 0, 0:NT], k.tri[0:pb, 0:pb], count[:], start=True, stop=True).then_inc(summed, 1)
            pe.matmul(psum[:, 1, 0:NT], k.ones[0:pb, :], count[:], start=True, stop=True).then_inc(summed, 1)


def read_slots(nc, tag, table, other, local):
    c_all = table.shape[0] // P
    parts = 4
    w = c_all // parts
    with stage(nc, tag) as st:
        meta = st.sb("meta", [P, c_all, 2], I32)
        meta_in = [st.sem(f"meta_in{q}") for q in range(parts)]
        noted = st.sem("noted")
        block = st.block()

        @block.sync
        def _(sp):
            by_part = table.rearrange("(p c) w -> p c w", p=P)
            for q in range(parts):
                sp.dma_start(meta[:, q * w:(q + 1) * w, :], by_part[:, q * w:(q + 1) * w, 0:2]).then_inc(meta_in[q], 16)

        @block.vector
        def _(dve):
            for q in range(parts):
                dve.wait_ge(meta_in[q], 1 + 16)
                cols = slice(q * w, (q + 1) * w)
                dve.tensor_copy(other[:, cols], meta[:, cols, 0]).then_inc(noted, 1)
                dve.tensor_copy(local[:, cols], meta[:, cols, 1].bitcast(F32)).then_inc(noted, 1)
            dve.wait_ge(noted, 1 + 2 * parts)


class Norm:

    def __init__(self, st, name):
        self.stats = st.sb(f"{name}_stats", [P, TG, 6])
        self.mv = st.sb(f"{name}_mv", [P, TG, 2])
        self.ve = st.sb(f"{name}_ve", [P, TG])
        self.sd = st.sb(f"{name}_sd", [P, TG])
        self.rs = st.sb(f"{name}_rs", [P, TG])
        self.has_stats, self.has_mv, self.has_var, self.has_sd, self.has_rs, self.applied = (
            st.sem(f"{name}_{s}") for s in ("stats", "mv", "var", "sd", "rs", "applied"))

    def dve_first(self, dve, it, src):
        dve.wait_ge(self.applied, 1 + it * TG)
        for u in range(TG):
            dve.bn_stats(self.stats[:, u, :], src(u)).then_inc(self.has_stats, 1)
        for u in range(TG):
            dve.wait_ge(self.has_stats, 1 + it * TG + u + 1)
            dve.nop(nofuse=True)
            dve.bn_aggr(self.mv[:, u, :], self.stats[:, u, :]).then_inc(self.has_mv, 1)
        dve.wait_ge(self.has_mv, 1 + it * TG + TG)
        dve.tensor_scalar(self.ve[:], self.mv[:, :, 1], LN_EPS, None, ALU.add).then_inc(self.has_var, 1)

    def act_root(self, act, it):
        act.wait_ge(self.has_var, 1 + it + 1)
        act.activation(self.sd[:], self.ve[:], ACT.Sqrt).then_inc(self.has_sd, 1)

    def dve_apply(self, dve, it, src, dst):
        dve.wait_ge(self.has_sd, 1 + it + 1)
        dve.reciprocal(self.rs[:], self.sd[:]).then_inc(self.has_rs, 1)
        dve.wait_ge(self.has_rs, 1 + it + 1)
        for u in range(TG):
            dve.tensor_scalar(dst(u), src(u), self.mv[:, u, 0:1], self.rs[:, u:u + 1], ALU.subtract, ALU.mult)\
               .then_inc(self.applied, 1)



def tile_ids(nc, engine, tile_of, g):
    ap = tile_of[0:1, ds(g, U)]
    return nc.values_load_multi_w_load_instructions(ap, engines=(engine,), min_val=0, max_val=NT - 1,
                                                     skip_runtime_bounds_check_because="order_edges makes only tiles 0 .. NT - 1")[1]


def make_table(nc, k, tag, w, a_far, a_near, table, near, acc=None, bias=None, guard=False, softmax=None, plain=None, jobs=()):
    na = near.shape[2]
    tw = table.shape[1]
    f1 = tw // na
    hd = f1 - 1
    cw = tw + na
    kc = D // P
    slabs = kc + (bias is not None)
    with stage(nc, tag) as st:
        W = st.sb("W", [P, kc + 1, cw])
        a_b = st.sb("a_b", [P, 2, na * hd])
        prod = st.sb("prod", [P, 2, kc + 1, na * hd])
        XN = st.sb("XN", [P, TG, D])
        XT = st.sb("XT", [P, TG, kc, P])
        ROW = st.sb("ROW", [P, TG, tw])
        odd = st.sb("odd", [P, TG, tw])
        far = st.sb("far", [P, NT, na])
        zeros = st.sb("zeros", [P, tw])
        least = st.sb("least", [P, na])
        most = st.sb("most", [P, na])
        less = st.sb("less", [P, na])
        norm = Norm(st, "n")
        psT = st.ps("psT", [P, 2, 512])
        psH = st.ps("psH", [P, 2, 512])
        w_in, multiplied, folded = (st.sem(s) for s in ("w_in", "multiplied", "folded"))
        turned, turned_out, made, row_out, row_found, row_kept = (
            st.sem(s) for s in ("turned", "turned_out", "made", "row_out", "row_found", "row_kept"))
        stored = [st.sem(f"stored{u}") for u in range(TG)]
        order, reduced, finished = st.sem("order"), st.sem("reduced"), st.sem("finished")
        pad_stored = st.sem("pad_stored")
        scatters = [Scatter(st, f"job{n}", *job) for n, job in enumerate(jobs)]
        block = st.block()

        @block.sync
        def _(sp):
            for s in range(kc):
                sp.dma_start(W[:, s, 0:tw].rearrange("p (h f) -> p h f", f=f1)[:, :, 0:hd],
                             w[s * P:(s + 1) * P, :].rearrange("p (h f) -> p h f", f=hd)).then_inc(w_in, 16)
            sp.dma_start(a_b[:, 0, :], a_far.partition_broadcast(P)).then_inc(w_in, 16)
            sp.dma_start(a_b[:, 1, :], a_near.partition_broadcast(P)).then_inc(w_in, 16)
            if bias is not None:
                sp.dma_start(W[:, kc, 0:tw].rearrange("p (h f) -> p h f", f=f1)[:, :, 0:hd],
                             bias.rearrange("(h f) -> h f", f=hd).partition_broadcast(P)).then_inc(w_in, 16)
            with sp.Fori(0, NTG) as it:
                for u in range(TG):
                    sp.wait_ge(row_kept if guard or softmax is not None else row_out, 1 + it * TG + u + 1)
                    sp.dma_start(table[ds(it * TOK + u * P, P), :], ROW[:, u, :]).then_inc(stored[u], 16)
            for u in range(TG):
                sp.wait_ge(stored[u], 1 + 16 * NTG)
            if softmax is not None:
                sp.wait_ge(order, 1 + 8)
                sp.dma_start(table[N:N + 1, hd:tw:f1], less[0:1, :], allow_slow_non_contiguous=True).then_inc(pad_stored, 16)
                sp.wait_ge(pad_stored, 1 + 16)

        @block.vector
        def _(dve):
            dve.memset(zeros[:], 0.0).then_inc(order, 1)
            dve.memset(far[:], 0.0).then_inc(order, 1)
            dve.wait_ge(w_in, 1 + 16 * (kc + 2 + (bias is not None)))
            for j in range(2):
                for s in range(slabs):
                    dve.tensor_tensor(prod[:, j, s, :].rearrange("p (h f) -> p h f", f=hd),
                                      W[:, s, 0:tw].rearrange("p (h f) -> p h f", f=f1)[:, :, 0:hd],
                                      a_b[:, j, :].rearrange("p (h f) -> p h f", f=hd), ALU.mult)\
                       .then_inc(multiplied, 1)
            dve.wait_ge(multiplied, 1 + 2 * slabs)
            for s in range(slabs):
                dve.tensor_reduce(W[:, s, hd:tw:f1], prod[:, 0, s, :].rearrange("p (h f) -> p h f", f=hd),
                                  AX.X, ALU.add).then_inc(folded, 1)
                dve.tensor_reduce(W[:, s, tw:cw], prod[:, 1, s, :].rearrange("p (h f) -> p h f", f=hd),
                                  AX.X, ALU.add).then_inc(folded, 1)
            dve.wait_ge(order, 1 + 2)
            with dve.Fori(0, NTG) as it:
                def x_tile(u):
                    return k.X[:, ds(it * TG + u, 1), :].squeeze(1)
                if plain is None:
                    norm.dve_first(dve, it, x_tile)
                dve.wait_ge(turned, 1 + it * TG)
                if plain is None:
                    norm.dve_apply(dve, it, x_tile, lambda u: XN[:, u, :])
                else:
                    for u in range(TG):
                        dve.tensor_scalar(XN[:, u, :], plain[:, ds(it * TG + u, 1), :].squeeze(1), 0.0, None, ALU.add)\
                           .then_inc(norm.applied, 1)
                for u in range(TG if guard or softmax is not None else 0):
                    t = it * TG + u
                    dve.wait_ge(row_out, 1 + t + 1)
                    if guard:
                        dve.tensor_tensor(odd[:, u, :], ROW[:, u, :], ROW[:, u, :], ALU.not_equal)\
                           .then_inc(row_found, 1)
                        dve.wait_ge(row_found, 1 + t + 1)
                        dve.nop(nofuse=True)
                        dve.copy_predicated(ROW[:, u, :], odd[:, u, :].bitcast(I32), zeros[:]).then_inc(row_kept, 1)
                    elif softmax is not None:
                        dve.tensor_scalar(far[:, ds(t, 1), :].squeeze(1), ROW[:, u, hd:tw:f1], 0.0, None, ALU.add).then_inc(row_found, 1)
                        dve.tensor_scalar(acc[:, ds(t, 1), :].squeeze(1), ROW[:, u, :], 0.0, None, ALU.add).then_inc(row_kept, 1)
            if softmax is not None:
                shift, base = softmax
                at = [2]

                def then(ins):
                    at[0] += 1
                    ins.then_inc(order, 1)
                    dve.wait_ge(order, 1 + at[0])

                dve.wait_ge(row_found, 1 + NT)
                dve.wait_ge(row_kept, 1 + NT)
                then(dve.tensor_reduce(least[:], far[:].rearrange("p t a -> p a t"), AX.X, ALU.min))
                then(dve.tensor_scalar(least[:], least[:], -1.0, None, ALU.mult))
                dve.wait_ge(reduced, 1 + 1)
                then(dve.tensor_scalar(shift, most[:], 1.0, None, ALU.add))
                sh = shift.unsqueeze(1).broadcast_to([P, NT, na])
                then(dve.tensor_tensor(far[:], far[:], sh, ALU.add))
                then(dve.tensor_tensor(near, near, sh, ALU.subtract))
                then(dve.tensor_scalar(less[:], shift, -1.0, None, ALU.mult))
                then(dve.tensor_tensor(far[:], far[:], near, ALU.add))
                then(dve.scalar_tensor_tensor(out=base, in0=far[:], scalar=0.2, in1=far[:],
                                              op0=ALU.mult, op1=ALU.max))
                then(dve.tensor_scalar(base, base, -1.0, None, ALU.mult))
                then(dve.memset(acc[:, :, hd:tw:f1], 1.0))

        @block.gpsimd
        def _(pool):
            if softmax is not None:
                pool.wait_ge(order, 1 + 4)
                pool.partition_all_reduce(most[:], least[:], P, RED.max).then_inc(reduced, 1)
            for scatter in scatters:
                scatter.run(pool)

        @block.tensor
        def _(pe):
            pe.wait_ge(folded, 1 + 2 * slabs)
            with pe.Fori(0, NTG) as it:
                for u in range(TG):
                    t = it * TG + u
                    pe.wait_ge(norm.applied, 1 + t + 1)
                    pe.wait_ge(turned_out, 1 + (it * TG if u < 2 else t - 1))
                    for s in range(kc):
                        ins = pe.transpose(psT[:, u % 2, s * P:(s + 1) * P], XN[:, u, s * P:(s + 1) * P], k.ident[:])
                    ins.then_inc(turned, 1)
                for u in range(TG):
                    t = it * TG + u
                    pe.wait_ge(turned_out, 1 + t + 1)
                    pe.wait_ge(row_out, 1 + (it * TG if u < 2 else t - 1))
                    for s in range(kc):
                        ins = pe.matmul(psH[:, u % 2, 0:cw], XT[:, u, s, :], W[:, s, :],
                                        start=(s == 0), stop=(s == slabs - 1))
                    if bias is not None:
                        ins = pe.matmul(psH[:, u % 2, 0:cw], k.ones[0:1, :], W[0:1, kc, :],
                                        start=False, stop=True)
                    ins.then_inc(made, 1)

        @block.scalar
        def _(act):
            with act.Fori(0, NTG) as it:
                if plain is None:
                    norm.act_root(act, it)
                for u in range(TG):
                    t = it * TG + u
                    act.wait_ge(turned, 1 + t + 1)
                    act.wait_ge(made, 1 + it * TG)
                    act.activation(XT[:, u, :, :], psT[:, u % 2, 0:D].rearrange("p (k q) -> p k q", q=P), ACT.Copy)\
                       .then_inc(turned_out, 1)
                for u in range(TG):
                    t = it * TG + u
                    act.wait_ge(made, 1 + t + 1)
                    act.wait_ge(stored[u], 1 + it * 16)
                    act.activation(near[:, ds(t, 1), :].squeeze(1), psH[:, u % 2, tw:cw], ACT.Copy)\
                       .then_inc(finished, 1)
                    act.activation(ROW[:, u, :], psH[:, u % 2, 0:tw], ACT.Copy).then_inc(row_out, 1)
            act.wait_ge(finished, 1 + NT)


def edge_pass(nc, k, tag, table, other, local, tile_of, near, acc, softmax=None, guard=False):
    na = near.shape[2]
    tw = table.shape[1]
    f1 = tw // na
    hd = f1 - 1
    n_loop = tile_of.shape[1] // U - 1
    nr = na if softmax is None else 2 * na
    with stage(nc, tag) as st:
        IDX = st.sb("IDX", [P, U, G], I32)
        ROWS = st.sb("ROWS", [P, U, G, tw])
        S = st.sb("S", [P, U, G, P])
        ST = st.sb("ST", [P, U, G, P])
        z = st.sb("z", [P, U, G, na])
        z2 = st.sb("z2", [P, U, G, na])
        psS = st.ps("psS", [P, 2, 512])
        psZ = st.ps("psZ", [P, 2, 512])
        psO = st.ps("psO", [P, 2, 512])
        q = {s: st.sem(s) for s in ("idx_made", "sel", "sel_t", "sel_out", "rated", "added", "leaky", "weighed",
                                    "guarded", "scaled", "summed", "kept")}
        gathered = [[st.gather_sem(f"gathered{u}_{i}") for i in range(G)] for u in range(U)]
        cleared = st.sem("cleared")
        if softmax is not None:
            shift, base = softmax
            FAR = st.sb("FAR", [P, U, G, na])
            VAL = st.sb("VAL", [P, U, G, na, P])
            best = st.sb("best", [P, U, na])
            sumt = st.sb("sumt", [P, U, na])
            leak = st.sb("leak", [P, U, na])
            joined = na > 1
            lead = 6 if joined else 5
            NB = st.sb("NB", [P, U, 2, na])
            drop = st.sb("drop", [P, U, na])
            keep = st.sb("keep", [P, U, na])
            z3 = st.sb("z3", [P, U, G, na])
            turned = [(G - 1, h) for h in range(na)] if joined else [(i, 0) for i in range(G)]
            psV = st.ps("psV", [P, 2, 512])
            q |= {s: st.sem(s) for s in ("far_made", "val", "joined", "val_t", "best_made", "sum_made", "leak_made",
                                         "near_made", "base_made", "drop_made", "base_kept", "keep_made", "based",
                                         "acc_scaled")}
        block = st.block()

        def zeta(v):
            return psZ[:, v % 2, 0:G * nr].rearrange("p (i a) -> p i a", a=nr)

        @block.gpsimd
        def _(pool):
            def gather(it, j):
                g, v = it * U + j, j % U
                pool.wait_ge(q["idx_made"], 1 + g + 1)
                need(pool, q["summed"], it, j - (U - 1))
                pool.nop(nofuse=True)
                for i in range(G):
                    pool.indirect_dma_start(out=ROWS[:, v, i, :], out_offset=None, in_=table,
                                            in_offset=bass.IndirectOffsetOnAxis(ap=IDX[:, v, i:i + 1], axis=0))\
                        .then_inc(gathered[v][i], 16)

            for j in range(U):
                gather(0, j)
            with pool.Fori(0, n_loop) as it:
                for j in range(U):
                    gather(it, j + U)

        @block.scalar
        def _(act):
            def index(it, j):
                g, v, n = it * U + j, j % U, it + j // U
                for i in range(G):
                    if not isinstance(n, int) or n > 0:
                        act.wait_ge(gathered[v][i], n * 16)
                act.activation(IDX[:, v, :], other[:, ds(g * G, G)], ACT.Copy).then_inc(q["idx_made"], 1)

            def turn(it, j):
                g, v = it * U + j, j % U
                act.wait_ge(q["sel_t"], 1 + g + 1)
                need(act, q["rated"], it, j - (U - 1))
                act.activation(ST[:, v, :, :], psS[:, v % 2, 0:G * P].rearrange("p (i n) -> p i n", n=P), ACT.Copy)\
                   .then_inc(q["sel_out"], 1)

            def rescale(it, j):
                g, v = it * U + j, j % U
                act.wait_ge(q["drop_made"], 1 + g + 1)
                need(act, q["kept"], it, j - (U - 1))
                act.activation(keep[:, v, :], drop[:, v, :], ACT.Exp).then_inc(q["keep_made"], 1)

            def weigh(it, j):
                g, v = it * U + j, j % U
                w = ROWS[:, v, :, hd:tw:f1]
                if softmax is None:
                    act.wait_ge(q["leaky"], 1 + g + 1)
                    act.activation(w, z2[:, v, :, :], ACT.Exp, scale=-1.0).then_inc(q["weighed"], 1)
                else:
                    act.wait_ge(q["based"], 1 + g + 1)
                    act.activation(w, z3[:, v, :, :], ACT.Exp).then_inc(q["weighed"], 1)

            def scale_rows(it, j):
                g, v = it * U + j, j % U
                act.wait_ge(q["weighed"], 1 + g + 1)
                for i in range(G):
                    ins = act.activation(ROWS[:, v, i, 0:hd], ROWS[:, v, i, 0:hd], ACT.Copy, scale=ROWS[:, v, i, hd:tw])
                ins.then_inc(q["scaled"], 1)

            def values(it, j):
                g, v = it * U + j, j % U
                act.wait_ge(q["far_made"], 1 + g + 1)
                act.wait_ge(q["sel"], 1 + g + 1)
                need(act, q["val_t"], it, j - (U - 1))
                for i in range(G - 1 if joined else G):
                    for h in range(na):
                        ins = act.activation(VAL[:, v, i, h, :], S[:, v, i, :], ACT.Copy, scale=FAR[:, v, i, h:h + 1])
                ins.then_inc(q["val"], 1)

            def body(it, j):
                if softmax is not None and na == 1:
                    ahead(scale_rows, it, j + 1)
                ahead(turn, it, j + 5)
                if softmax is not None:
                    ahead(values, it, j + lead)
                ahead(weigh, it, j + 2)
                if softmax is not None:
                    ahead(rescale, it, j + 3)
                ahead(index, it, j + U)

            for j in range(-U, 0):
                body(0, j)
            with act.Fori(0, n_loop) as it:
                for j in range(U):
                    body(it, j)

        @block.tensor
        def _(pe):
            def add_up(it, j):
                g, v = it * U + j, j % U
                pe.wait_ge(q["scaled"], 1 + g + 1)
                need(pe, q["kept"], it, j - 1)
                for i in range(G):
                    ins = pe.matmul(psO[:, v % 2, 0:tw], S[:, v, i, :], ROWS[:, v, i, :],
                                    start=(i == 0), stop=(i == G - 1))
                ins.then_inc(q["summed"], 1)

            def rate(it, j, tile):
                g, v = it * U + j, j % U
                pe.wait_ge(q["sel_out"], 1 + g + 1)
                need(pe, q["added" if softmax is None else "based"], it, j - 1)
                if softmax is not None:
                    pe.wait_ge(q["base_made"], 1 + g + 1)
                    pe.wait_ge(q["near_made"], 1 + g + 1)
                rhs = near[:, ds(tile, 1), :].squeeze(1) if softmax is None else NB[:, v, :, :].rearrange("p b a -> p (b a)")
                for i in range(G):
                    ins = pe.matmul(zeta(v)[:, i, :], ST[:, v, i, :], rhs, start=True, stop=True)
                ins.then_inc(q["rated"], 1)

            def turn_values(it, j):
                g, v = it * U + j, j % U
                pe.wait_ge(q["joined" if joined else "val"], 1 + g + 1)
                need(pe, q["best_made"], it, j - 1)
                for n, (i, h) in enumerate(turned):
                    ins = pe.transpose(psV[:, v % 2, n * P:(n + 1) * P], VAL[:, v, i, h, :], k.ident[:])
                ins.then_inc(q["val_t"], 1)

            def turn(it, j):
                g, v = it * U + j, j % U
                pe.wait_ge(q["sel"], 1 + g + 1)
                need(pe, q["sel_out"], it, j - 1)
                for i in range(G):
                    ins = pe.transpose(psS[:, v % 2, i * P:(i + 1) * P], S[:, v, i, :], k.ident[:])
                ins.then_inc(q["sel_t"], 1)

            def body(it, j, tile):
                ahead(turn, it, j + 5)
                ahead(rate, it, j + 3, tile)
                ahead(add_up, it, j + 1)
                if softmax is not None:
                    ahead(turn_values, it, j + 5)

            tiles = [None] * U
            if softmax is None:
                tiles = tile_ids(nc, mybir.EngineType.PE, tile_of, 0)
            for j in range(-U, 0):
                body(0, j, tiles[max(j + 3, 0)])
            with pe.Fori(0, n_loop) as it:
                if softmax is None:
                    tiles = tile_ids(nc, mybir.EngineType.PE, tile_of, it * U + 3)
                for j in range(U):
                    body(it, j, tiles[j])

        @block.vector
        def _(dve):
            def keep_sum(it, j, tile):
                g, v = it * U + j, j % U
                dve.wait_ge(q["summed"], 1 + g + 1)
                need(dve, q["kept"], it, j)
                a = acc[:, ds(tile, 1), :].squeeze(1)
                o = psO[:, v % 2, 0:tw]
                if softmax is None:
                    dve.tensor_tensor(a, o, a, ALU.add).then_inc(q["kept"], 1)
                elif na == 1:
                    dve.wait_ge(q["keep_made"], 1 + g + 1)
                    dve.scalar_tensor_tensor(out=a, in0=a, scalar=keep[:, v, :], in1=o,
                                             op0=ALU.mult, op1=ALU.add).then_inc(q["kept"], 1)
                else:
                    dve.wait_ge(q["keep_made"], 1 + g + 1)
                    ah = a.rearrange("p (h f) -> p h f", f=f1)
                    dve.tensor_tensor(ah, ah, keep[:, v, :].unsqueeze(2).broadcast_to([P, na, f1]), ALU.mult)\
                       .then_inc(q["acc_scaled"], 1)
                    dve.wait_ge(q["acc_scaled"], 1 + g + 1)
                    dve.tensor_tensor(a, o, a, ALU.add).then_inc(q["kept"], 1)

            def scale_rows(it, j):
                g, v = it * U + j, j % U
                dve.wait_ge(q["weighed"], 1 + g + 1)
                w = ROWS[:, v, :, hd:tw:f1]
                if guard:
                    dve.tensor_scalar(w, w, 0.0, None, ALU.max).then_inc(q["guarded"], 1)
                    dve.wait_ge(q["guarded"], 1 + g + 1)
                r = ROWS[:, v, :, :].rearrange("p i (h f) -> p (i h) f", f=f1)
                dve.tensor_tensor(r[:, :, 0:hd], r[:, :, 0:hd], r[:, :, hd:f1].broadcast_to([P, G * na, hd]),
                                  ALU.mult).then_inc(q["scaled"], 1)

            def add_near(it, j):
                g, v, n = it * U + j, j % U, it + j // U + 1
                dve.wait_ge(q["rated"], 1 + g + 1)
                if softmax is None:
                    for i in range(G):
                        dve.wait_ge(gathered[v][i], n * 16)
                    f = ROWS[:, v, :, hd:tw:f1]
                else:
                    f = FAR[:, v, :, :]
                dve.tensor_tensor(z[:, v, :, :], zeta(v)[:, :, 0:na], f, ALU.add).then_inc(q["added"], 1)

            def leaky(it, j):
                g, v = it * U + j, j % U
                dve.wait_ge(q["added"], 1 + g + 1)
                dve.scalar_tensor_tensor(out=z2[:, v, :, :], in0=z[:, v, :, :], scalar=0.2, in1=z[:, v, :, :],
                                         op0=ALU.mult, op1=ALU.max).then_inc(q["leaky"], 1)

            def minus_base(it, j):
                g, v = it * U + j, j % U
                dve.wait_ge(q["leaky"], 1 + g + 1)
                dve.tensor_tensor(z3[:, v, :, :], z2[:, v, :, :], zeta(v)[:, :, na:nr], ALU.add)\
                   .then_inc(q["based"], 1)

            def col(t, tile):
                return t[:, ds(tile, 1), :].squeeze(1)

            def find_best(it, j):
                g, v = it * U + j, j % U
                dve.wait_ge(q["val_t"], 1 + g + 1)
                flat = psV[:, v % 2, 0:len(turned) * P]
                dve.tensor_reduce(best[:, v, :], flat.rearrange("p (a e) -> p a e", a=na), AX.X, ALU.max)\
                   .then_inc(q["best_made"], 1)

            def best_sum(it, j, tile):
                g, v = it * U + j, j % U
                dve.wait_ge(q["best_made"], 1 + g + 1)
                dve.tensor_tensor(sumt[:, v, :], best[:, v, :], col(near, tile), ALU.add).then_inc(q["sum_made"], 1)

            def best_leaky(it, j):
                g, v = it * U + j, j % U
                dve.wait_ge(q["sum_made"], 1 + g + 1)
                dve.scalar_tensor_tensor(out=leak[:, v, :], in0=sumt[:, v, :], scalar=0.2, in1=sumt[:, v, :],
                                         op0=ALU.mult, op1=ALU.max).then_inc(q["leak_made"], 1)

            def copy_near(it, j, tile):
                v = j % U
                need(dve, q["rated"], it, j - (U - 1))
                dve.tensor_scalar(NB[:, v, 0, :], col(near, tile), 0.0, None, ALU.add).then_inc(q["near_made"], 1)

            def new_base(it, j, tile):
                g, v = it * U + j, j % U
                dve.wait_ge(q["leak_made"], 1 + g + 1)
                need(dve, q["base_kept"], it, j)
                dve.scalar_tensor_tensor(out=NB[:, v, 1, :], in0=leak[:, v, :], scalar=-1.0, in1=col(base, tile),
                                         op0=ALU.mult, op1=ALU.min).then_inc(q["base_made"], 1)

            def base_drop(it, j, tile):
                g, v = it * U + j, j % U
                dve.wait_ge(q["base_made"], 1 + g + 1)
                dve.tensor_tensor(drop[:, v, :], NB[:, v, 1, :], col(base, tile), ALU.subtract)\
                   .then_inc(q["drop_made"], 1)

            def keep_base(it, j, tile):
                g, v = it * U + j, j % U
                dve.wait_ge(q["drop_made"], 1 + g + 1)
                dve.tensor_scalar(col(base, tile), NB[:, v, 1, :], 0.0, None, ALU.add).then_inc(q["base_kept"], 1)

            def shift_far(it, j):
                v, n = j % U, it + j // U + 1
                for i in range(G):
                    dve.wait_ge(gathered[v][i], n * 16)
                dve.tensor_tensor(FAR[:, v, :, :], ROWS[:, v, :, hd:tw:f1],
                                  shift.unsqueeze(1).broadcast_to([P, G, na]), ALU.add).then_inc(q["far_made"], 1)

            def join(it, j):
                g, v = it * U + j, j % U
                dve.wait_ge(q["val"], 1 + g + 1)
                for h in range(na):
                    ins = dve.scalar_tensor_tensor(out=VAL[:, v, 1, h, :], in0=S[:, v, 1, :],
                                                   scalar=FAR[:, v, 1, h:h + 1], in1=VAL[:, v, 0, h, :],
                                                   op0=ALU.mult, op1=ALU.max)
                ins.then_inc(q["joined"], 1)

            def select(it, j):
                g, v = it * U + j, j % U
                need(dve, q["summed"], it, j - (U - 1))
                dve.tensor_tensor(S[:, v, :, :], k.iota[:].unsqueeze(1).broadcast_to([P, G, P]),
                                  local[:, ds(g * G, G)].unsqueeze(2).broadcast_to([P, G, P]), ALU.is_equal)\
                   .then_inc(q["sel"], 1)

            def body(it, j, tile, tile4):
                if softmax is None:
                    ahead(add_near, it, j + 2)
                    ahead(select, it, j + 5)
                    ahead(leaky, it, j + 2)
                    ahead(scale_rows, it, j + 1)
                    ahead(keep_sum, it, j, tile)
                    return
                if na > 1:
                    ahead(scale_rows, it, j + 1)
                ahead(add_near, it, j + 2)
                ahead(shift_far, it, j + lead)
                ahead(leaky, it, j + 2)
                if joined:
                    ahead(join, it, j + 5)
                ahead(minus_base, it, j + 2)
                ahead(find_best, it, j + 4)
                ahead(copy_near, it, j + 4, tile4)
                ahead(best_sum, it, j + 4, tile4)
                ahead(select, it, j + lead + 1)
                ahead(best_leaky, it, j + 4)
                ahead(keep_sum, it, j, tile)
                ahead(new_base, it, j + 4, tile4)
                ahead(base_drop, it, j + 4, tile4)
                ahead(keep_base, it, j + 4, tile4)

            if softmax is not None:
                tiles4 = tile_ids(nc, mybir.EngineType.DVE, tile_of, 0)
            else:
                tiles4 = [None] * U
            if softmax is None:
                dve.memset(acc, 0.0).then_inc(cleared, 1)
            for j in range(-U, 0):
                body(0, j, None, tiles4[max(j + 4, 0)])
            if softmax is None:
                dve.wait_ge(cleared, 1 + 1)
            with dve.Fori(0, n_loop) as it:
                tiles = tile_ids(nc, mybir.EngineType.DVE, tile_of, it * U)
                if softmax is not None:
                    tiles4 = tile_ids(nc, mybir.EngineType.DVE, tile_of, it * U + 4)
                for j in range(U):
                    body(it, j, tiles[j], tiles4[j])
            for v in range(U):
                for i in range(G):
                    dve.wait_ge(gathered[v][i], 16 * (n_loop + 1))


def finish_attention(nc, k, tag, acc, na, hd, elus, guard):
    f1 = hd + 1
    with stage(nc, tag) as st:
        rec = st.sb("rec", [P, NT, na])
        h = st.sb("h", [P, 2, TG, D])
        lo = st.sb("lo", [P, 2, TG, D])
        ex = st.sb("ex", [P, 2, TG, D])
        zeros = st.sb("zeros", [P, TG, D])
        order = st.sem("order")
        lows, exps = st.sem("lows"), st.sem("exps")
        block = st.block()

        @block.vector
        def _(dve):
            at = [0]

            def then(ins):
                at[0] += 1
                ins.then_inc(order, 1)
                dve.wait_ge(order, 1 + at[0])

            then(dve.memset(zeros[:], 0.0))
            view = acc.rearrange("p t (h f) -> p t h f", f=f1)
            ends = view[:, NT - 1, :, hd]
            then(dve.tensor_scalar(ends, ends, k.past_end[:], None, ALU.add))
            if guard:
                w = view[:, :, :, hd]
                then(dve.scalar_tensor_tensor(out=w, in0=w, scalar=0.0, in1=w, op0=ALU.is_equal, op1=ALU.add))
            then(dve.reciprocal(rec[:], view[:, :, :, hd]))

            def divide(c):
                s = c % 2
                then(dve.tensor_tensor(h[:, s, :, :].rearrange("p t (h f) -> p t h f", f=hd),
                                       view[:, c * TG:(c + 1) * TG, :, 0:hd],
                                       rec[:, c * TG:(c + 1) * TG, :].unsqueeze(3).broadcast_to([P, TG, na, hd]),
                                       ALU.mult))
                if guard:
                    then(dve.tensor_tensor(lo[:, s, :, :], h[:, s, :, :], h[:, s, :, :], ALU.not_equal))
                    then(dve.copy_predicated(h[:, s, :, :], lo[:, s, :, :].bitcast(I32), zeros[:]))

            def low(c):
                s = c % 2
                then(dve.tensor_scalar(lo[:, s, :, :], h[:, s, :, :], 0.0, None, ALU.min))
                dve.sem_inc(lows, 1)

            def join(c, r):
                s = c % 2
                dve.wait_ge(exps, 1 + r)
                then(dve.tensor_scalar(ex[:, s, :, :], ex[:, s, :, :], -1.0, None, ALU.add))
                then(dve.scalar_tensor_tensor(out=h[:, s, :, :], in0=h[:, s, :, :], scalar=0.0,
                                              in1=ex[:, s, :, :], op0=ALU.max, op1=ALU.add))

            for c in range(NTG):
                divide(c)
                for e in range(elus):
                    low(c)
                    join(c, c * elus + e + 1)
                xs = k.X[:, c * TG:(c + 1) * TG, :]
                then(dve.tensor_tensor(xs, xs, h[:, c % 2, :, :], ALU.add))

        @block.scalar
        def _(act):
            for r in range(NTG * elus):
                s = (r // elus) % 2
                act.wait_ge(lows, 1 + r + 1)
                act.activation(ex[:, s, :, :], lo[:, s, :, :], ACT.Exp).then_inc(exps, 1)


def finish_conv(nc, k, tag, acc, bias, dst, relu, add):
    with stage(nc, tag) as st:
        rec = st.sb("rec", [P, NT])
        b = st.sb("b", [P, D])
        h = st.sb("h", [P, 2, TG, D])
        b_in, order = st.sem("b_in"), st.sem("order")
        block = st.block()

        @block.sync
        def _(sp):
            sp.dma_start(b[:], bias.partition_broadcast(P)).then_inc(b_in, 16)

        @block.vector
        def _(dve):
            at = [0]

            def then(ins):
                at[0] += 1
                ins.then_inc(order, 1)
                dve.wait_ge(order, 1 + at[0])

            then(dve.reciprocal(rec[:], acc[:, :, D]))
            dve.wait_ge(b_in, 1 + 16)
            for c in range(NTG):
                t = slice(c * TG, (c + 1) * TG)
                whole = [P, TG, D]
                hc = h[:, c % 2, :, :]
                then(dve.tensor_tensor(hc, acc[:, t, 0:D], rec[:, t].unsqueeze(2).broadcast_to(whole), ALU.mult))
                if relu:
                    then(dve.tensor_tensor(hc, hc, b[:].unsqueeze(1).broadcast_to(whole), ALU.add))
                    then(dve.tensor_scalar(dst[:, t, :], hc, 0.0, None, ALU.max))
                if add:
                    then(dve.tensor_tensor(hc, hc, b[:].unsqueeze(1).broadcast_to(whole), ALU.add))
                    then(dve.tensor_tensor(dst[:, t, :], dst[:, t, :], hc, ALU.add))


def tokens(nc, k, tag, XT, logits=None, w=None, b=None, hidden=None, twice=False, keep=False):
    kc = D // P
    ne = 0 if w is None else w.shape[1]
    with stage(nc, tag) as st:
        XN = st.sb("XN", [P, TG, D])
        XN2 = st.sb("XN2", [P, TG, D])
        XS = st.sb("XS", [P, TG, kc, P])
        norm = Norm(st, "n")
        norm2 = Norm(st, "m") if twice else None
        psT = st.ps("psT", [P, 2, 512])
        turned, turned_out, kept = st.sem("turned"), st.sem("turned_out"), st.sem("kept")
        turned2, turned2_out = st.sem("turned2"), st.sem("turned2_out")
        w_in, rated, rated_out = st.sem("w_in"), st.sem("rated"), st.sem("rated_out")
        hid, hid_out = st.sem("hid"), st.sem("hid_out")
        if twice:
            psT2 = st.ps("psT2", [P, 2, 512])
        if w is not None:
            psL = st.ps("psL", [P, 2, 512])
            WR = st.sb("WR", [P, kc, ne])
            BR = st.sb("BR", [P, ne])
        if hidden is not None:
            hw = hidden[0].shape[1]
            psH = st.ps("psH", [P, 2, 512])
            W1 = st.sb("W1", [P, kc, hw])
            B1 = st.sb("B1", [P, 1])
            RH = st.sb("RH", [P, TG, P])
        loads = (0 if w is None else 2) + (0 if hidden is None else 2)
        block = st.block()

        @block.sync
        def _(sp):
            if w is not None:
                if hidden is None:
                    sp.dma_start(WR[:], w.rearrange("(k p) e -> p k e", p=P), allow_slow_non_contiguous=True).then_inc(w_in, 16)
                else:
                    sp.dma_start(WR[:, 0, :], w).then_inc(w_in, 16)
                sp.dma_start(BR[:], b.partition_broadcast(P)).then_inc(w_in, 16)
            if hidden is not None:
                sp.dma_start(W1[:], hidden[0].rearrange("(k p) e -> p k e", p=P)).then_inc(w_in, 16)
                sp.dma_start(B1[:], hidden[1].unsqueeze(1)).then_inc(w_in, 16)
            if loads:
                sp.wait_ge(w_in, 1 + 16 * loads)

        @block.vector
        def _(dve):
            if w is not None:
                dve.wait_ge(w_in, 1 + 16 * loads)
            with dve.Fori(0, NTG) as it:
                def x_tile(u):
                    return k.X[:, ds(it * TG + u, 1), :].squeeze(1)
                norm.dve_first(dve, it, x_tile)
                dve.wait_ge(turned, 1 + it * TG)
                norm.dve_apply(dve, it, x_tile, lambda u: XN[:, u, :])
                if keep:
                    for u in range(TG):
                        dve.wait_ge(norm.applied, 1 + it * TG + u + 1)
                        dve.tensor_tensor(x_tile(u), x_tile(u), XN[:, u, :], ALU.add).then_inc(kept, 1)
                if twice:
                    dve.wait_ge(norm.applied, 1 + it * TG + TG)
                    norm2.dve_first(dve, it, lambda u: XN[:, u, :])
                    dve.wait_ge(turned2, 1 + it * TG)
                    norm2.dve_apply(dve, it, lambda u: XN[:, u, :], lambda u: XN2[:, u, :])
                if w is not None:
                    for u in range(TG):
                        t = it * TG + u
                        dve.wait_ge(rated, 1 + t + 1)
                        dve.tensor_tensor(logits[:, ds(t, 1), :].squeeze(1), psL[:, u % 2, 0:ne], BR[:], ALU.add)\
                           .then_inc(rated_out, 1)
            if keep:
                dve.wait_ge(kept, 1 + NT)

        @block.tensor
        def _(pe):
            if w is not None:
                pe.wait_ge(w_in, 1 + 16 * loads)
            with pe.Fori(0, NTG) as it:
                def free(u):
                    return it * TG if u < 2 else it * TG + u - 1
                for u in range(TG):
                    pe.wait_ge(norm.applied, 1 + it * TG + u + 1)
                    pe.wait_ge(turned_out, 1 + free(u))
                    for s in range(kc):
                        ins = pe.transpose(psT[:, u % 2, s * P:(s + 1) * P], XN[:, u, s * P:(s + 1) * P], k.ident[:])
                    ins.then_inc(turned, 1)
                for u in range(TG if twice else 0):
                    pe.wait_ge(norm2.applied, 1 + it * TG + u + 1)
                    pe.wait_ge(turned2_out, 1 + free(u))
                    for s in range(kc):
                        ins = pe.transpose(psT2[:, u % 2, s * P:(s + 1) * P], XN2[:, u, s * P:(s + 1) * P], k.ident[:])
                    ins.then_inc(turned2, 1)
                for u in range(0 if hidden is None else TG):
                    pe.wait_ge(turned_out, 1 + it * TG + u + 1)
                    pe.wait_ge(hid_out, 1 + free(u))
                    for s in range(kc):
                        ins = pe.matmul(psH[:, u % 2, 0:P], W1[:, s, :], XS[:, u, s, :],
                                        start=(s == 0), stop=(s == kc - 1))
                    ins.then_inc(hid, 1)
                for u in range(0 if w is None else TG):
                    pe.wait_ge(rated_out, 1 + free(u))
                    if hidden is None:
                        pe.wait_ge(turned_out, 1 + it * TG + u + 1)
                        for s in range(kc):
                            ins = pe.matmul(psL[:, u % 2, 0:ne], XS[:, u, s, :], WR[:, s, :],
                                            start=(s == 0), stop=(s == kc - 1))
                    else:
                        pe.wait_ge(hid_out, 1 + it * TG + u + 1)
                        ins = pe.matmul(psL[:, u % 2, 0:ne], RH[:, u, :], WR[:, 0, :], start=True, stop=True)
                    ins.then_inc(rated, 1)

        @block.scalar
        def _(act):
            if hidden is not None:
                act.wait_ge(w_in, 1 + 16 * loads)
            with act.Fori(0, NTG) as it:
                def persist(u, ps):
                    return act.activation(XT[:, :, ds(it * TOK + u * P, P)],
                                          ps[:, u % 2, 0:D].rearrange("p (k q) -> p k q", q=P), ACT.Copy)
                norm.act_root(act, it)
                for u in range(TG):
                    act.wait_ge(turned, 1 + it * TG + u + 1)
                    if w is not None:
                        act.wait_ge(rated, 1 + it * TG)
                        ins = act.activation(XS[:, u, :, :], psT[:, u % 2, 0:D].rearrange("p (k q) -> p k q", q=P),
                                             ACT.Copy)
                        if not twice:
                            ins = persist(u, psT)
                    else:
                        ins = persist(u, psT)
                    ins.then_inc(turned_out, 1)
                if twice:
                    norm2.act_root(act, it)
                    for u in range(TG):
                        act.wait_ge(turned2, 1 + it * TG + u + 1)
                        persist(u, psT2).then_inc(turned2_out, 1)
                for u in range(0 if hidden is None else TG):
                    act.wait_ge(hid, 1 + it * TG + u + 1)
                    act.activation(RH[:, u, :], psH[:, u % 2, 0:P], ACT.Relu, bias=B1[:, 0:1]).then_inc(hid_out, 1)
            act.wait_ge(turned2_out if twice else turned_out, 1 + NT)


def choose(nc, k, tag, scores, gates, probs, renorm):
    ne = scores.shape[2]
    whole = [P, NT, ne]
    with stage(nc, tag) as st:
        p = st.sb("p", whole)
        d = st.sb("d", whole)
        e = st.sb("e", whole)
        rev = st.sb("rev", [P, ne])
        v = st.sb("v", whole)
        hot = [st.sb(f"hot{i}", whole) for i in range(2)]
        best = [st.sb(f"best{i}", [P, NT]) for i in range(2)]
        wt = [st.sb(f"wt{i}", [P, NT]) for i in range(2)]
        m, s1, s2 = (st.sb(n, [P, NT]) for n in ("m", "s1", "s2"))
        order, exps = st.sem("order"), st.sem("exps")
        at_diff = []
        block = st.block()

        @block.vector
        def _(dve):
            at = [0]

            def then(ins):
                at[0] += 1
                ins.then_inc(order, 1)
                dve.wait_ge(order, 1 + at[0])

            def wide(t):
                return t[:].unsqueeze(2).broadcast_to(whole)

            if probs:
                then(dve.tensor_reduce(m[:], scores, AX.X, ALU.max))
                then(dve.tensor_tensor(d[:], scores, wide(m), ALU.subtract))
                dve.wait_ge(exps, 1 + 1)
                then(dve.tensor_reduce(s1[:], e[:], AX.X, ALU.add))
                then(dve.reciprocal(s2[:], s1[:]))
                then(dve.tensor_tensor(p[:], e[:], wide(s2), ALU.mult))
            else:
                then(dve.tensor_scalar(p[:], scores, 0.0, None, ALU.add))
            then(dve.tensor_scalar(rev[:], k.iota[:, 0:ne], -1.0, float(ne), ALU.mult, ALU.add))
            for i in range(2):
                then(dve.tensor_reduce(best[i][:], p[:], AX.X, ALU.max))
                then(dve.tensor_tensor(v[:], p[:], wide(best[i]), ALU.is_equal))
                then(dve.tensor_tensor(v[:], v[:], rev[:].unsqueeze(1).broadcast_to(whole), ALU.mult))
                then(dve.tensor_reduce(m[:], v[:], AX.X, ALU.max))
                then(dve.tensor_tensor(hot[i][:], v[:], wide(m), ALU.is_equal))
                if i == 0:
                    then(dve.scalar_tensor_tensor(out=p[:], in0=hot[0][:], scalar=-BIG, in1=p[:],
                                                  op0=ALU.mult, op1=ALU.add))
            if renorm:
                then(dve.tensor_tensor(s1[:], best[0][:], best[1][:], ALU.add))
                then(dve.reciprocal(s2[:], s1[:]))
                then(dve.tensor_tensor(wt[0][:], best[0][:], s2[:], ALU.mult))
                then(dve.tensor_tensor(wt[1][:], best[1][:], s2[:], ALU.mult))
            else:
                then(dve.tensor_tensor(m[:], best[1][:], best[0][:], ALU.subtract))
                at_diff.append(at[0])
                dve.wait_ge(exps, 1 + 1 + probs)
                then(dve.tensor_scalar(s2[:], s1[:], 1.0, None, ALU.add))
                then(dve.reciprocal(wt[0][:], s2[:]))
                then(dve.tensor_tensor(wt[1][:], s1[:], wt[0][:], ALU.mult))
            for i in range(2):
                then(dve.tensor_tensor(hot[i][:], hot[i][:], wide(wt[i]), ALU.mult))
            then(dve.tensor_tensor(gates.rearrange("p e t -> p t e"), hot[0][:], hot[1][:], ALU.add))

        @block.scalar
        def _(act):
            if probs:
                act.wait_ge(order, 1 + 2)
                act.activation(e[:], d[:], ACT.Exp).then_inc(exps, 1)
            if not renorm:
                act.wait_ge(order, 1 + at_diff[0])
                act.activation(s1[:], m[:], ACT.Exp).then_inc(exps, 1)


def add_bias(nc, k, tag, gates, b2):
    ne = gates.shape[1]
    with stage(nc, tag) as st:
        B2 = st.sb("B2", [ne, D])
        GS = st.sb("GS", [P, TG, ne])
        GT = st.sb("GT", [ne, TG, P])
        psG = st.ps("psG", [P, 2, 512])
        psB = st.ps("psB", [P, 2, 512])
        b_in, set_out, turned, turned_out, made, kept = (
            st.sem(s) for s in ("b_in", "set_out", "turned", "turned_out", "made", "kept"))
        block = st.block()

        @block.sync
        def _(sp):
            sp.dma_start(B2[:], b2).then_inc(b_in, 16)

        @block.vector
        def _(dve):
            with dve.Fori(0, NTG) as it:
                dve.wait_ge(turned, 1 + it * TG)
                for u in range(TG):
                    dve.tensor_scalar(GS[:, u, :], gates[:, :, ds(it * TG + u, 1)].squeeze(2), 0.0, None, ALU.add)\
                       .then_inc(set_out, 1)
                for u in range(TG):
                    t = it * TG + u
                    dve.wait_ge(made, 1 + t + 1)
                    x = k.X[:, ds(t, 1), :].squeeze(1)
                    dve.tensor_tensor(x, x, psB[:, u % 2, 0:D], ALU.add).then_inc(kept, 1)
            dve.wait_ge(kept, 1 + NT)

        @block.scalar
        def _(act):
            with act.Fori(0, NTG) as it:
                for u in range(TG):
                    act.wait_ge(turned, 1 + it * TG + u + 1)
                    act.wait_ge(made, 1 + it * TG)
                    act.activation(GT[:, u, :], psG[0:ne, u % 2, 0:P], ACT.Copy).then_inc(turned_out, 1)

        @block.tensor
        def _(pe):
            pe.wait_ge(b_in, 1 + 16)
            with pe.Fori(0, NTG) as it:
                def free(u):
                    return it * TG if u < 2 else it * TG + u - 1
                for u in range(TG):
                    pe.wait_ge(set_out, 1 + it * TG + u + 1)
                    pe.wait_ge(turned_out, 1 + free(u))
                    pe.transpose(psG[0:ne, u % 2, 0:P], GS[:, u, :], k.ident[:]).then_inc(turned, 1)
                for u in range(TG):
                    pe.wait_ge(turned_out, 1 + it * TG + u + 1)
                    pe.wait_ge(kept, 1 + free(u))
                    pe.matmul(psB[:, u % 2, 0:D], GT[:, u, :], B2[:], start=True, stop=True).then_inc(made, 1)


def feed_forward(nc, k, tag, XT, w1, b1, w2, gates, func, mid=None, affine=None, jobs=()):
    ne, _, h1 = w1.shape
    kc = D // P
    hc = h1 // P
    mc = 0 if mid is None else mid[0].shape[2] // P
    lc = mc or hc
    pair = min(2, ne)
    na = pair * (hc + mc)
    nb = pair * TG
    with stage(nc, tag) as st:
        W1 = [st.sb(f"W1_{e}", [P, kc, h1]) for e in range(pair)]
        B1 = [st.sb(f"B1_{e}", [P, hc]) for e in range(pair)]
        W2 = [st.sb(f"W2_{e}", [P, lc, D]) for e in range(pair)]
        H = [st.sb(f"H_{e}", [P, hc, 2, HALF]) for e in range(pair)]
        if mid is not None:
            WM = [st.sb(f"WM_{e}", [P, hc, mc * P]) for e in range(pair)]
            BM = [st.sb(f"BM_{e}", [P, mc]) for e in range(pair)]
            HM = [st.sb(f"HM_{e}", [P, mc, 2, HALF]) for e in range(pair)]
        if affine is not None:
            AF = [st.sb(f"AF_{e}", [P, 2, kc]) for e in range(pair)]
            XE = [st.sb(f"XE_{e}", [P, kc, TOK]) for e in range(pair)]
        psA = st.ps("psA", [P, 2, 2, 512])
        psB = st.ps("psB", [P, 4, 512])
        first_in = [st.sem(f"first_in{e}") for e in range(pair)]
        rest_in = [st.sem(f"rest_in{e}") for e in range(pair)]
        first_used = [st.sem(f"first_used{e}") for e in range(pair)]
        rest_used = [st.sem(f"rest_used{e}") for e in range(pair)]
        made, active, out_made, kept, scaled = (
            st.sem(s) for s in ("made", "active", "out_made", "kept", "scaled"))
        n_first = 2 if affine is not None else 1
        n_rest = 4 if mid is not None else 2
        scatters = [Scatter(st, f"job{n}", *job) for n, job in enumerate(jobs)]
        block = st.block()

        @block.gpsimd
        def _(pool):
            for scatter in scatters:
                scatter.run(pool)

        @block.sync
        def _(sp):
            with sp.Fori(0, ne // pair) as pr:
                for e in range(pair):
                    x = pr * pair + e
                    sp.wait_ge(first_used[e], 1 + pr * NTG)
                    sp.dma_start(W1[e][:], w1[ds(x, 1), :, :].rearrange("o (k p) h -> p (o k) h", p=P))\
                      .then_inc(first_in[e], 16)
                    if affine is not None:
                        sp.dma_start(AF[e][:], affine[ds(x, 1)].squeeze(0)).then_inc(first_in[e], 16)
                for e in range(pair):
                    x = pr * pair + e
                    sp.wait_ge(rest_used[e], 1 + pr * NTG)
                    sp.dma_start(B1[e][:], b1[ds(x, 1)].squeeze(0)).then_inc(rest_in[e], 16)
                    if mid is not None:
                        sp.dma_start(WM[e][:], mid[0][ds(x, 1), :, :].rearrange("o (k p) h -> p (o k) h", p=P))\
                          .then_inc(rest_in[e], 16)
                        sp.dma_start(BM[e][:], mid[1][ds(x, 1)].squeeze(0)).then_inc(rest_in[e], 16)
                    sp.dma_start(W2[e][:], w2[ds(x, 1), :, :].rearrange("o (k p) h -> p (o k) h", p=P))\
                      .then_inc(rest_in[e], 16)

        def steps(eng, body):
            with eng.Fori(0, ne // pair) as pr:
                with eng.Fori(0, NTG) as g:
                    body(pr, g, pr * NTG + g)

        @block.tensor
        def _(pe):
            def layer(s, w, src, chunks, ks, at):
                for c in range(chunks):
                    n = at + c
                    pe.wait_ge(active, 1 + (s * na if n < 2 else s * na + n - 1))
                    for half in range(2):
                        for i in range(ks):
                            ins = pe.matmul(psA[:, n % 2, half, 0:HALF], w[:, i, c * P:(c + 1) * P], src(i, half),
                                            start=(i == 0), stop=(i == ks - 1))
                    ins.then_inc(made, 1)
                return ins

            def body(pr, g, s):
                for e in range(pair):
                    pe.wait_ge(first_in[e], 1 + pr * (16 * n_first) + 16 * n_first)
                    if affine is not None:
                        pe.wait_ge(scaled, 1 + s * (kc * pair) + kc * (e + 1))
                        layer(s, W1[e], lambda i, half: XE[e][:, i, half * HALF:(half + 1) * HALF], hc, kc, e * hc)
                    else:
                        layer(s, W1[e], lambda i, half: XT[:, i, ds(g * TOK + half * HALF, HALF)], hc, kc, e * hc)
                    pe.wait_ge(made, 1 + s * na + (e + 1) * hc)
                    pe.sem_inc(first_used[e], 1)
                for e in range(pair if mid is not None else 0):
                    pe.wait_ge(rest_in[e], 1 + pr * (16 * n_rest) + 16 * n_rest)
                    pe.wait_ge(active, 1 + s * na + (e + 1) * hc)
                    layer(s, WM[e], lambda i, half: H[e][:, i, half, :], mc, hc, pair * hc + e * mc)
                for e in range(pair):
                    pe.wait_ge(rest_in[e], 1 + pr * (16 * n_rest) + 16 * n_rest)
                    pe.wait_ge(active, 1 + (s * na + (pair * hc + (e + 1) * mc if mid is not None else (e + 1) * hc)))
                    hid = H[e] if mid is None else HM[e]
                    for j in range(TG):
                        n = e * TG + j
                        pe.wait_ge(kept, 1 + (s * nb if n < 4 else s * nb + n - 3))
                        flat = hid[:].rearrange("p c a t -> p c (a t)")
                        for c in range(lc):
                            ins = pe.matmul(psB[:, n % 4, 0:D], flat[:, c, j * P:(j + 1) * P], W2[e][:, c, :],
                                            start=(c == 0), stop=(c == lc - 1))
                        ins.then_inc(out_made, 1)
                    pe.wait_ge(out_made, 1 + s * nb + (e + 1) * TG)
                    pe.sem_inc(rest_used[e], 1)
            steps(pe, body)

        @block.scalar
        def _(act):
            def body(pr, g, s):
                for e in range(pair):
                    act.wait_ge(rest_used[e], 1 + s)
                    act.wait_ge(rest_in[e], 1 + pr * (16 * n_rest) + 16 * n_rest)
                    for c in range(hc):
                        n = e * hc + c
                        act.wait_ge(made, 1 + s * na + n + 1)
                        act.activation(H[e][:, c, :, :], psA[:, n % 2, :, 0:HALF], func, bias=B1[e][:, c:c + 1])\
                           .then_inc(active, 1)
                for e in range(pair if mid is not None else 0):
                    for c in range(mc):
                        n = pair * hc + e * mc + c
                        act.wait_ge(made, 1 + s * na + n + 1)
                        act.activation(HM[e][:, c, :, :], psA[:, n % 2, :, 0:HALF], func, bias=BM[e][:, c:c + 1])\
                           .then_inc(active, 1)
            steps(act, body)

        @block.vector
        def _(dve):
            def body(pr, g, s):
                if affine is not None:
                    for e in range(pair):
                        dve.wait_ge(first_in[e], 1 + pr * (16 * n_first) + 16 * n_first)
                        dve.wait_ge(first_used[e], 1 + s)
                        for i in range(kc):
                            dve.tensor_scalar(XE[e][:, i, :], XT[:, i, ds(g * TOK, TOK)], AF[e][:, 0, i:i + 1],
                                              AF[e][:, 1, i:i + 1], ALU.mult, ALU.add).then_inc(scaled, 1)
                for e in range(pair):
                    for j in range(TG):
                        n = e * TG + j
                        dve.wait_ge(out_made, 1 + s * nb + n + 1)
                        dve.wait_ge(kept, 1 + s * nb + n)
                        x = k.X[:, ds(g * TG + j, 1), :].squeeze(1)
                        gate = gates.rearrange("p e t -> p (e t)")[:, ds(pr * (pair * NT) + e * NT + g * TG + j, 1)]
                        dve.scalar_tensor_tensor(out=x, in0=psB[:, n % 4, 0:D], scalar=gate, in1=x,
                                                 op0=ALU.mult, op1=ALU.add).then_inc(kept, 1)
            steps(dve, body)
            dve.wait_ge(kept, 1 + nb * NTG * (ne // pair))


def pick_tokens(nc, k, tag, scores, gates, n_best):
    flat = nc.dram_tensor(f"{tag}_scores", (NT, P), F32, kind="Internal").ap()
    with stage(nc, tag) as st:
        sc = st.sb("sc", [P, NT])
        row = st.sb("row", [P, NP])
        cmp = st.sb("cmp", [P, 2, NP])
        low = st.sb("low", [P, P])
        cnt = st.sb("cnt", [P, NT, 3])
        rank = st.sb("rank", [P, NT])
        order, lows, moved, counted = (st.sem(s) for s in ("order", "lows", "moved", "counted"))
        block = st.block()

        @block.gpsimd
        def _(pool):
            pool.memset(low[:], 1.0).then_inc(lows, 1)
            pool.wait_ge(lows, 1 + 1)
            pool.affine_select(out=low[:], in_=low[:], compare_op=ALU.is_gt, fill=0.0, base=0,
                               pattern=[[-1, P]], channel_multiplier=1).then_inc(lows, 1)

        @block.sync
        def _(sp):
            sp.wait_ge(order, 1 + 3)
            sp.dma_start(flat.rearrange("t p -> p t"), sc[:], allow_slow_non_contiguous=True).then_inc(moved, 16)
            sp.wait_ge(moved, 1 + 16)
            sp.dma_start(row[:], flat.rearrange("t p -> (t p)").partition_broadcast(P)).then_inc(moved, 16)

        @block.vector
        def _(dve):
            at = [0]

            def then(ins):
                at[0] += 1
                ins.then_inc(order, 1)
                dve.wait_ge(order, 1 + at[0])

            then(dve.tensor_scalar(sc[:], scores, 0.0, None, ALU.add))
            then(dve.scalar_tensor_tensor(out=sc[:, NT - 1:NT], in0=k.past_end[:], scalar=-BIG, in1=sc[:, NT - 1:NT],
                                          op0=ALU.mult, op1=ALU.add))
            then(dve.memset(cnt[:], 0.0))
            dve.wait_ge(moved, 1 + 32)
            dve.wait_ge(lows, 1 + 2)
            n = 0
            for t in range(NT):
                own = sc[:, t:t + 1]
                steps = [
                    lambda o: dve.tensor_scalar(o[:, t * P:NP], row[:, t * P:NP], own, 0.0, ALU.is_gt, ALU.add,
                                                accum_out=cnt[:, t, 0:1]),
                    lambda o: dve.scalar_tensor_tensor(out=o[:, 0:P], in0=row[:, t * P:(t + 1) * P], scalar=own,
                                                       in1=low[:], op0=ALU.is_equal, op1=ALU.mult,
                                                       accum_out=cnt[:, t, 1:2]),
                ]
                if t:
                    steps.append(lambda o: dve.tensor_scalar(o[:, 0:t * P], row[:, 0:t * P], own, 0.0, ALU.is_ge,
                                                             ALU.add, accum_out=cnt[:, t, 2:3]))
                for step in steps:
                    if n >= 2:
                        dve.wait_ge(counted, 1 + n - 1)
                    step(cmp[:, n % 2, :]).then_inc(counted, 1)
                    n += 1
            dve.wait_ge(counted, 1 + n)
            then(dve.tensor_reduce(rank[:], cnt[:], AX.X, ALU.add))
            then(dve.scalar_tensor_tensor(out=gates, in0=rank[:], scalar=float(n_best), in1=scores,
                                          op0=ALU.is_lt, op1=ALU.mult))


class Softplus:

    def __init__(self, st, name, shape):
        self.ab, self.ex = st.sb(f"{name}_ab", shape), st.sb(f"{name}_ex", shape)
        self.has_abs, self.has_exp, self.has_log, self.done = (
            st.sem(f"{name}_{s}") for s in ("abs", "exp", "log", "done"))

    def dve_first(self, dve, src):
        dve.scalar_tensor_tensor(out=self.ab[:], in0=src, scalar=-1.0, in1=src, op0=ALU.mult, op1=ALU.max)\
           .then_inc(self.has_abs, 1)

    def act_part(self, act, n):
        act.wait_ge(self.has_abs, 1 + n + 1)
        act.activation(self.ex[:], self.ab[:], ACT.Exp, scale=-1.0).then_inc(self.has_exp, 1)
        act.wait_ge(self.has_exp, 1 + n + 1)
        act.activation(self.ex[:], self.ex[:], ACT.Ln, bias=1.0).then_inc(self.has_log, 1)

    def dve_last(self, dve, src, ex, dst):
        return dve.scalar_tensor_tensor(out=dst, in0=src, scalar=0.0, in1=ex, op0=ALU.max, op1=ALU.add)


def atom_tables(nc, k, tag, w, b, table, acc):
    kc = D // P
    wide = 2 * D
    with stage(nc, tag) as st:
        W = st.sb("W", [P, kc, wide])
        B = st.sb("B", [1, wide])
        XN = st.sb("XN", [P, TG, D])
        XP = st.sb("XP", [P, TG, D])
        XS = st.sb("XS", [P, TG, kc, P])
        PRE = st.sb("PRE", [P, TG, wide])
        ROW = st.sb("ROW", [P, TG, D])
        norm = Norm(st, "n")
        sp1 = Softplus(st, "s1", [P, TG, D])
        sp2 = Softplus(st, "s2", [P, TG, wide])
        psT = st.ps("psT", [P, 2, 512])
        psH = st.ps("psH", [P, 2, 512])
        w_in, turned, turned_out, made, pre_out, ready, stored, own = (
            st.sem(s) for s in ("w_in", "turned", "turned_out", "made", "pre_out", "ready", "stored", "own"))
        block = st.block()

        @block.sync
        def _(sp):
            sp.dma_start(W[:], w.rearrange("(k p) c -> p k c", p=P)).then_inc(w_in, 16)
            sp.dma_start(B[:], b.unsqueeze(0)).then_inc(w_in, 16)
            with sp.Fori(0, NTG) as it:
                sp.wait_ge(sp2.done, 1 + it * 2 + 2)
                sp.dma_start(table[ds(it * TOK, TOK), :].rearrange("(t p) d -> p t d", p=P), ROW[:]).then_inc(stored, 16)
            sp.wait_ge(stored, 1 + 16 * NTG)

        @block.vector
        def _(dve):
            with dve.Fori(0, NTG) as it:
                def x_tile(u):
                    return k.X[:, ds(it * TG + u, 1), :].squeeze(1)
                norm.dve_first(dve, it, x_tile)
                norm.dve_apply(dve, it, x_tile, lambda u: XN[:, u, :])
                dve.wait_ge(norm.applied, 1 + it * TG + TG)
                sp1.dve_first(dve, XN[:])
                dve.wait_ge(sp1.has_log, 1 + it + 1)
                dve.wait_ge(turned, 1 + it * TG)
                sp1.dve_last(dve, XN[:], sp1.ex[:], XP[:]).then_inc(own, 1)
                dve.wait_ge(own, 1 + it + 1)
                dve.tensor_scalar(XP[:], XP[:], -LN2, None, ALU.add).then_inc(sp1.done, 1)
                dve.wait_ge(pre_out, 1 + it * TG + TG)
                sp2.dve_first(dve, PRE[:])
                dve.wait_ge(sp2.has_log, 1 + it + 1)
                sp2.dve_last(dve, PRE[:, :, 0:D], sp2.ex[:, :, 0:D], acc[:, ds(it * TG, TG), :]).then_inc(sp2.done, 1)
                dve.wait_ge(stored, 1 + it * 16)
                sp2.dve_last(dve, PRE[:, :, D:wide], sp2.ex[:, :, D:wide], ROW[:]).then_inc(sp2.done, 1)

        @block.tensor
        def _(pe):
            pe.wait_ge(w_in, 1 + 32)
            with pe.Fori(0, NTG) as it:
                def free(u):
                    return it * TG if u < 2 else it * TG + u - 1
                for u in range(TG):
                    pe.wait_ge(sp1.done, 1 + it + 1)
                    pe.wait_ge(turned_out, 1 + free(u))
                    for s in range(kc):
                        ins = pe.transpose(psT[:, u % 2, s * P:(s + 1) * P], XP[:, u, s * P:(s + 1) * P], k.ident[:])
                    ins.then_inc(turned, 1)
                for u in range(TG):
                    pe.wait_ge(turned_out, 1 + it * TG + u + 1)
                    pe.wait_ge(pre_out, 1 + free(u))
                    for s in range(kc):
                        pe.matmul(psH[:, u % 2, :], XS[:, u, s, :], W[:, s, :], start=(s == 0), stop=False)
                    pe.matmul(psH[:, u % 2, :], k.ones[0:1, :], B[:], start=False, stop=True).then_inc(made, 1)

        @block.scalar
        def _(act):
            with act.Fori(0, NTG) as it:
                norm.act_root(act, it)
                sp1.act_part(act, it)
                for u in range(TG):
                    act.wait_ge(turned, 1 + it * TG + u + 1)
                    act.wait_ge(made, 1 + it * TG)
                    act.activation(XS[:, u, :, :], psT[:, u % 2, 0:D].rearrange("p (k q) -> p k q", q=P), ACT.Copy)\
                       .then_inc(turned_out, 1)
                act.wait_ge(sp2.done, 1 + it * 2)
                for u in range(TG):
                    act.wait_ge(made, 1 + it * TG + u + 1)
                    act.activation(PRE[:, u, :], psH[:, u % 2, :], ACT.Copy).then_inc(pre_out, 1)
                sp2.act_part(act, it)


def edge_filter(nc, k, tag, table, records, gt, other, local, tile_of, acc):
    nf = gt.shape[0]
    n_loop = tile_of.shape[1] // U - 1
    by_part = records.rearrange("(p c) w -> p c w", p=P)
    with stage(nc, tag) as st:
        IDX = st.sb("IDX", [P, U, G], I32)
        ROWS = st.sb("ROWS", [P, U, G, D])
        S = st.sb("S", [P, U, G, P])
        FE = st.sb("FE", [P, U, G, nf], I32)
        FT = st.sb("FT", [nf, U, G, P])
        GT = st.sb("GT", [nf, D])
        psF = st.ps("psF", [P, 2, 512])
        psM = st.ps("psM", [P, 2, 512])
        psO = st.ps("psO", [P, 2, 512])
        q = {s: st.sem(s) for s in ("g_in", "idx_made", "sel", "attr_t", "attr_out", "filtered", "scaled",
                                    "summed", "kept")}
        gathered = [[st.gather_sem(f"gathered{u}_{i}") for i in range(G)] for u in range(U)]
        attr_in = [st.sem(f"attr_in{u}") for u in range(U)]
        block = st.block()

        @block.sync
        def _(sp):
            sp.dma_start(GT[:], gt).then_inc(q["g_in"], 16)

            def load(it, j):
                g, v = it * U + j, j % U
                need(sp, q["attr_t"], it, j - (U - 1))
                sp.dma_start(FE[:, v, :, :], by_part[:, ds(g * G, G), 2:2 + nf]).then_inc(attr_in[v], 16)

            for j in range(U):
                load(0, j)
            with sp.Fori(0, n_loop) as it:
                for j in range(U):
                    load(it, j + U)
            for v in range(U):
                sp.wait_ge(attr_in[v], 1 + 16 * (n_loop + 1))

        @block.gpsimd
        def _(pool):
            def gather(it, j):
                g, v = it * U + j, j % U
                pool.wait_ge(q["idx_made"], 1 + g + 1)
                need(pool, q["summed"], it, j - (U - 1))
                pool.nop(nofuse=True)
                for i in range(G):
                    pool.indirect_dma_start(out=ROWS[:, v, i, :], out_offset=None, in_=table,
                                            in_offset=bass.IndirectOffsetOnAxis(ap=IDX[:, v, i:i + 1], axis=0))\
                        .then_inc(gathered[v][i], 16)

            for j in range(U):
                gather(0, j)
            with pool.Fori(0, n_loop) as it:
                for j in range(U):
                    gather(it, j + U)

        @block.scalar
        def _(act):
            def index(it, j):
                g, v, n = it * U + j, j % U, it + j // U
                for i in range(G):
                    if not isinstance(n, int) or n > 0:
                        act.wait_ge(gathered[v][i], n * 16)
                act.activation(IDX[:, v, :], other[:, ds(g * G, G)], ACT.Copy).then_inc(q["idx_made"], 1)

            def turn(it, j):
                g, v = it * U + j, j % U
                act.wait_ge(q["attr_t"], 1 + g + 1)
                need(act, q["filtered"], it, j - (U - 1))
                act.activation(FT[:, v, :, :], psF[0:nf, v % 2, 0:G * P].rearrange("p (i n) -> p i n", n=P), ACT.Copy)\
                   .then_inc(q["attr_out"], 1)

            def body(it, j):
                ahead(turn, it, j + 4)
                ahead(index, it, j + U)

            for j in range(-U, 0):
                body(0, j)
            with act.Fori(0, n_loop) as it:
                for j in range(U):
                    body(it, j)

        @block.tensor
        def _(pe):
            pe.wait_ge(q["g_in"], 1 + 16)

            def add_up(it, j):
                g, v = it * U + j, j % U
                pe.wait_ge(q["scaled"], 1 + g + 1)
                need(pe, q["kept"], it, j - 1)
                for i in range(G):
                    ins = pe.matmul(psO[:, v % 2, 0:D], S[:, v, i, :], ROWS[:, v, i, :],
                                    start=(i == 0), stop=(i == G - 1))
                ins.then_inc(q["summed"], 1)

            def filt(it, j):
                g, v = it * U + j, j % U
                pe.wait_ge(q["attr_out"], 1 + g + 1)
                need(pe, q["scaled"], it, j - 1)
                for i in range(G):
                    ins = pe.matmul(psM[:, v % 2, i * D:(i + 1) * D], FT[:, v, i, :], GT[:], start=True, stop=True)
                ins.then_inc(q["filtered"], 1)

            def turn(it, j):
                g, v, n = it * U + j, j % U, it + j // U + 1
                pe.wait_ge(attr_in[v], 1 + n * 16)
                need(pe, q["attr_out"], it, j - 1)
                pe.nop(nofuse=True)
                for i in range(G):
                    ins = pe.transpose(psF[0:nf, v % 2, i * P:(i + 1) * P], FE[:, v, i, :].bitcast(F32), k.ident[:])
                ins.then_inc(q["attr_t"], 1)

            def body(it, j):
                ahead(turn, it, j + 4)
                ahead(filt, it, j + 2)
                ahead(add_up, it, j + 1)

            for j in range(-U, 0):
                body(0, j)
            with pe.Fori(0, n_loop) as it:
                for j in range(U):
                    body(it, j)

        @block.vector
        def _(dve):
            def scale_rows(it, j):
                g, v, n = it * U + j, j % U, it + j // U + 1
                dve.wait_ge(q["filtered"], 1 + g + 1)
                for i in range(G):
                    dve.wait_ge(gathered[v][i], n * 16)
                r = ROWS[:, v, :, :].rearrange("p i d -> p (i d)")
                dve.tensor_tensor(r, psM[:, v % 2, :], r, ALU.mult).then_inc(q["scaled"], 1)

            def keep_sum(it, j, tile):
                g, v = it * U + j, j % U
                dve.wait_ge(q["summed"], 1 + g + 1)
                need(dve, q["kept"], it, j)
                a = acc[:, ds(tile, 1), :].squeeze(1)
                dve.tensor_tensor(a, psO[:, v % 2, 0:D], a, ALU.add).then_inc(q["kept"], 1)

            def select(it, j):
                g, v = it * U + j, j % U
                need(dve, q["summed"], it, j - (U - 1))
                dve.tensor_tensor(S[:, v, :, :], k.iota[:].unsqueeze(1).broadcast_to([P, G, P]),
                                  local[:, ds(g * G, G)].unsqueeze(2).broadcast_to([P, G, P]), ALU.is_equal)\
                   .then_inc(q["sel"], 1)

            def body(it, j, tile):
                ahead(scale_rows, it, j + 1)
                ahead(keep_sum, it, j, tile)
                ahead(select, it, j + 5)

            for j in range(-U, 0):
                body(0, j, None)
            with dve.Fori(0, n_loop) as it:
                tiles = tile_ids(nc, mybir.EngineType.DVE, tile_of, it * U)
                for j in range(U):
                    body(it, j, tiles[j])
            for v in range(U):
                for i in range(G):
                    dve.wait_ge(gathered[v][i], 16 * (n_loop + 1))


def residual_blocks(nc, k, tag, acc, VT, r1, b1, r2, b2):
    kc = D // P
    nb = r1.shape[0]
    with stage(nc, tag) as st:
        R1, R2 = st.sb("R1", [P, nb, kc, D]), st.sb("R2", [P, nb, kc, D])
        B1, B2 = st.sb("B1", [P, nb, kc]), st.sb("B2", [P, nb, kc])
        PRE = st.sb("PRE", [P, 2, kc, TOK])
        HS = st.sb("HS", [P, 2, kc, TOK])
        soft = Softplus(st, "s", [P, kc, TOK])
        w_in, turned, turned_out, made, pre_out, out_made, updated = (
            st.sem(s) for s in ("w_in", "turned", "turned_out", "made", "pre_out", "out_made", "updated"))
        psA = st.ps("psA", [P, kc, 2, 512])
        psB = st.ps("psB", [P, kc, 2, 512])
        block = st.block()

        @block.sync
        def _(sp):
            sp.dma_start(R1[:], r1.rearrange("b (k p) c -> p b k c", p=P)).then_inc(w_in, 16)
            sp.dma_start(R2[:], r2.rearrange("b (k p) c -> p b k c", p=P)).then_inc(w_in, 16)
            sp.dma_start(B1[:], b1.rearrange("b p k -> p b k")).then_inc(w_in, 16)
            sp.dma_start(B2[:], b2.rearrange("b p k -> p b k")).then_inc(w_in, 16)
            sp.wait_ge(w_in, 1 + 64)

        @block.tensor
        def _(pe):
            for t in range(NT):
                if t >= 4:
                    pe.wait_ge(turned_out, 1 + t - 3)
                for s in range(kc):
                    ins = pe.transpose(psA[:, (t // 2) % 2, t % 2, s * P:(s + 1) * P], acc[:, t, s * P:(s + 1) * P],
                                       k.ident[:])
                ins.then_inc(turned, 1)
            pe.wait_ge(w_in, 1 + 64)
            pe.wait_ge(turned_out, 1 + NT)

            def first(b, g):
                n = b * NTG + g
                if b:
                    pe.wait_ge(updated, 1 + (n - NTG) * kc + kc)
                for c in range(kc):
                    if b or not isinstance(g, int) or g:
                        pe.wait_ge(pre_out, 1 + (n - 1) * kc + c + 1)
                    for half in range(2):
                        for i in range(kc):
                            ins = pe.matmul(psA[:, c, half, 0:HALF], R1[:, b, i, c * P:(c + 1) * P],
                                            VT[:, i, ds(g * TOK + half * HALF, HALF)],
                                            start=(i == 0), stop=(i == kc - 1))
                    ins.then_inc(made, 1)

            def second(b, g):
                n = b * NTG + g
                pe.wait_ge(soft.done, 1 + n + 1)
                if b or not isinstance(g, int):
                    pe.wait_ge(updated, 1 + n * kc)
                for c in range(kc):
                    for half in range(2):
                        for i in range(kc):
                            ins = pe.matmul(psB[:, c, half, 0:HALF], R2[:, b, i, c * P:(c + 1) * P],
                                            half_of(HS, b, g, i, half), start=(i == 0), stop=(i == kc - 1))
                    ins.then_inc(out_made, 1)

            def half_of(h, b, g, i, half):
                return h[:, 0, i, half * HALF:(half + 1) * HALF]

            for b in range(nb):
                first(b, 0)
                with pe.Fori(0, NTG - 1) as g:
                    first(b, g + 1)
                    second(b, g)
                second(b, NTG - 1)

        @block.scalar
        def _(act):
            for t in range(NT):
                act.wait_ge(turned, 1 + t + 1)
                act.activation(VT[:, :, t * P:(t + 1) * P],
                               psA[:, (t // 2) % 2, t % 2, 0:D].rearrange("p (k q) -> p k q", q=P), ACT.Copy)\
                   .then_inc(turned_out, 1)
            act.wait_ge(w_in, 1 + 64)

            def part(b, g):
                n = b * NTG + g
                for c in range(kc):
                    act.wait_ge(made, 1 + n * kc + c + 1)
                    if b or not isinstance(g, int) or g:
                        act.wait_ge(soft.done, 1 + n)
                    act.activation(PRE[:, 0, c, :].rearrange("p (a t) -> p a t", a=2), psA[:, c, :, 0:HALF],
                                   ACT.Identity, bias=B1[:, b, c:c + 1]).then_inc(pre_out, 1)
                soft.act_part(act, n)

            for b in range(nb):
                part(b, 0)
                with act.Fori(0, NTG - 1) as g:
                    part(b, g + 1)

        @block.vector
        def _(dve):
            dve.wait_ge(turned_out, 1 + NT)

            def first(b, g):
                n = b * NTG + g
                dve.wait_ge(pre_out, 1 + n * kc + kc)
                soft.dve_first(dve, PRE[:, 0, :, :])

            def last(b, g):
                n = b * NTG + g
                dve.wait_ge(soft.has_log, 1 + n + 1)
                soft.dve_last(dve, PRE[:, 0, :, :], soft.ex[:], HS[:, 0, :, :]).then_inc(soft.done, 1)

            def update(b, g):
                n = b * NTG + g
                for c in range(kc):
                    dve.wait_ge(out_made, 1 + n * kc + c + 1)
                    v = VT[:, c, ds(g * TOK, TOK)].rearrange("p (a t) -> p a t", a=2)
                    dve.scalar_tensor_tensor(out=v, in0=psB[:, c, :, 0:HALF], scalar=B2[:, b, c:c + 1], in1=v,
                                             op0=ALU.add, op1=ALU.add).then_inc(updated, 1)

            for b in range(nb):
                first(b, 0)
                last(b, 0)
                with dve.Fori(0, NTG - 1) as g:
                    first(b, g + 1)
                    update(b, g)
                    last(b, g + 1)
                update(b, NTG - 1)
            dve.wait_ge(updated, 1 + nb * NTG * kc)


def project_out(nc, k, tag, VT, w, b):
    kc = D // P
    with stage(nc, tag) as st:
        W = st.sb("W", [P, kc, D])
        B = st.sb("B", [1, D])
        Z = st.sb("Z", [P, kc, TOK])
        soft = Softplus(st, "s", [P, kc, TOK])
        psO = st.ps("psO", [P, 4, 512])
        w_in, made, kept = (st.sem(s) for s in ("w_in", "made", "kept"))
        block = st.block()

        @block.sync
        def _(sp):
            sp.dma_start(W[:], w.rearrange("(k p) c -> p k c", p=P)).then_inc(w_in, 16)
            sp.dma_start(B[:], b.unsqueeze(0)).then_inc(w_in, 16)

        @block.scalar
        def _(act):
            with act.Fori(0, NTG) as it:
                soft.act_part(act, it)

        @block.vector
        def _(dve):
            with dve.Fori(0, NTG) as it:
                v = VT[:, :, ds(it * TOK, TOK)]
                soft.dve_first(dve, v)
                dve.wait_ge(soft.has_log, 1 + it + 1)
                dve.wait_ge(made, 1 + it * TG)
                soft.dve_last(dve, v, soft.ex[:], Z[:]).then_inc(soft.done, 1)
                for u in range(TG):
                    dve.wait_ge(made, 1 + it * TG + u + 1)
                    x = k.X[:, ds(it * TG + u, 1), :].squeeze(1)
                    dve.tensor_tensor(x, x, psO[:, u % 4, 0:D], ALU.add).then_inc(kept, 1)
            dve.wait_ge(kept, 1 + NT)

        @block.tensor
        def _(pe):
            pe.wait_ge(w_in, 1 + 32)
            with pe.Fori(0, NTG) as it:
                pe.wait_ge(soft.done, 1 + it + 1)
                for u in range(TG):
                    pe.wait_ge(kept, 1 + (it * TG if u < 4 else it * TG + u - 3))
                    for i in range(kc):
                        pe.matmul(psO[:, u % 4, 0:D], Z[:, i, u * P:(u + 1) * P], W[:, i, :],
                                  start=(i == 0), stop=False)
                    pe.matmul(psO[:, u % 4, 0:D], k.ones[0:1, :], B[:], start=False, stop=True).then_inc(made, 1)


def expert_scores(nc, k, tag, acc, na, bias, gamma, beta, scores):
    f1 = acc.shape[2] // na
    hd = f1 - 1
    nf = na * hd
    whole = [P, NT, nf]
    with stage(nc, tag) as st:
        rows = st.sb("rows", [P, 3, nf])
        rec, m, v, sd, rs = (st.sb(n, [P, NT]) for n in ("rec", "m", "v", "sd", "rs"))
        den = st.sb("den", [P, NT, na])
        h, c2 = st.sb("h", whole), st.sb("c2", whole)
        in_, order, root = (st.sem(s) for s in ("in", "order", "root"))
        at_var = []
        block = st.block()

        @block.sync
        def _(sp):
            for n, r in enumerate((bias, gamma, beta)):
                sp.dma_start(rows[:, n, :], r.partition_broadcast(P)).then_inc(in_, 16)

        @block.vector
        def _(dve):
            at = [0]

            def then(ins):
                at[0] += 1
                ins.then_inc(order, 1)
                dve.wait_ge(order, 1 + at[0])

            view = acc.rearrange("p t (h f) -> p t h f", f=f1)
            h4 = h[:].rearrange("p t (h f) -> p t h f", f=hd)
            dve.wait_ge(in_, 1 + 48)
            then(dve.tensor_scalar(den[:], view[:, :, :, hd], 1e-16, None, ALU.add))
            then(dve.reciprocal(den[:], den[:]))
            for a in range(na):
                ins = dve.tensor_tensor(h4[:, :, a, :], view[:, :, a, 0:hd],
                                        den[:, :, a:a + 1].broadcast_to([P, NT, hd]), ALU.mult)
            then(ins)
            then(dve.tensor_tensor(h[:], h[:], rows[:, 0:1, :].broadcast_to(whole), ALU.add))
            then(dve.tensor_reduce(m[:], h[:], AX.X, ALU.add))
            then(dve.scalar_tensor_tensor(out=h[:], in0=m[:].unsqueeze(2).broadcast_to(whole), scalar=-1.0 / nf,
                                          in1=h[:], op0=ALU.mult, op1=ALU.add))
            then(dve.tensor_tensor(c2[:], h[:], h[:], ALU.mult))
            then(dve.tensor_reduce(rec[:], c2[:], AX.X, ALU.add))
            then(dve.tensor_scalar(v[:], rec[:], 1.0 / nf, LN_EPS, ALU.mult, ALU.add))
            at_var.append(at[0])
            dve.wait_ge(root, 1 + 1)
            then(dve.reciprocal(rs[:], sd[:]))
            then(dve.tensor_tensor(h[:], h[:], rs[:].unsqueeze(2).broadcast_to(whole), ALU.mult))
            then(dve.tensor_tensor(h[:], h[:], rows[:, 1:2, :].broadcast_to(whole), ALU.mult))
            then(dve.tensor_tensor(h[:], h[:], rows[:, 2:3, :].broadcast_to(whole), ALU.add))
            then(dve.tensor_reduce(scores, h[:].rearrange("p t (h f) -> p t f h", f=hd), AX.X, ALU.add))
            then(dve.tensor_scalar(scores, scores, 1.0 / na, None, ALU.mult))

        @block.scalar
        def _(act):
            act.wait_ge(order, 1 + at_var[0])
            act.activation(sd[:], v[:], ACT.Sqrt).then_inc(root, 1)


def program(nc, a, out, upto=99):
    with ExitStack() as ctx:
        k = Consts()

        def sb(name, shape, dt=F32):
            return ctx.enter_context(nc.sbuf_tensor(name, shape, dt))

        k.X = sb("X", [P, NT, D])
        k.ident = sb("ident", [P, P])
        k.tri = sb("tri", [P, P])
        k.ones = sb("ones", [P, P])
        k.iota = sb("iota", [P, P])
        k.past_end = sb("past_end", [P, 1])
        setup(nc, k, a["x"])
        n_groups = groups_of(a["src"].shape[0] * a["src"].shape[1])
        cols = n_groups * G
        rw = 2 + a["attr"].shape[2]
        by_src = [sb("src_other", [P, cols], I32), sb("src_local", [P, cols]), sb("src_tile", [1, n_groups], I32)]
        by_dst = [sb("dst_other", [P, cols], I32), sb("dst_local", [P, cols]), sb("dst_tile", [1, n_groups], I32)]
        rg = groups_of(a["rdst"].shape[0] * a["rdst"].shape[1])
        rcols = rg * G
        r_tile = sb("r_tile", [1, rg], I32)
        src_table = nc.dram_tensor("src_table", (P * cols, rw), I32, kind="Internal").ap()
        dst_table = nc.dram_tensor("dst_table", (P * cols, 2), I32, kind="Internal").ap()
        rtable = nc.dram_tensor("router_table", (P * rcols, 2), I32, kind="Internal").ap()
        pb, m = a["src"].shape
        rb, rm = a["rdst"].shape
        S = [t[:] for t in by_src]
        late = ExitStack()
        dst_row, r_row = (late.enter_context(nc.sbuf_tensor(n, s, I32)) for n, s in
                          (("dst_row", [pb, m]), ("r_row", [rb, rm])))
        dst_rec, r_rec = (late.enter_context(nc.sbuf_tensor(n, s, I32)) for n, s in
                          (("dst_rec", [pb, m, 2]), ("r_rec", [rb, rm, 2])))
        table0 = nc.dram_tensor("table0", (NP, 260), F32, kind="Internal").ap()
        with nc.sbuf_tensor("near0", [P, NT, 4], F32) as near, ExitStack() as acc_at:
            with nc.sbuf_tensor("src_row", [pb, m], I32) as row, nc.sbuf_tensor("src_rec", [pb, m, rw], I32) as rec:
                place_edges(nc, k, "os", a["src"], a["dst"], a["attr"], src_table, row[:], rec[:], by_src[2][:])
                def part(start, end):
                    return [(row[:], rec[:], src_table, start, end)]
                cuts = [0, 80, 144, 224, m]
                place_edges(nc, k, "od", a["dst"], a["src"], None, dst_table, dst_row[:], dst_rec[:], by_dst[2][:],
                            jobs=part(cuts[0], cuts[1]))
                place_edges(nc, k, "or", a["rdst"], a["rsrc"], None, rtable, r_row[:], r_rec[:], r_tile[:],
                            jobs=part(cuts[1], cuts[2]))
                make_table(nc, k, "t0", a["W0"], a["a0f"], a["a0n"], table0, near[:], guard=True,
                           jobs=part(cuts[2], cuts[3]))
                scatter_edges(nc, "os_rest", part(cuts[3], cuts[4]))
            read_slots(nc, "os_read", src_table, *S[0:2])
            if upto >= 1:
                acc = acc_at.enter_context(nc.sbuf_tensor("acc0", [P, NT, 260], F32))
                edge_pass(nc, k, "e0", table0, *S, near[:], acc[:], guard=True)
                finish_attention(nc, k, "f0", acc[:], 4, 64, 2, True)
        if upto >= 2:
            with (nc.sbuf_tensor("XT1", [P, D // P, NP], F32) as XT, nc.sbuf_tensor("logits1", [P, NT, 6], F32) as lg,
                  nc.sbuf_tensor("gates1", [P, 6, NT], F32) as gates):
                tokens(nc, k, "k1", XT[:], lg[:], a["rw2"], a["rb2"], hidden=(a["rw1"], a["rb1"]))
                choose(nc, k, "c1", lg[:], gates[:], probs=True, renorm=False)
                add_bias(nc, k, "b1", gates[:], a["eb3"])
                feed_forward(nc, k, "m1", XT[:], a["ew1"], a["eb1"], a["ew3"], gates[:], ACT.Relu,
                             mid=(a["ew2"], a["eb2"]))
        if upto >= 3:
            with nc.sbuf_tensor("acc2", [P, NT, 258], F32) as acc, nc.sbuf_tensor("near2", [P, NT, 2], F32) as near:
                table = nc.dram_tensor("table2", (NP, 258), F32, kind="Internal").ap()
                make_table(nc, k, "t2", a["W1"], a["a1f"], a["a1n"], table, near[:], bias=a["b1"])
                edge_pass(nc, k, "e2", table, *S, near[:], acc[:])
                finish_attention(nc, k, "f2", acc[:], 2, 128, 1, False)
        late_jobs = [(dst_row[:], dst_rec[:], dst_table, 0, m), (r_row[:], r_rec[:], rtable, 0, rm)]
        if upto >= 4:
            with (nc.sbuf_tensor("XT3", [P, D // P, NP], F32) as XT, nc.sbuf_tensor("logits3", [P, NT, 8], F32) as lg,
                  nc.sbuf_tensor("gates3", [P, 8, NT], F32) as gates):
                tokens(nc, k, "k3", XT[:], lg[:], a["Wr"], a["br"], twice=True)
                choose(nc, k, "c3", lg[:], gates[:], probs=True, renorm=True)
                add_bias(nc, k, "b3", gates[:], a["mb2"])
                feed_forward(nc, k, "m3", XT[:], a["mW1"], a["mb1"], a["mW2"], gates[:], ACT.Gelu, affine=a["affine"],
                             jobs=late_jobs)
        else:
            scatter_edges(nc, "late", late_jobs)
        late.close()
        if upto >= 5:
            with (nc.sbuf_tensor("acc4", [P, NT, D + 1], F32) as acc, nc.sbuf_tensor("near4", [P, NT, 1], F32) as near,
                  nc.sbuf_tensor("shift4", [P, 1], F32) as shift,
                  nc.sbuf_tensor("base4", [P, NT, 1], F32) as base, nc.sbuf_tensor("h4", [P, NT, D], F32) as h4):
                read_slots(nc, "od_read", dst_table, by_dst[0][:], by_dst[1][:])
                soft = (shift[:], base[:])
                for r in range(2):
                    table = nc.dram_tensor(f"table4_{r}", (NP, D + 1), F32, kind="Internal").ap()
                    make_table(nc, k, f"t4{r}", a["W2"][r], a["a2f"][r], a["a2n"][r], table, near[:], acc[:],
                               softmax=soft, plain=h4[:] if r else None)
                    edge_pass(nc, k, f"e4{r}", table, *(t[:] for t in by_dst), near[:], acc[:], softmax=soft)
                    finish_conv(nc, k, f"f4{r}", acc[:], a["b2"][r], h4[:] if r == 0 else k.X[:], r == 0, r == 1)
        if upto >= 6:
            with (nc.sbuf_tensor("XT5", [P, D // P, NP], F32) as XT, nc.sbuf_tensor("score5", [P, NT, 1], F32) as sc,
                  nc.sbuf_tensor("gates5", [P, 1, NT], F32) as gates):
                tokens(nc, k, "k5", XT[:], sc[:], a["wr"], a["br5"], keep=True)
                pick_tokens(nc, k, "p5", sc[:].squeeze(2), gates[:].squeeze(1), N // 2 - 1)
                add_bias(nc, k, "b5", gates[:], a["fb2"])
                feed_forward(nc, k, "m5", XT[:], a["fw1"], a["fb1"], a["fw2"], gates[:], ACT.Gelu_apprx_tanh)
        if upto >= 7:
            with nc.sbuf_tensor("acc6", [P, NT, D], F32) as acc, nc.sbuf_tensor("VT6", [P, D // P, NP], F32) as VT:
                table = nc.dram_tensor("table6", (NP, D), F32, kind="Internal").ap()
                atom_tables(nc, k, "t6", a["Wij"], a["bij"], table, acc[:])
                edge_filter(nc, k, "e6", table, src_table, a["GT"], *S, acc[:])
                residual_blocks(nc, k, "r6", acc[:], VT[:], a["res1"], a["resb1"], a["res2"], a["resb2"])
                project_out(nc, k, "o6", VT[:], a["Wv"], a["bv"])
        if upto >= 8:
            with (nc.sbuf_tensor("sc7", [P, NT, 4], F32) as scores, nc.sbuf_tensor("gates7", [P, 4, NT], F32) as gates):
                with (nc.sbuf_tensor("acc7", [P, NT, 20], F32) as acc, nc.sbuf_tensor("near7", [P, NT, 4], F32) as near,
                      nc.sbuf_tensor("shift7", [P, 4], F32) as shift,
                      nc.sbuf_tensor("base7", [P, NT, 4], F32) as base, nc.sbuf_tensor("r_other", [P, rcols], I32) as ro,
                      nc.sbuf_tensor("r_local", [P, rcols], F32) as rl):
                    read_slots(nc, "or_read", rtable, ro[:], rl[:])
                    soft = (shift[:], base[:])
                    table = nc.dram_tensor("table7", (NP, 20), F32, kind="Internal").ap()
                    make_table(nc, k, "t7", a["W3"], a["a3f"], a["a3n"], table, near[:], acc[:], softmax=soft)
                    edge_pass(nc, k, "e7", table, ro[:], rl[:], r_tile[:], near[:], acc[:], softmax=soft)
                    expert_scores(nc, k, "s7", acc[:], 4, a["gb"], a["lg"], a["lb"], scores[:])
                choose(nc, k, "c7", scores[:], gates[:], probs=False, renorm=False)
                with nc.sbuf_tensor("XT7", [P, D // P, NP], F32) as XT:
                    tokens(nc, k, "k7", XT[:])
                    add_bias(nc, k, "b7", gates[:], a["xb2"])
                    feed_forward(nc, k, "m7", XT[:], a["xw1"], a["xb1"], a["xw2"], gates[:], ACT.Gelu)
        with stage(nc, "out") as st:
            stored = st.sem("stored")
            block = st.block()

            @block.sync
            def _(sp):
                full = (NT - 1) * P
                sp.dma_start(out[0:full, :].rearrange("(t p) d -> p t d", p=P), k.X[:, 0:NT - 1, :]).then_inc(stored, 16)
                sp.dma_start(out[full:N, :], k.X[0:REST, NT - 1, :]).then_inc(stored, 16)
                sp.wait_ge(stored, 1 + 32)


def layout(inputs):
    import numpy as np

    def arr(x):
        return np.ascontiguousarray(x)

    def chunks(x):
        return np.ascontiguousarray(x.reshape(x.shape[0], -1, P).transpose(0, 2, 1))

    i = {n: np.asarray(v) for n, v in inputs.items()}
    e = i["src"].shape[0]
    m = e // 125
    a0, a1 = i["L0_gnn_a"], i["L1_gnn_a"]
    return {
        "x": arr(i["x"]),
        "src": arr(i["src"].reshape(125, m)),
        "dst": arr(i["dst"].reshape(125, m)),
        "attr": arr(i["edge_attr_64"].reshape(125, m, 64).view(np.int32)),
        "W0": arr(i["L0_gnn_W"].transpose(1, 0, 2).reshape(D, D)),
        "a0n": arr(a0[:, 0, :64].reshape(-1)),
        "a0f": arr(a0[:, 0, 64:].reshape(-1)),
        "rw1": arr(i["L0_ffn_router_w1"]),
        "rb1": arr(i["L0_ffn_router_b1"]),
        "rw2": arr(i["L0_ffn_router_w2"]),
        "rb2": arr(i["L0_ffn_router_b2"]),
        "ew1": arr(i["L0_ffn_expert_w1"]),
        "eb1": chunks(i["L0_ffn_expert_b1"]),
        "ew2": arr(i["L0_ffn_expert_w2"]),
        "eb2": chunks(i["L0_ffn_expert_b2"]),
        "ew3": arr(i["L0_ffn_expert_w3"]),
        "eb3": arr(i["L0_ffn_expert_b3"]),
        "W1": arr(i["L1_gnn_W"].transpose(2, 0, 1).reshape(D, D)),
        "b1": arr(i["L1_gnn_b"].reshape(-1)),
        "a1n": arr(a1[:, :128].reshape(-1)),
        "a1f": arr(a1[:, 128:].reshape(-1)),
        "Wr": arr(i["L1_ffn_Wr"]),
        "br": arr(i["L1_ffn_br"]),
        "affine": arr(np.stack([chunks(i["L1_ffn_ln_g"]), chunks(i["L1_ffn_ln_b"])], 2)),
        "mW1": arr(i["L1_ffn_W1"]),
        "mb1": chunks(i["L1_ffn_b1"]),
        "mW2": arr(i["L1_ffn_W2"]),
        "mb2": arr(i["L1_ffn_b2"]),
        "W2": arr(i["L2_gnn_W"]),
        "a2f": arr(i["L2_gnn_attn_l"]),
        "a2n": arr(i["L2_gnn_attn_r"]),
        "b2": arr(i["L2_gnn_bias"]),
        "wr": arr(i["L2_ffn_wr"]),
        "br5": arr(i["L2_ffn_br"]),
        "fw1": arr(i["L2_ffn_w1"][None]),
        "fb1": chunks(i["L2_ffn_b1"][None]),
        "fw2": arr(i["L2_ffn_w2"][None]),
        "fb2": arr(i["L2_ffn_b2"][None]),
        "Wij": arr(np.concatenate([i["L3_gnn_Wi"].T, i["L3_gnn_Wj"].T], 1)),
        "bij": arr(np.concatenate([i["L3_gnn_bi"], i["L3_gnn_bj"]])),
        "GT": arr(i["L3_gnn_G"].T),
        "res1": arr(i["L3_gnn_res_w1"].transpose(0, 2, 1)),
        "resb1": chunks(i["L3_gnn_res_b1"]),
        "res2": arr(i["L3_gnn_res_w2"].transpose(0, 2, 1)),
        "resb2": chunks(i["L3_gnn_res_b2"]),
        "Wv": arr(i["L3_gnn_Wv"].T),
        "bv": arr(i["L3_gnn_bv"]),
        "rsrc": arr(i["L3_ffn_edge_index"][0].reshape(128, -1)),
        "rdst": arr(i["L3_ffn_edge_index"][1].reshape(128, -1)),
        "W3": arr(i["L3_ffn_W_gat"]),
        "a3f": arr(i["L3_ffn_att_src"].reshape(-1)),
        "a3n": arr(i["L3_ffn_att_dst"].reshape(-1)),
        "gb": arr(i["L3_ffn_b_gat"]),
        "lg": arr(i["L3_ffn_ln_gamma"]),
        "lb": arr(i["L3_ffn_ln_beta"]),
        "xw1": arr(i["L3_ffn_W1"]),
        "xb1": chunks(i["L3_ffn_b1"]),
        "xw2": arr(i["L3_ffn_W2"]),
        "xb2": arr(i["L3_ffn_b2"]),
    }


def kernel(**inputs):
    import concourse.bacc as bacc
    from concourse.bass_utils import run_bass_kernel_spmd

    nc = bacc.Bacc("TRN2", target_bir_lowering=False, num_devices=1)
    arrays = {f"in_{name}": v for name, v in layout(inputs).items()}
    args = {name[3:]: nc.dram_tensor(name, v.shape, mybir.dt.from_np(v.dtype), kind="ExternalInput").ap()
            for name, v in arrays.items()}
    out = nc.dram_tensor("out", (N, D), F32, kind="ExternalOutput").ap()
    program(nc, args, out)
    return run_bass_kernel_spmd(nc, [arrays], core_ids=[0]).results[0]["out"]
```

```python
from contextlib import ExitStack, contextmanager

import concourse.bass as bass
from concourse import mybir

P = 128
N = 3125
D = 256
NT = -(-N // P)
NP = NT * P
REST = N - (NT - 1) * P
G = 2
SLOTS = G * P
U = 8
TG = 5
TOK = TG * P
HALF = TOK // 2
NTG = NT // TG
SB = 8
SG = 2 * P
LN_EPS = 1e-5
LN2 = 0.6931471805599453
BIG = 1e30

F32 = mybir.dt.float32
I32 = mybir.dt.int32
ALU = mybir.AluOpType
ACT = mybir.ActivationFunctionType
AX = mybir.AxisListType
RED = bass.bass_isa.ReduceOp
ds = bass.ds


class Stage:

    def __init__(self, nc, ctx, tag):
        self.nc, self.ctx, self.tag, self.sems, self.from_zero = nc, ctx, tag, [], []

    def sb(self, name, shape, dt=F32):
        return self.ctx.enter_context(self.nc.sbuf_tensor(f"{self.tag}_{name}", shape, dt))

    def ps(self, name, shape, dt=F32):
        return self.ctx.enter_context(self.nc.psum_tensor(f"{self.tag}_{name}", shape, dt))

    def sem(self, name):
        self.sems.append(self.nc.alloc_semaphore(f"{self.tag}_{name}"))
        return self.sems[-1]

    def gather_sem(self, name):
        self.from_zero.append(self.sem(name))
        return self.from_zero[-1]

    def block(self):
        for sem in self.sems:
            if not any(sem is z for z in self.from_zero):
                self.nc.gpsimd.sem_inc(sem, 1)
        self.nc.all_engine_barrier()
        return self.ctx.enter_context(self.nc.Block())


@contextmanager
def stage(nc, tag):
    with ExitStack() as ctx:
        st = Stage(nc, ctx, tag)
        yield st
    nc.clear_and_free_semaphores(st.sems)


def need(eng, sem, it, back):
    if isinstance(it, int):
        if it * U + back > 0:
            eng.wait_ge(sem, 1 + it * U + back)
    else:
        eng.wait_ge(sem, 1 + it * U + max(back, 0))


def ahead(part, it, j, *more):
    if not isinstance(it, int) or j >= 0:
        part(it, j, *more)


class Consts:
    pass


def groups_of(edges):
    most = (edges + NT * (SLOTS - 1)) // SLOTS
    return -(-most // U) * U + U


def setup(nc, k, x):
    with stage(nc, "set") as st:
        iota_i = st.sb("iota_i", [P, P], I32)
        zeroed, cast, made, loaded = (st.sem(s) for s in ("zeroed", "cast", "made", "loaded"))
        block = st.block()

        @block.gpsimd
        def _(pool):
            pool.memset(k.ident[:], 0.0).then_inc(zeroed, 1)
            pool.memset(k.tri[:], 0.0).then_inc(zeroed, 1)
            pool.memset(k.ones[:], 1.0).then_inc(zeroed, 1)
            pool.memset(k.X[:, NT - 1, :], 0.0).then_inc(zeroed, 1)
            pool.memset(k.past_end[:], 0.0).then_inc(zeroed, 1)
            pool.iota(iota_i[:], pattern=[[1, P]], base=0, channel_multiplier=0).then_inc(zeroed, 1)
            pool.wait_ge(zeroed, 1 + 6)
            pool.affine_select(out=k.ident[:], in_=k.ident[:], compare_op=ALU.not_equal, fill=1.0, base=0,
                               pattern=[[-1, P]], channel_multiplier=1).then_inc(made, 1)
            pool.affine_select(out=k.tri[:], in_=k.tri[:], compare_op=ALU.is_ge, fill=1.0, base=0,
                               pattern=[[-1, P]], channel_multiplier=1).then_inc(made, 1)
            pool.affine_select(out=k.past_end[:], in_=k.past_end[:], compare_op=ALU.is_ge, fill=1.0,
                               base=REST - 1, pattern=[[0, 1]], channel_multiplier=-1).then_inc(made, 1)
            pool.wait_ge(made, 1 + 3)

        @block.vector
        def _(dve):
            dve.wait_ge(zeroed, 1 + 6)
            dve.tensor_copy(k.iota[:], iota_i[:]).then_inc(cast, 1)
            dve.wait_ge(cast, 1 + 1)

        @block.sync
        def _(sp):
            full = (NT - 1) * P
            sp.dma_start(k.X[:, 0:NT - 1, :], x[0:full, :].rearrange("(t p) d -> p t d", p=P)).then_inc(loaded, 16)
            sp.wait_ge(zeroed, 1 + 6)
            sp.dma_start(k.X[0:REST, NT - 1, :], x[full:N, :]).then_inc(loaded, 16)
            sp.wait_ge(loaded, 1 + 32)


class Scatter:

    def __init__(self, st, name, row, rec, table, start, end):
        self.row, self.rec, self.table, self.start = row, rec, table, start
        self.batches = (end - start) // (2 * SB)
        self.idx = [st.sb(f"{name}_idx{s}", [row.shape[0], SB], I32) for s in range(2)]
        self.out = [st.sb(f"{name}_out{s}", [row.shape[0], SB, rec.shape[2]], I32) for s in range(2)]
        self.copied = st.sem(f"{name}_copied")
        self.scattered = [st.gather_sem(f"{name}_scattered{s}") for s in range(2)]

    def run(self, pool):
        def batch(it, s):
            c = it * (2 * SB) + (self.start + s * SB)
            if not isinstance(it, int):
                pool.wait_ge(self.scattered[s], it * (16 * SB))
                pool.nop(nofuse=True)
            pool.tensor_copy(self.idx[s][:], self.row[:, ds(c, SB)]).then_inc(self.copied, 1)
            pool.tensor_copy(self.out[s][:], self.rec[:, ds(c, SB), :]).then_inc(self.copied, 1)
            pool.wait_ge(self.copied, 1 + it * 4 + s * 2 + 2)
            pool.nop(nofuse=True)
            for j in range(SB):
                pool.indirect_dma_start(
                    out=self.table, out_offset=bass.IndirectOffsetOnAxis(ap=self.idx[s][:, j:j + 1], axis=0),
                    in_=self.out[s][:, j, :], in_offset=None).then_inc(self.scattered[s], 16)

        batch(0, 0)
        batch(0, 1)
        with pool.Fori(1, self.batches) as it:
            batch(it, 0)
            batch(it, 1)
        for s in range(2):
            pool.wait_ge(self.scattered[s], 16 * SB * self.batches)


def scatter_edges(nc, tag, jobs):
    with stage(nc, tag) as st:
        scatters = [Scatter(st, f"job{n}", *job) for n, job in enumerate(jobs)]
        block = st.block()

        @block.gpsimd
        def _(pool):
            for scatter in scatters:
                scatter.run(pool)


def place_edges(nc, k, tag, seg, oth, attr, table, row, rec, tile_of, jobs=()):
    pb, m = seg.shape
    rows, rw = table.shape
    c_all = rows // P
    n_groups = tile_of.shape[1]
    fill_cols = c_all // (U * G)
    batches = m // (2 * SB)
    with stage(nc, tag) as st:
        seg_i = st.sb("seg_i", [pb, m], I32)
        oth_i = st.sb("oth_i", [pb, m], I32)
        seg_f = st.sb("seg_f", [pb, m])
        tile_i = st.sb("tile_i", [pb, m], I32)
        tile_f = st.sb("tile_f", [pb, m])
        loc = st.sb("loc", [pb, m])
        ones_m = st.sb("ones_m", [pb, m])
        hit = st.sb("hit", [pb, 2, m])
        rank = st.sb("rank", [pb, 2, m])
        slot_f = st.sb("slot_f", [pb, m])
        slot_i = st.sb("slot_i", [pb, m], I32)
        part_i = st.sb("part_i", [pb, m], I32)
        col_i = st.sb("col_i", [pb, m], I32)
        count = st.sb("count", [pb, NT])
        tot_i = st.sb("tot_i", [P, NT], I32)
        tot_j = st.sb("tot_j", [P, NT], I32)
        n_grp = st.sb("n_grp", [P, NT])
        ones_t = st.sb("ones_t", [P, NT])
        end_g = st.sb("end_g", [P, NT])
        start = st.sb("start", [P, NT])
        g_i = st.sb("g_i", [1, n_groups], I32)
        g_f = st.sb("g_f", [1, n_groups])
        past = st.sb("past", [1, n_groups, NT])
        tile_r = st.sb("tile_r", [1, n_groups])
        fill = st.sb("fill", [P, fill_cols, rw], I32)
        psum = st.ps("psum", [P, 2, 512])

        loaded = st.sem("loaded")
        iota_made = st.sem("iota_made")
        v = st.sem("dve_order")
        counted = st.sem("counted")
        summed = st.sem("summed")
        hits = st.sem("hits")
        ranks = st.sem("ranks")
        placed = st.sem("placed")
        noted = st.sem("noted")
        fill_made = st.sem("fill_made")
        filled = st.sem("filled")
        attr_in = st.sem("attr_in")
        scatters = [Scatter(st, f"job{n}", *job) for n, job in enumerate(jobs)]
        block = st.block()

        @block.gpsimd
        def _(pool):
            pool.iota(g_i[:], pattern=[[1, n_groups]], base=0, channel_multiplier=0).then_inc(iota_made, 1)
            pool.memset(fill[:], 0).then_inc(fill_made, 1)
            pool.wait_ge(fill_made, 1 + 1)
            pool.memset(fill[:, :, 0:1], N).then_inc(fill_made, 1)
            pool.memset(fill[:, :, 1:2].bitcast(F32), -1.0).then_inc(fill_made, 1)
            for scatter in scatters:
                scatter.run(pool)

        @block.sync
        def _(sp):
            sp.dma_start(seg_i[:], seg).then_inc(loaded, 16)
            sp.dma_start(oth_i[:], oth).then_inc(loaded, 16)
            sp.wait_ge(fill_made, 1 + 3)
            by_part = table.rearrange("(p c) w -> p c w", p=P)
            for q in range(U * G):
                sp.dma_start(by_part[:, q * fill_cols:(q + 1) * fill_cols, :], fill[:]).then_inc(filled, 16)
            if attr is not None:
                for q in range(4):
                    w = m // 4
                    sp.dma_start(rec[:, q * w:(q + 1) * w, 2:rw], attr[:, q * w:(q + 1) * w, :]).then_inc(attr_in, 16)
                sp.wait_ge(attr_in, 1 + 64)
            sp.wait_ge(filled, 1 + 16 * U * G)

        @block.vector
        def _(dve):
            at = [0]

            def then(ins):
                at[0] += 1
                ins.then_inc(v, 1)
                dve.wait_ge(v, 1 + at[0])

            dve.wait_ge(loaded, 1 + 32)
            dve.tensor_copy(seg_f[:], seg_i[:]).then_inc(v, 1)
            dve.memset(ones_m[:], 1.0).then_inc(v, 1)
            dve.memset(ones_t[:], 1.0).then_inc(v, 1)
            dve.memset(slot_f[:], 0.0).then_inc(v, 1)
            at[0] = 4
            then(dve.tensor_scalar(tile_i[:], seg_i[:], 7, None, ALU.arith_shift_right))
            then(dve.tensor_copy(tile_f[:], tile_i[:]))
            then(dve.scalar_tensor_tensor(out=loc[:], in0=tile_f[:], scalar=-float(P), in1=seg_f[:],
                                          op0=ALU.mult, op1=ALU.add))
            with dve.Fori(0, NT) as b:
                dve.wait_ge(counted, 1 + b)
                dve.tensor_scalar(hit[:, 0, :], tile_f[:], k.iota[0:pb, ds(b, 1)], 0.0, ALU.is_equal, ALU.add,
                                  accum_out=count[:, ds(b, 1)]).then_inc(counted, 1)
            dve.wait_ge(summed, 1 + 2)
            then(dve.tensor_scalar(tot_i[:], psum[:, 1, 0:NT], float(SLOTS - 1), None, ALU.add))
            then(dve.tensor_scalar(tot_j[:], tot_i[:], SLOTS.bit_length() - 1, None, ALU.arith_shift_right))
            then(dve.tensor_copy(n_grp[:], tot_j[:]))
            then(dve.tensor_tensor_scan(end_g[:], ones_t[:], n_grp[:], 0.0, ALU.mult, ALU.add))
            then(dve.tensor_tensor(start[:], end_g[:], n_grp[:], ALU.subtract))
            then(dve.tensor_scalar(start[:], start[:], float(SLOTS), -1.0, ALU.mult, ALU.add))
            then(dve.tensor_tensor(start[0:pb, :], psum[0:pb, 0, 0:NT], start[0:pb, :], ALU.add))
            dve.wait_ge(iota_made, 1 + 1)
            then(dve.tensor_copy(g_f[:], g_i[:]))
            then(dve.tensor_tensor(past[:], g_f[:].unsqueeze(2).broadcast_to([1, n_groups, NT]),
                                   end_g[0:1, :].unsqueeze(1).broadcast_to([1, n_groups, NT]), ALU.is_ge))
            then(dve.tensor_reduce(tile_r[:], past[:], AX.X, ALU.add))
            then(dve.tensor_scalar(tile_of, tile_r[:], float(NT - 1), None, ALU.min))

            def place(b, h, first):
                if not first:
                    dve.wait_ge(placed, 1 + b - 1)
                dve.tensor_scalar(hit[:, h, :], tile_f[:], k.iota[0:pb, ds(b, 1)], None, ALU.is_equal)\
                   .then_inc(hits, 1)
                dve.wait_ge(hits, 1 + b + 1)
                dve.tensor_tensor_scan(rank[:, h, :], ones_m[:], hit[:, h, :], start[0:pb, ds(b, 1)],
                                       ALU.mult, ALU.add).then_inc(ranks, 1)
                dve.wait_ge(ranks, 1 + b + 1)
                dve.wait_ge(placed, 1 + b)
                dve.nop(nofuse=True)
                dve.copy_predicated(slot_f[:], hit[:, h, :].bitcast(I32), rank[:, h, :]).then_inc(placed, 1)

            place(0, 0, True)
            with dve.Fori(0, (NT - 1) // 2) as i:
                place(i * 2 + 1, 1, False)
                place(i * 2 + 2, 0, False)
            dve.wait_ge(placed, 1 + NT)
            then(dve.tensor_copy(slot_i[:], slot_f[:]))
            then(dve.tensor_scalar(part_i[:], slot_i[:], P - 1, None, ALU.bitwise_and))
            then(dve.tensor_scalar(col_i[:], slot_i[:], 7, None, ALU.arith_shift_right))
            then(dve.scalar_tensor_tensor(out=row, in0=part_i[:], scalar=float(c_all), in1=col_i[:],
                                          op0=ALU.mult, op1=ALU.add))
            dve.tensor_scalar(rec[:, :, 0:1], oth_i[:].unsqueeze(2), 0, None, ALU.add).then_inc(noted, 1)
            dve.tensor_scalar(rec[:, :, 1:2].bitcast(F32), loc[:].unsqueeze(2), 0.0, None, ALU.add).then_inc(noted, 1)
            dve.wait_ge(noted, 1 + 2)

        @block.tensor
        def _(pe):
            pe.wait_ge(counted, 1 + NT)
            pe.matmul(psum[0:pb, 0, 0:NT], k.tri[0:pb, 0:pb], count[:], start=True, stop=True).then_inc(summed, 1)
            pe.matmul(psum[:, 1, 0:NT], k.ones[0:pb, :], count[:], start=True, stop=True).then_inc(summed, 1)


def read_slots(nc, tag, table, other, local):
    c_all = table.shape[0] // P
    parts = 4
    w = c_all // parts
    with stage(nc, tag) as st:
        meta = st.sb("meta", [P, c_all, 2], I32)
        meta_in = [st.sem(f"meta_in{q}") for q in range(parts)]
        noted = st.sem("noted")
        block = st.block()

        @block.sync
        def _(sp):
            by_part = table.rearrange("(p c) w -> p c w", p=P)
            for q in range(parts):
                sp.dma_start(meta[:, q * w:(q + 1) * w, :], by_part[:, q * w:(q + 1) * w, 0:2]).then_inc(meta_in[q], 16)

        @block.vector
        def _(dve):
            for q in range(parts):
                dve.wait_ge(meta_in[q], 1 + 16)
                cols = slice(q * w, (q + 1) * w)
                dve.tensor_copy(other[:, cols], meta[:, cols, 0]).then_inc(noted, 1)
                dve.tensor_copy(local[:, cols], meta[:, cols, 1].bitcast(F32)).then_inc(noted, 1)
            dve.wait_ge(noted, 1 + 2 * parts)


class Norm:

    def __init__(self, st, name):
        self.stats = st.sb(f"{name}_stats", [P, TG, 6])
        self.mv = st.sb(f"{name}_mv", [P, TG, 2])
        self.ve = st.sb(f"{name}_ve", [P, TG])
        self.sd = st.sb(f"{name}_sd", [P, TG])
        self.rs = st.sb(f"{name}_rs", [P, TG])
        self.has_stats, self.has_mv, self.has_var, self.has_sd, self.has_rs, self.applied = (
            st.sem(f"{name}_{s}") for s in ("stats", "mv", "var", "sd", "rs", "applied"))

    def dve_first(self, dve, it, src):
        dve.wait_ge(self.applied, 1 + it * TG)
        for u in range(TG):
            dve.bn_stats(self.stats[:, u, :], src(u)).then_inc(self.has_stats, 1)
        for u in range(TG):
            dve.wait_ge(self.has_stats, 1 + it * TG + u + 1)
            dve.nop(nofuse=True)
            dve.bn_aggr(self.mv[:, u, :], self.stats[:, u, :]).then_inc(self.has_mv, 1)
        dve.wait_ge(self.has_mv, 1 + it * TG + TG)
        dve.tensor_scalar(self.ve[:], self.mv[:, :, 1], LN_EPS, None, ALU.add).then_inc(self.has_var, 1)

    def act_root(self, act, it):
        act.wait_ge(self.has_var, 1 + it + 1)
        act.activation(self.sd[:], self.ve[:], ACT.Sqrt).then_inc(self.has_sd, 1)

    def dve_apply(self, dve, it, src, dst):
        dve.wait_ge(self.has_sd, 1 + it + 1)
        dve.reciprocal(self.rs[:], self.sd[:]).then_inc(self.has_rs, 1)
        dve.wait_ge(self.has_rs, 1 + it + 1)
        for u in range(TG):
            dve.tensor_scalar(dst(u), src(u), self.mv[:, u, 0:1], self.rs[:, u:u + 1], ALU.subtract, ALU.mult)\
               .then_inc(self.applied, 1)



def tile_ids(nc, engine, tile_of, g):
    ap = tile_of[0:1, ds(g, U)]
    return nc.values_load_multi_w_load_instructions(ap, engines=(engine,), min_val=0, max_val=NT - 1,
                                                     skip_runtime_bounds_check_because="order_edges makes only tiles 0 .. NT - 1")[1]


def make_table(nc, k, tag, w, a_far, a_near, table, near, acc=None, bias=None, guard=False, softmax=None, plain=None, jobs=()):
    na = near.shape[2]
    tw = table.shape[1]
    f1 = tw // na
    hd = f1 - 1
    cw = tw + na
    kc = D // P
    slabs = kc + (bias is not None)
    with stage(nc, tag) as st:
        W = st.sb("W", [P, kc + 1, cw])
        a_b = st.sb("a_b", [P, 2, na * hd])
        prod = st.sb("prod", [P, 2, kc + 1, na * hd])
        XN = st.sb("XN", [P, TG, D])
        XT = st.sb("XT", [P, TG, kc, P])
        ROW = st.sb("ROW", [P, TG, tw])
        odd = st.sb("odd", [P, TG, tw])
        far = st.sb("far", [P, NT, na])
        zeros = st.sb("zeros", [P, tw])
        least = st.sb("least", [P, na])
        most = st.sb("most", [P, na])
        less = st.sb("less", [P, na])
        norm = Norm(st, "n")
        psT = st.ps("psT", [P, 2, 512])
        psH = st.ps("psH", [P, 2, 512])
        w_in, multiplied, folded = (st.sem(s) for s in ("w_in", "multiplied", "folded"))
        turned, turned_out, made, row_out, row_found, row_kept = (
            st.sem(s) for s in ("turned", "turned_out", "made", "row_out", "row_found", "row_kept"))
        stored = [st.sem(f"stored{u}") for u in range(TG)]
        order, reduced, finished = st.sem("order"), st.sem("reduced"), st.sem("finished")
        pad_stored = st.sem("pad_stored")
        scatters = [Scatter(st, f"job{n}", *job) for n, job in enumerate(jobs)]
        block = st.block()

        @block.sync
        def _(sp):
            for s in range(kc):
                sp.dma_start(W[:, s, 0:tw].rearrange("p (h f) -> p h f", f=f1)[:, :, 0:hd],
                             w[s * P:(s + 1) * P, :].rearrange("p (h f) -> p h f", f=hd)).then_inc(w_in, 16)
            sp.dma_start(a_b[:, 0, :], a_far.partition_broadcast(P)).then_inc(w_in, 16)
            sp.dma_start(a_b[:, 1, :], a_near.partition_broadcast(P)).then_inc(w_in, 16)
            if bias is not None:
                sp.dma_start(W[:, kc, 0:tw].rearrange("p (h f) -> p h f", f=f1)[:, :, 0:hd],
                             bias.rearrange("(h f) -> h f", f=hd).partition_broadcast(P)).then_inc(w_in, 16)
            with sp.Fori(0, NTG) as it:
                for u in range(TG):
                    sp.wait_ge(row_kept if guard or softmax is not None else row_out, 1 + it * TG + u + 1)
                    sp.dma_start(table[ds(it * TOK + u * P, P), :], ROW[:, u, :]).then_inc(stored[u], 16)
            for u in range(TG):
                sp.wait_ge(stored[u], 1 + 16 * NTG)
            if softmax is not None:
                sp.wait_ge(order, 1 + 8)
                sp.dma_start(table[N:N + 1, hd:tw:f1], less[0:1, :], allow_slow_non_contiguous=True).then_inc(pad_stored, 16)
                sp.wait_ge(pad_stored, 1 + 16)

        @block.vector
        def _(dve):
            dve.memset(zeros[:], 0.0).then_inc(order, 1)
            dve.memset(far[:], 0.0).then_inc(order, 1)
            dve.wait_ge(w_in, 1 + 16 * (kc + 2 + (bias is not None)))
            for j in range(2):
                for s in range(slabs):
                    dve.tensor_tensor(prod[:, j, s, :].rearrange("p (h f) -> p h f", f=hd),
                                      W[:, s, 0:tw].rearrange("p (h f) -> p h f", f=f1)[:, :, 0:hd],
                                      a_b[:, j, :].rearrange("p (h f) -> p h f", f=hd), ALU.mult)\
                       .then_inc(multiplied, 1)
            dve.wait_ge(multiplied, 1 + 2 * slabs)
            for s in range(slabs):
                dve.tensor_reduce(W[:, s, hd:tw:f1], prod[:, 0, s, :].rearrange("p (h f) -> p h f", f=hd),
                                  AX.X, ALU.add).then_inc(folded, 1)
                dve.tensor_reduce(W[:, s, tw:cw], prod[:, 1, s, :].rearrange("p (h f) -> p h f", f=hd),
                                  AX.X, ALU.add).then_inc(folded, 1)
            dve.wait_ge(order, 1 + 2)
            def normed(it):
                def x_tile(u):
                    return k.X[:, ds(it * TG + u, 1), :].squeeze(1)
                if plain is None:
                    norm.dve_first(dve, it, x_tile)
                dve.wait_ge(turned, 1 + it * TG)
                if plain is None:
                    norm.dve_apply(dve, it, x_tile, lambda u: XN[:, u, :])
                else:
                    for u in range(TG):
                        dve.tensor_scalar(XN[:, u, :], plain[:, ds(it * TG + u, 1), :].squeeze(1), 0.0, None, ALU.add)\
                           .then_inc(norm.applied, 1)

            def rows(it):
                for u in range(TG if guard or softmax is not None else 0):
                    t = it * TG + u
                    dve.wait_ge(row_out, 1 + t + 1)
                    if guard:
                        dve.tensor_tensor(odd[:, u, :], ROW[:, u, :], ROW[:, u, :], ALU.not_equal)\
                           .then_inc(row_found, 1)
                        dve.wait_ge(row_found, 1 + t + 1)
                        dve.nop(nofuse=True)
                        dve.copy_predicated(ROW[:, u, :], odd[:, u, :].bitcast(I32), zeros[:]).then_inc(row_kept, 1)
                    elif softmax is not None:
                        dve.tensor_scalar(far[:, ds(t, 1), :].squeeze(1), ROW[:, u, hd:tw:f1], 0.0, None, ALU.add).then_inc(row_found, 1)
                        dve.tensor_scalar(acc[:, ds(t, 1), :].squeeze(1), ROW[:, u, :], 0.0, None, ALU.add).then_inc(row_kept, 1)

            normed(0)
            with dve.Fori(0, NTG - 1) as it:
                normed(it + 1)
                rows(it)
            rows(NTG - 1)
            if softmax is not None:
                shift, base = softmax
                at = [2]

                def then(ins):
                    at[0] += 1
                    ins.then_inc(order, 1)
                    dve.wait_ge(order, 1 + at[0])

                dve.wait_ge(row_found, 1 + NT)
                dve.wait_ge(row_kept, 1 + NT)
                then(dve.tensor_reduce(least[:], far[:].rearrange("p t a -> p a t"), AX.X, ALU.min))
                then(dve.tensor_scalar(least[:], least[:], -1.0, None, ALU.mult))
                dve.wait_ge(reduced, 1 + 1)
                then(dve.tensor_scalar(shift, most[:], 1.0, None, ALU.add))
                sh = shift.unsqueeze(1).broadcast_to([P, NT, na])
                then(dve.tensor_tensor(far[:], far[:], sh, ALU.add))
                then(dve.tensor_tensor(near, near, sh, ALU.subtract))
                then(dve.tensor_scalar(less[:], shift, -1.0, None, ALU.mult))
                then(dve.tensor_tensor(far[:], far[:], near, ALU.add))
                then(dve.scalar_tensor_tensor(out=base, in0=far[:], scalar=0.2, in1=far[:],
                                              op0=ALU.mult, op1=ALU.max))
                then(dve.tensor_scalar(base, base, -1.0, None, ALU.mult))
                then(dve.memset(acc[:, :, hd:tw:f1], 1.0))

        @block.gpsimd
        def _(pool):
            if softmax is not None:
                pool.wait_ge(order, 1 + 4)
                pool.partition_all_reduce(most[:], least[:], P, RED.max).then_inc(reduced, 1)
            for scatter in scatters:
                scatter.run(pool)

        @block.tensor
        def _(pe):
            pe.wait_ge(folded, 1 + 2 * slabs)
            with pe.Fori(0, NTG) as it:
                for u in range(TG):
                    t = it * TG + u
                    pe.wait_ge(norm.applied, 1 + t + 1)
                    pe.wait_ge(turned_out, 1 + (it * TG if u < 2 else t - 1))
                    for s in range(kc):
                        ins = pe.transpose(psT[:, u % 2, s * P:(s + 1) * P], XN[:, u, s * P:(s + 1) * P], k.ident[:])
                    ins.then_inc(turned, 1)
                for u in range(TG):
                    t = it * TG + u
                    pe.wait_ge(turned_out, 1 + t + 1)
                    pe.wait_ge(row_out, 1 + (it * TG if u < 2 else t - 1))
                    for s in range(kc):
                        ins = pe.matmul(psH[:, u % 2, 0:cw], XT[:, u, s, :], W[:, s, :],
                                        start=(s == 0), stop=(s == slabs - 1))
                    if bias is not None:
                        ins = pe.matmul(psH[:, u % 2, 0:cw], k.ones[0:1, :], W[0:1, kc, :],
                                        start=False, stop=True)
                    ins.then_inc(made, 1)

        @block.scalar
        def _(act):
            def rows(it, last):
                for u in range(TG):
                    t = it * TG + u
                    act.wait_ge(turned, 1 + t + 1)
                    act.wait_ge(made, 1 + it * TG)
                    act.activation(XT[:, u, :, :], psT[:, u % 2, 0:D].rearrange("p (k q) -> p k q", q=P), ACT.Copy)\
                       .then_inc(turned_out, 1)
                if plain is None and not last:
                    norm.act_root(act, it + 1)
                for u in range(TG):
                    t = it * TG + u
                    act.wait_ge(made, 1 + t + 1)
                    act.wait_ge(stored[u], 1 + it * 16)
                    act.activation(near[:, ds(t, 1), :].squeeze(1), psH[:, u % 2, tw:cw], ACT.Copy)\
                       .then_inc(finished, 1)
                    act.activation(ROW[:, u, :], psH[:, u % 2, 0:tw], ACT.Copy).then_inc(row_out, 1)

            if plain is None:
                norm.act_root(act, 0)
            with act.Fori(0, NTG - 1) as it:
                rows(it, False)
            rows(NTG - 1, True)
            act.wait_ge(finished, 1 + NT)


def edge_pass(nc, k, tag, table, other, local, tile_of, near, acc, softmax=None, guard=False):
    na = near.shape[2]
    tw = table.shape[1]
    f1 = tw // na
    hd = f1 - 1
    n_loop = tile_of.shape[1] // U - 1
    nr = na if softmax is None else 2 * na
    with stage(nc, tag) as st:
        IDX = st.sb("IDX", [P, U, G], I32)
        ROWS = st.sb("ROWS", [P, U, G, tw])
        S = st.sb("S", [P, U, G, P])
        ST = st.sb("ST", [P, U, G, P])
        z = st.sb("z", [P, U, G, na])
        z2 = st.sb("z2", [P, U, G, na])
        psS = st.ps("psS", [P, 2, 512])
        psZ = st.ps("psZ", [P, 2, 512])
        psO = st.ps("psO", [P, 2, 512])
        q = {s: st.sem(s) for s in ("idx_made", "sel", "sel_t", "sel_out", "rated", "added", "leaky", "weighed",
                                    "guarded", "scaled", "summed", "kept")}
        gathered = [[st.gather_sem(f"gathered{u}_{i}") for i in range(G)] for u in range(U)]
        cleared = st.sem("cleared")
        if softmax is not None:
            shift, base = softmax
            FAR = st.sb("FAR", [P, U, G, na])
            VAL = st.sb("VAL", [P, U, G, na, P])
            best = st.sb("best", [P, U, na])
            sumt = st.sb("sumt", [P, U, na])
            leak = st.sb("leak", [P, U, na])
            joined = na > 1
            lead = 6 if joined else 5
            NB = st.sb("NB", [P, U, 2, na])
            drop = st.sb("drop", [P, U, na])
            keep = st.sb("keep", [P, U, na])
            z3 = st.sb("z3", [P, U, G, na])
            turned = [(G - 1, h) for h in range(na)] if joined else [(i, 0) for i in range(G)]
            psV = st.ps("psV", [P, 2, 512])
            q |= {s: st.sem(s) for s in ("far_made", "val", "joined", "val_t", "best_made", "sum_made", "leak_made",
                                         "near_made", "base_made", "drop_made", "base_kept", "keep_made", "based",
                                         "acc_scaled")}
        block = st.block()

        def zeta(v):
            return psZ[:, v % 2, 0:G * nr].rearrange("p (i a) -> p i a", a=nr)

        @block.gpsimd
        def _(pool):
            def gather(it, j):
                g, v = it * U + j, j % U
                pool.wait_ge(q["idx_made"], 1 + g + 1)
                need(pool, q["summed"], it, j - (U - 1))
                pool.nop(nofuse=True)
                for i in range(G):
                    pool.indirect_dma_start(out=ROWS[:, v, i, :], out_offset=None, in_=table,
                                            in_offset=bass.IndirectOffsetOnAxis(ap=IDX[:, v, i:i + 1], axis=0))\
                        .then_inc(gathered[v][i], 16)

            for j in range(U):
                gather(0, j)
            with pool.Fori(0, n_loop) as it:
                for j in range(U):
                    gather(it, j + U)

        @block.scalar
        def _(act):
            def index(it, j):
                g, v, n = it * U + j, j % U, it + j // U
                for i in range(G):
                    if not isinstance(n, int) or n > 0:
                        act.wait_ge(gathered[v][i], n * 16)
                act.activation(IDX[:, v, :], other[:, ds(g * G, G)], ACT.Copy).then_inc(q["idx_made"], 1)

            def turn(it, j):
                g, v = it * U + j, j % U
                act.wait_ge(q["sel_t"], 1 + g + 1)
                need(act, q["rated"], it, j - (U - 1))
                act.activation(ST[:, v, :, :], psS[:, v % 2, 0:G * P].rearrange("p (i n) -> p i n", n=P), ACT.Copy)\
                   .then_inc(q["sel_out"], 1)

            def rescale(it, j):
                g, v = it * U + j, j % U
                act.wait_ge(q["drop_made"], 1 + g + 1)
                need(act, q["kept"], it, j - (U - 1))
                act.activation(keep[:, v, :], drop[:, v, :], ACT.Exp).then_inc(q["keep_made"], 1)

            def weigh(it, j):
                g, v = it * U + j, j % U
                w = ROWS[:, v, :, hd:tw:f1]
                if softmax is None:
                    act.wait_ge(q["leaky"], 1 + g + 1)
                    act.activation(w, z2[:, v, :, :], ACT.Exp, scale=-1.0).then_inc(q["weighed"], 1)
                else:
                    act.wait_ge(q["based"], 1 + g + 1)
                    act.activation(w, z3[:, v, :, :], ACT.Exp).then_inc(q["weighed"], 1)

            def scale_rows(it, j):
                g, v = it * U + j, j % U
                act.wait_ge(q["weighed"], 1 + g + 1)
                for i in range(G):
                    ins = act.activation(ROWS[:, v, i, 0:hd], ROWS[:, v, i, 0:hd], ACT.Copy, scale=ROWS[:, v, i, hd:tw])
                ins.then_inc(q["scaled"], 1)

            def values(it, j):
                g, v = it * U + j, j % U
                act.wait_ge(q["far_made"], 1 + g + 1)
                act.wait_ge(q["sel"], 1 + g + 1)
                need(act, q["val_t"], it, j - (U - 1))
                for i in range(G - 1 if joined else G):
                    for h in range(na):
                        ins = act.activation(VAL[:, v, i, h, :], S[:, v, i, :], ACT.Copy, scale=FAR[:, v, i, h:h + 1])
                ins.then_inc(q["val"], 1)

            def body(it, j):
                if softmax is not None and na == 1:
                    ahead(scale_rows, it, j + 1)
                ahead(turn, it, j + 5)
                if softmax is not None:
                    ahead(values, it, j + lead)
                ahead(weigh, it, j + 2)
                if softmax is not None:
                    ahead(rescale, it, j + 3)
                ahead(index, it, j + U)

            for j in range(-U, 0):
                body(0, j)
            with act.Fori(0, n_loop) as it:
                for j in range(U):
                    body(it, j)

        @block.tensor
        def _(pe):
            def add_up(it, j):
                g, v = it * U + j, j % U
                pe.wait_ge(q["scaled"], 1 + g + 1)
                need(pe, q["kept"], it, j - 1)
                for i in range(G):
                    ins = pe.matmul(psO[:, v % 2, 0:tw], S[:, v, i, :], ROWS[:, v, i, :],
                                    start=(i == 0), stop=(i == G - 1))
                ins.then_inc(q["summed"], 1)

            def rate(it, j, tile):
                g, v = it * U + j, j % U
                pe.wait_ge(q["sel_out"], 1 + g + 1)
                need(pe, q["added" if softmax is None else "based"], it, j - 1)
                if softmax is not None:
                    pe.wait_ge(q["base_made"], 1 + g + 1)
                    pe.wait_ge(q["near_made"], 1 + g + 1)
                rhs = near[:, ds(tile, 1), :].squeeze(1) if softmax is None else NB[:, v, :, :].rearrange("p b a -> p (b a)")
                for i in range(G):
                    ins = pe.matmul(zeta(v)[:, i, :], ST[:, v, i, :], rhs, start=True, stop=True)
                ins.then_inc(q["rated"], 1)

            def turn_values(it, j):
                g, v = it * U + j, j % U
                pe.wait_ge(q["joined" if joined else "val"], 1 + g + 1)
                need(pe, q["best_made"], it, j - 1)
                for n, (i, h) in enumerate(turned):
                    ins = pe.transpose(psV[:, v % 2, n * P:(n + 1) * P], VAL[:, v, i, h, :], k.ident[:])
                ins.then_inc(q["val_t"], 1)

            def turn(it, j):
                g, v = it * U + j, j % U
                pe.wait_ge(q["sel"], 1 + g + 1)
                need(pe, q["sel_out"], it, j - 1)
                for i in range(G):
                    ins = pe.transpose(psS[:, v % 2, i * P:(i + 1) * P], S[:, v, i, :], k.ident[:])
                ins.then_inc(q["sel_t"], 1)

            def body(it, j, tile):
                ahead(turn, it, j + 5)
                ahead(rate, it, j + 3, tile)
                ahead(add_up, it, j + 1)
                if softmax is not None:
                    ahead(turn_values, it, j + 5)

            tiles = [None] * U
            if softmax is None:
                tiles = tile_ids(nc, mybir.EngineType.PE, tile_of, 0)
            for j in range(-U, 0):
                body(0, j, tiles[max(j + 3, 0)])
            with pe.Fori(0, n_loop) as it:
                if softmax is None:
                    tiles = tile_ids(nc, mybir.EngineType.PE, tile_of, it * U + 3)
                for j in range(U):
                    body(it, j, tiles[j])

        @block.vector
        def _(dve):
            def keep_sum(it, j, tile):
                g, v = it * U + j, j % U
                dve.wait_ge(q["summed"], 1 + g + 1)
                need(dve, q["kept"], it, j)
                a = acc[:, ds(tile, 1), :].squeeze(1)
                o = psO[:, v % 2, 0:tw]
                if softmax is None:
                    dve.tensor_tensor(a, o, a, ALU.add).then_inc(q["kept"], 1)
                elif na == 1:
                    dve.wait_ge(q["keep_made"], 1 + g + 1)
                    dve.scalar_tensor_tensor(out=a, in0=a, scalar=keep[:, v, :], in1=o,
                                             op0=ALU.mult, op1=ALU.add).then_inc(q["kept"], 1)
                else:
                    dve.wait_ge(q["keep_made"], 1 + g + 1)
                    ah = a.rearrange("p (h f) -> p h f", f=f1)
                    dve.tensor_tensor(ah, ah, keep[:, v, :].unsqueeze(2).broadcast_to([P, na, f1]), ALU.mult)\
                       .then_inc(q["acc_scaled"], 1)
                    dve.wait_ge(q["acc_scaled"], 1 + g + 1)
                    dve.tensor_tensor(a, o, a, ALU.add).then_inc(q["kept"], 1)

            def scale_rows(it, j):
                g, v = it * U + j, j % U
                dve.wait_ge(q["weighed"], 1 + g + 1)
                w = ROWS[:, v, :, hd:tw:f1]
                if guard:
                    dve.tensor_scalar(w, w, 0.0, None, ALU.max).then_inc(q["guarded"], 1)
                    dve.wait_ge(q["guarded"], 1 + g + 1)
                r = ROWS[:, v, :, :].rearrange("p i (h f) -> p (i h) f", f=f1)
                dve.tensor_tensor(r[:, :, 0:hd], r[:, :, 0:hd], r[:, :, hd:f1].broadcast_to([P, G * na, hd]),
                                  ALU.mult).then_inc(q["scaled"], 1)

            def add_near(it, j):
                g, v, n = it * U + j, j % U, it + j // U + 1
                dve.wait_ge(q["rated"], 1 + g + 1)
                if softmax is None:
                    for i in range(G):
                        dve.wait_ge(gathered[v][i], n * 16)
                    f = ROWS[:, v, :, hd:tw:f1]
                else:
                    f = FAR[:, v, :, :]
                dve.tensor_tensor(z[:, v, :, :], zeta(v)[:, :, 0:na], f, ALU.add).then_inc(q["added"], 1)

            def leaky(it, j):
                g, v = it * U + j, j % U
                dve.wait_ge(q["added"], 1 + g + 1)
                dve.scalar_tensor_tensor(out=z2[:, v, :, :], in0=z[:, v, :, :], scalar=0.2, in1=z[:, v, :, :],
                                         op0=ALU.mult, op1=ALU.max).then_inc(q["leaky"], 1)

            def minus_base(it, j):
                g, v = it * U + j, j % U
                dve.wait_ge(q["leaky"], 1 + g + 1)
                dve.tensor_tensor(z3[:, v, :, :], z2[:, v, :, :], zeta(v)[:, :, na:nr], ALU.add)\
                   .then_inc(q["based"], 1)

            def col(t, tile):
                return t[:, ds(tile, 1), :].squeeze(1)

            def find_best(it, j):
                g, v = it * U + j, j % U
                dve.wait_ge(q["val_t"], 1 + g + 1)
                flat = psV[:, v % 2, 0:len(turned) * P]
                dve.tensor_reduce(best[:, v, :], flat.rearrange("p (a e) -> p a e", a=na), AX.X, ALU.max)\
                   .then_inc(q["best_made"], 1)

            def best_sum(it, j, tile):
                g, v = it * U + j, j % U
                dve.wait_ge(q["best_made"], 1 + g + 1)
                dve.tensor_tensor(sumt[:, v, :], best[:, v, :], col(near, tile), ALU.add).then_inc(q["sum_made"], 1)

            def best_leaky(it, j):
                g, v = it * U + j, j % U
                dve.wait_ge(q["sum_made"], 1 + g + 1)
                dve.scalar_tensor_tensor(out=leak[:, v, :], in0=sumt[:, v, :], scalar=0.2, in1=sumt[:, v, :],
                                         op0=ALU.mult, op1=ALU.max).then_inc(q["leak_made"], 1)

            def copy_near(it, j, tile):
                v = j % U
                need(dve, q["rated"], it, j - (U - 1))
                dve.tensor_scalar(NB[:, v, 0, :], col(near, tile), 0.0, None, ALU.add).then_inc(q["near_made"], 1)

            def new_base(it, j, tile):
                g, v = it * U + j, j % U
                dve.wait_ge(q["leak_made"], 1 + g + 1)
                need(dve, q["base_kept"], it, j)
                dve.scalar_tensor_tensor(out=NB[:, v, 1, :], in0=leak[:, v, :], scalar=-1.0, in1=col(base, tile),
                                         op0=ALU.mult, op1=ALU.min).then_inc(q["base_made"], 1)

            def base_drop(it, j, tile):
                g, v = it * U + j, j % U
                dve.wait_ge(q["base_made"], 1 + g + 1)
                dve.tensor_tensor(drop[:, v, :], NB[:, v, 1, :], col(base, tile), ALU.subtract)\
                   .then_inc(q["drop_made"], 1)

            def keep_base(it, j, tile):
                g, v = it * U + j, j % U
                dve.wait_ge(q["drop_made"], 1 + g + 1)
                dve.tensor_scalar(col(base, tile), NB[:, v, 1, :], 0.0, None, ALU.add).then_inc(q["base_kept"], 1)

            def shift_far(it, j):
                v, n = j % U, it + j // U + 1
                for i in range(G):
                    dve.wait_ge(gathered[v][i], n * 16)
                dve.tensor_tensor(FAR[:, v, :, :], ROWS[:, v, :, hd:tw:f1],
                                  shift.unsqueeze(1).broadcast_to([P, G, na]), ALU.add).then_inc(q["far_made"], 1)

            def join(it, j):
                g, v = it * U + j, j % U
                dve.wait_ge(q["val"], 1 + g + 1)
                for h in range(na):
                    ins = dve.scalar_tensor_tensor(out=VAL[:, v, 1, h, :], in0=S[:, v, 1, :],
                                                   scalar=FAR[:, v, 1, h:h + 1], in1=VAL[:, v, 0, h, :],
                                                   op0=ALU.mult, op1=ALU.max)
                ins.then_inc(q["joined"], 1)

            def select(it, j):
                g, v = it * U + j, j % U
                need(dve, q["summed"], it, j - (U - 1))
                dve.tensor_tensor(S[:, v, :, :], k.iota[:].unsqueeze(1).broadcast_to([P, G, P]),
                                  local[:, ds(g * G, G)].unsqueeze(2).broadcast_to([P, G, P]), ALU.is_equal)\
                   .then_inc(q["sel"], 1)

            def body(it, j, tile, tile4):
                if softmax is None:
                    ahead(add_near, it, j + 2)
                    ahead(select, it, j + 5)
                    ahead(leaky, it, j + 2)
                    ahead(scale_rows, it, j + 1)
                    ahead(keep_sum, it, j, tile)
                    return
                if na > 1:
                    ahead(scale_rows, it, j + 1)
                ahead(add_near, it, j + 2)
                ahead(shift_far, it, j + lead)
                ahead(leaky, it, j + 2)
                if joined:
                    ahead(join, it, j + 5)
                ahead(minus_base, it, j + 2)
                ahead(find_best, it, j + 4)
                ahead(copy_near, it, j + 4, tile4)
                ahead(best_sum, it, j + 4, tile4)
                ahead(select, it, j + lead + 1)
                ahead(best_leaky, it, j + 4)
                ahead(keep_sum, it, j, tile)
                ahead(new_base, it, j + 4, tile4)
                ahead(base_drop, it, j + 4, tile4)
                ahead(keep_base, it, j + 4, tile4)

            if softmax is not None:
                tiles4 = tile_ids(nc, mybir.EngineType.DVE, tile_of, 0)
            else:
                tiles4 = [None] * U
            if softmax is None:
                dve.memset(acc, 0.0).then_inc(cleared, 1)
            for j in range(-U, 0):
                body(0, j, None, tiles4[max(j + 4, 0)])
            if softmax is None:
                dve.wait_ge(cleared, 1 + 1)
            with dve.Fori(0, n_loop) as it:
                tiles = tile_ids(nc, mybir.EngineType.DVE, tile_of, it * U)
                if softmax is not None:
                    tiles4 = tile_ids(nc, mybir.EngineType.DVE, tile_of, it * U + 4)
                for j in range(U):
                    body(it, j, tiles[j], tiles4[j])
            for v in range(U):
                for i in range(G):
                    dve.wait_ge(gathered[v][i], 16 * (n_loop + 1))


def finish_attention(nc, k, tag, acc, na, hd, elus, guard):
    f1 = hd + 1
    with stage(nc, tag) as st:
        rec = st.sb("rec", [P, NT, na])
        h = st.sb("h", [P, 2, TG, D])
        lo = st.sb("lo", [P, 2, TG, D])
        ex = st.sb("ex", [P, 2, TG, D])
        zeros = st.sb("zeros", [P, TG, D])
        order = st.sem("order")
        lows, exps = st.sem("lows"), st.sem("exps")
        block = st.block()

        @block.vector
        def _(dve):
            at = [0]

            def then(ins):
                at[0] += 1
                ins.then_inc(order, 1)
                dve.wait_ge(order, 1 + at[0])

            then(dve.memset(zeros[:], 0.0))
            view = acc.rearrange("p t (h f) -> p t h f", f=f1)
            ends = view[:, NT - 1, :, hd]
            then(dve.tensor_scalar(ends, ends, k.past_end[:], None, ALU.add))
            if guard:
                w = view[:, :, :, hd]
                then(dve.scalar_tensor_tensor(out=w, in0=w, scalar=0.0, in1=w, op0=ALU.is_equal, op1=ALU.add))
            then(dve.reciprocal(rec[:], view[:, :, :, hd]))

            def divide(c):
                s = c % 2
                then(dve.tensor_tensor(h[:, s, :, :].rearrange("p t (h f) -> p t h f", f=hd),
                                       view[:, c * TG:(c + 1) * TG, :, 0:hd],
                                       rec[:, c * TG:(c + 1) * TG, :].unsqueeze(3).broadcast_to([P, TG, na, hd]),
                                       ALU.mult))
                if guard:
                    then(dve.tensor_tensor(lo[:, s, :, :], h[:, s, :, :], h[:, s, :, :], ALU.not_equal))
                    then(dve.copy_predicated(h[:, s, :, :], lo[:, s, :, :].bitcast(I32), zeros[:]))

            def low(c):
                s = c % 2
                then(dve.tensor_scalar(lo[:, s, :, :], h[:, s, :, :], 0.0, None, ALU.min))
                dve.sem_inc(lows, 1)

            def join(c, r):
                s = c % 2
                dve.wait_ge(exps, 1 + r)
                then(dve.tensor_scalar(ex[:, s, :, :], ex[:, s, :, :], -1.0, None, ALU.add))
                then(dve.scalar_tensor_tensor(out=h[:, s, :, :], in0=h[:, s, :, :], scalar=0.0,
                                              in1=ex[:, s, :, :], op0=ALU.max, op1=ALU.add))

            for c in range(NTG):
                divide(c)
                for e in range(elus):
                    low(c)
                    join(c, c * elus + e + 1)
                xs = k.X[:, c * TG:(c + 1) * TG, :]
                then(dve.tensor_tensor(xs, xs, h[:, c % 2, :, :], ALU.add))

        @block.scalar
        def _(act):
            for r in range(NTG * elus):
                s = (r // elus) % 2
                act.wait_ge(lows, 1 + r + 1)
                act.activation(ex[:, s, :, :], lo[:, s, :, :], ACT.Exp).then_inc(exps, 1)


def finish_conv(nc, k, tag, acc, bias, dst, relu, add):
    with stage(nc, tag) as st:
        rec = st.sb("rec", [P, NT])
        b = st.sb("b", [P, D])
        h = st.sb("h", [P, 2, TG, D])
        b_in, order = st.sem("b_in"), st.sem("order")
        block = st.block()

        @block.sync
        def _(sp):
            sp.dma_start(b[:], bias.partition_broadcast(P)).then_inc(b_in, 16)

        @block.vector
        def _(dve):
            at = [0]

            def then(ins):
                at[0] += 1
                ins.then_inc(order, 1)
                dve.wait_ge(order, 1 + at[0])

            then(dve.reciprocal(rec[:], acc[:, :, D]))
            dve.wait_ge(b_in, 1 + 16)
            for c in range(NTG):
                t = slice(c * TG, (c + 1) * TG)
                whole = [P, TG, D]
                hc = h[:, c % 2, :, :]
                then(dve.tensor_tensor(hc, acc[:, t, 0:D], rec[:, t].unsqueeze(2).broadcast_to(whole), ALU.mult))
                if relu:
                    then(dve.tensor_tensor(hc, hc, b[:].unsqueeze(1).broadcast_to(whole), ALU.add))
                    then(dve.tensor_scalar(dst[:, t, :], hc, 0.0, None, ALU.max))
                if add:
                    then(dve.tensor_tensor(hc, hc, b[:].unsqueeze(1).broadcast_to(whole), ALU.add))
                    then(dve.tensor_tensor(dst[:, t, :], dst[:, t, :], hc, ALU.add))


def tokens(nc, k, tag, XT, logits=None, w=None, b=None, hidden=None, keep=False, rows=None):
    kc = D // P
    ne = 0 if w is None else w.shape[1]
    with stage(nc, tag) as st:
        XN = st.sb("XN", [P, TG, D])
        XS = st.sb("XS", [P, TG, kc, P])
        norm = Norm(st, "n")
        norm2 = None if rows is None else Norm(st, "m")
        psT = st.ps("psT", [P, 2, 512])
        turned, turned_out, kept = st.sem("turned"), st.sem("turned_out"), st.sem("kept")
        w_in, rated, rated_out = st.sem("w_in"), st.sem("rated"), st.sem("rated_out")
        hid, hid_out = st.sem("hid"), st.sem("hid_out")
        if w is not None:
            psL = st.ps("psL", [P, 2, 512])
            WR = st.sb("WR", [P, kc, ne])
            BR = st.sb("BR", [P, ne])
        if hidden is not None:
            hw = hidden[0].shape[1]
            psH = st.ps("psH", [P, 2, 512])
            W1 = st.sb("W1", [P, kc, hw])
            B1 = st.sb("B1", [P, 1])
            RH = st.sb("RH", [P, TG, P])
        loads = (0 if w is None else 2) + (0 if hidden is None else 2)
        block = st.block()

        @block.sync
        def _(sp):
            if w is not None:
                if hidden is None:
                    sp.dma_start(WR[:], w.rearrange("(k p) e -> p k e", p=P), allow_slow_non_contiguous=True).then_inc(w_in, 16)
                else:
                    sp.dma_start(WR[:, 0, :], w).then_inc(w_in, 16)
                sp.dma_start(BR[:], b.partition_broadcast(P)).then_inc(w_in, 16)
            if hidden is not None:
                sp.dma_start(W1[:], hidden[0].rearrange("(k p) e -> p k e", p=P)).then_inc(w_in, 16)
                sp.dma_start(B1[:], hidden[1].unsqueeze(1)).then_inc(w_in, 16)
            if loads:
                sp.wait_ge(w_in, 1 + 16 * loads)

        @block.vector
        def _(dve):
            if w is not None:
                dve.wait_ge(w_in, 1 + 16 * loads)
            def normed(it):
                def x_tile(u):
                    return k.X[:, ds(it * TG + u, 1), :].squeeze(1)
                norm.dve_first(dve, it, x_tile)
                dve.wait_ge(turned, 1 + it * TG)
                norm.dve_apply(dve, it, x_tile, lambda u: XN[:, u, :])
                if keep:
                    for u in range(TG):
                        dve.wait_ge(norm.applied, 1 + it * TG + u + 1)
                        dve.tensor_tensor(x_tile(u), x_tile(u), XN[:, u, :], ALU.add).then_inc(kept, 1)
                if rows is not None:
                    dve.wait_ge(norm.applied, 1 + it * TG + TG)
                    norm2.dve_first(dve, it, lambda u: XN[:, u, :])
                    norm2.dve_apply(dve, it, lambda u: XN[:, u, :],
                                    lambda u: rows[:, ds(it * TG + u, 1), :].squeeze(1))

            def rates(it):
                for u in range(0 if w is None else TG):
                    t = it * TG + u
                    dve.wait_ge(rated, 1 + t + 1)
                    dve.tensor_tensor(logits[:, ds(t, 1), :].squeeze(1), psL[:, u % 2, 0:ne], BR[:], ALU.add)\
                       .then_inc(rated_out, 1)

            normed(0)
            with dve.Fori(0, NTG - 1) as it:
                normed(it + 1)
                rates(it)
            rates(NTG - 1)
            if keep:
                dve.wait_ge(kept, 1 + NT)
            if rows is not None:
                dve.wait_ge(norm2.applied, 1 + NT)

        @block.tensor
        def _(pe):
            if w is not None:
                pe.wait_ge(w_in, 1 + 16 * loads)
            with pe.Fori(0, NTG) as it:
                def free(u):
                    return it * TG if u < 2 else it * TG + u - 1
                for u in range(TG):
                    pe.wait_ge(norm.applied, 1 + it * TG + u + 1)
                    pe.wait_ge(turned_out, 1 + free(u))
                    for s in range(kc):
                        ins = pe.transpose(psT[:, u % 2, s * P:(s + 1) * P], XN[:, u, s * P:(s + 1) * P], k.ident[:])
                    ins.then_inc(turned, 1)
                for u in range(0 if hidden is None else TG):
                    pe.wait_ge(turned_out, 1 + it * TG + u + 1)
                    pe.wait_ge(hid_out, 1 + free(u))
                    for s in range(kc):
                        ins = pe.matmul(psH[:, u % 2, 0:P], W1[:, s, :], XS[:, u, s, :],
                                        start=(s == 0), stop=(s == kc - 1))
                    ins.then_inc(hid, 1)
                for u in range(0 if w is None else TG):
                    pe.wait_ge(rated_out, 1 + free(u))
                    if hidden is None:
                        pe.wait_ge(turned_out, 1 + it * TG + u + 1)
                        for s in range(kc):
                            ins = pe.matmul(psL[:, u % 2, 0:ne], XS[:, u, s, :], WR[:, s, :],
                                            start=(s == 0), stop=(s == kc - 1))
                    else:
                        pe.wait_ge(hid_out, 1 + it * TG + u + 1)
                        ins = pe.matmul(psL[:, u % 2, 0:ne], RH[:, u, :], WR[:, 0, :], start=True, stop=True)
                    ins.then_inc(rated, 1)

        @block.scalar
        def _(act):
            if hidden is not None:
                act.wait_ge(w_in, 1 + 16 * loads)
            def roots(it):
                norm.act_root(act, it)
                if rows is not None:
                    norm2.act_root(act, it)

            def turn(it, last):
                def persist(u, ps):
                    return act.activation(XT[:, :, ds(it * TOK + u * P, P)],
                                          ps[:, u % 2, 0:D].rearrange("p (k q) -> p k q", q=P), ACT.Copy)
                for u in range(TG):
                    act.wait_ge(turned, 1 + it * TG + u + 1)
                    if w is not None:
                        act.wait_ge(rated, 1 + it * TG)
                        ins = act.activation(XS[:, u, :, :], psT[:, u % 2, 0:D].rearrange("p (k q) -> p k q", q=P),
                                             ACT.Copy)
                        if rows is None:
                            ins = persist(u, psT)
                    else:
                        ins = persist(u, psT)
                    ins.then_inc(turned_out, 1)
                if not last:
                    roots(it + 1)
                for u in range(0 if hidden is None else TG):
                    act.wait_ge(hid, 1 + it * TG + u + 1)
                    act.activation(RH[:, u, :], psH[:, u % 2, 0:P], ACT.Relu, bias=B1[:, 0:1]).then_inc(hid_out, 1)

            roots(0)
            with act.Fori(0, NTG - 1) as it:
                turn(it, False)
            turn(NTG - 1, True)
            act.wait_ge(turned_out, 1 + NT)


def choose(nc, k, tag, scores, gates, probs, renorm):
    ne = scores.shape[2]
    whole = [P, NT, ne]
    with stage(nc, tag) as st:
        p = st.sb("p", whole)
        d = st.sb("d", whole)
        e = st.sb("e", whole)
        rev = st.sb("rev", [P, ne])
        v = st.sb("v", whole)
        hot = [st.sb(f"hot{i}", whole) for i in range(2)]
        best = [st.sb(f"best{i}", [P, NT]) for i in range(2)]
        wt = [st.sb(f"wt{i}", [P, NT]) for i in range(2)]
        m, s1, s2 = (st.sb(n, [P, NT]) for n in ("m", "s1", "s2"))
        order, exps = st.sem("order"), st.sem("exps")
        at_diff = []
        block = st.block()

        @block.vector
        def _(dve):
            at = [0]

            def then(ins):
                at[0] += 1
                ins.then_inc(order, 1)
                dve.wait_ge(order, 1 + at[0])

            def wide(t):
                return t[:].unsqueeze(2).broadcast_to(whole)

            if probs:
                then(dve.tensor_reduce(m[:], scores, AX.X, ALU.max))
                then(dve.tensor_tensor(d[:], scores, wide(m), ALU.subtract))
                dve.wait_ge(exps, 1 + 1)
                then(dve.tensor_reduce(s1[:], e[:], AX.X, ALU.add))
                then(dve.reciprocal(s2[:], s1[:]))
                then(dve.tensor_tensor(p[:], e[:], wide(s2), ALU.mult))
            else:
                then(dve.tensor_scalar(p[:], scores, 0.0, None, ALU.add))
            then(dve.tensor_scalar(rev[:], k.iota[:, 0:ne], -1.0, float(ne), ALU.mult, ALU.add))
            for i in range(2):
                then(dve.tensor_reduce(best[i][:], p[:], AX.X, ALU.max))
                then(dve.tensor_tensor(v[:], p[:], wide(best[i]), ALU.is_equal))
                then(dve.tensor_tensor(v[:], v[:], rev[:].unsqueeze(1).broadcast_to(whole), ALU.mult))
                then(dve.tensor_reduce(m[:], v[:], AX.X, ALU.max))
                then(dve.tensor_tensor(hot[i][:], v[:], wide(m), ALU.is_equal))
                if i == 0:
                    then(dve.scalar_tensor_tensor(out=p[:], in0=hot[0][:], scalar=-BIG, in1=p[:],
                                                  op0=ALU.mult, op1=ALU.add))
            if renorm:
                then(dve.tensor_tensor(s1[:], best[0][:], best[1][:], ALU.add))
                then(dve.reciprocal(s2[:], s1[:]))
                then(dve.tensor_tensor(wt[0][:], best[0][:], s2[:], ALU.mult))
                then(dve.tensor_tensor(wt[1][:], best[1][:], s2[:], ALU.mult))
            else:
                then(dve.tensor_tensor(m[:], best[1][:], best[0][:], ALU.subtract))
                at_diff.append(at[0])
                dve.wait_ge(exps, 1 + 1 + probs)
                then(dve.tensor_scalar(s2[:], s1[:], 1.0, None, ALU.add))
                then(dve.reciprocal(wt[0][:], s2[:]))
                then(dve.tensor_tensor(wt[1][:], s1[:], wt[0][:], ALU.mult))
            for i in range(2):
                then(dve.tensor_tensor(hot[i][:], hot[i][:], wide(wt[i]), ALU.mult))
            then(dve.tensor_tensor(gates.rearrange("p e t -> p t e"), hot[0][:], hot[1][:], ALU.add))

        @block.scalar
        def _(act):
            if probs:
                act.wait_ge(order, 1 + 2)
                act.activation(e[:], d[:], ACT.Exp).then_inc(exps, 1)
            if not renorm:
                act.wait_ge(order, 1 + at_diff[0])
                act.activation(s1[:], m[:], ACT.Exp).then_inc(exps, 1)


def feed_forward(nc, k, tag, XT, w1, b1, w2, b2, gates, func, mid=None, jobs=()):
    ne, _, h1 = w1.shape
    kc = D // P
    hc = h1 // P
    mc = 0 if mid is None else mid[0].shape[2] // P
    lc = mc or hc
    pair = min(2, ne)
    na = pair * (hc + mc)
    nb = pair * TG
    with stage(nc, tag) as st:
        W1 = [st.sb(f"W1_{e}", [P, kc, h1]) for e in range(pair)]
        B1 = [st.sb(f"B1_{e}", [P, hc]) for e in range(pair)]
        W2 = [st.sb(f"W2_{e}", [P, lc, D]) for e in range(pair)]
        H = [st.sb(f"H_{e}", [P, hc, 2, HALF]) for e in range(pair)]
        if mid is not None:
            WM = [st.sb(f"WM_{e}", [P, hc, mc * P]) for e in range(pair)]
            BM = [st.sb(f"BM_{e}", [P, mc]) for e in range(pair)]
            HM = [st.sb(f"HM_{e}", [P, mc, 2, HALF]) for e in range(pair)]
        B2 = st.sb("B2", [P, ne, D])
        psA = st.ps("psA", [P, 2, 2, 512])
        psB = st.ps("psB", [P, 4, 512])
        b2_in, biased = st.sem("b2_in"), st.sem("biased")
        first_in = [st.sem(f"first_in{e}") for e in range(pair)]
        rest_in = [st.sem(f"rest_in{e}") for e in range(pair)]
        first_used = [st.sem(f"first_used{e}") for e in range(pair)]
        rest_used = [st.sem(f"rest_used{e}") for e in range(pair)]
        made, active, out_made, kept = (st.sem(s) for s in ("made", "active", "out_made", "kept"))
        n_rest = 4 if mid is not None else 2
        scatters = [Scatter(st, f"job{n}", *job) for n, job in enumerate(jobs)]
        block = st.block()

        @block.gpsimd
        def _(pool):
            for scatter in scatters:
                scatter.run(pool)

        @block.sync
        def _(sp):
            sp.dma_start(B2[:].rearrange("p e d -> p (e d)"), b2.rearrange("e d -> (e d)").partition_broadcast(P))\
              .then_inc(b2_in, 16)
            with sp.Fori(0, ne // pair) as pr:
                for e in range(pair):
                    x = pr * pair + e
                    sp.wait_ge(first_used[e], 1 + pr * NTG)
                    sp.dma_start(W1[e][:], w1[ds(x, 1), :, :].rearrange("o (k p) h -> p (o k) h", p=P))\
                      .then_inc(first_in[e], 16)
                for e in range(pair):
                    x = pr * pair + e
                    sp.wait_ge(rest_used[e], 1 + pr * NTG)
                    sp.dma_start(B1[e][:], b1[ds(x, 1)].squeeze(0)).then_inc(rest_in[e], 16)
                    if mid is not None:
                        sp.dma_start(WM[e][:], mid[0][ds(x, 1), :, :].rearrange("o (k p) h -> p (o k) h", p=P))\
                          .then_inc(rest_in[e], 16)
                        sp.dma_start(BM[e][:], mid[1][ds(x, 1)].squeeze(0)).then_inc(rest_in[e], 16)
                    sp.dma_start(W2[e][:], w2[ds(x, 1), :, :].rearrange("o (k p) h -> p (o k) h", p=P))\
                      .then_inc(rest_in[e], 16)

        def steps(eng, body):
            with eng.Fori(0, ne // pair) as pr:
                with eng.Fori(0, NTG) as g:
                    body(pr, g, pr * NTG + g)

        @block.tensor
        def _(pe):
            def layer(s, w, src, chunks, ks, at):
                for c in range(chunks):
                    n = at + c
                    pe.wait_ge(active, 1 + (s * na if n < 2 else s * na + n - 1))
                    for half in range(2):
                        for i in range(ks):
                            ins = pe.matmul(psA[:, n % 2, half, 0:HALF], w[:, i, c * P:(c + 1) * P], src(i, half),
                                            start=(i == 0), stop=(i == ks - 1))
                    ins.then_inc(made, 1)
                return ins

            def body(pr, g, s):
                for e in range(pair):
                    pe.wait_ge(first_in[e], 1 + pr * 16 + 16)
                    layer(s, W1[e], lambda i, half: XT[:, i, ds(g * TOK + half * HALF, HALF)], hc, kc, e * hc)
                    pe.wait_ge(made, 1 + s * na + (e + 1) * hc)
                    pe.sem_inc(first_used[e], 1)
                for e in range(pair if mid is not None else 0):
                    pe.wait_ge(rest_in[e], 1 + pr * (16 * n_rest) + 16 * n_rest)
                    pe.wait_ge(active, 1 + s * na + (e + 1) * hc)
                    layer(s, WM[e], lambda i, half: H[e][:, i, half, :], mc, hc, pair * hc + e * mc)
                for e in range(pair):
                    pe.wait_ge(rest_in[e], 1 + pr * (16 * n_rest) + 16 * n_rest)
                    pe.wait_ge(active, 1 + (s * na + (pair * hc + (e + 1) * mc if mid is not None else (e + 1) * hc)))
                    hid = H[e] if mid is None else HM[e]
                    for j in range(TG):
                        n = e * TG + j
                        pe.wait_ge(kept, 1 + (s * nb if n < 4 else s * nb + n - 3))
                        flat = hid[:].rearrange("p c a t -> p c (a t)")
                        for c in range(lc):
                            ins = pe.matmul(psB[:, n % 4, 0:D], flat[:, c, j * P:(j + 1) * P], W2[e][:, c, :],
                                            start=(c == 0), stop=(c == lc - 1))
                        ins.then_inc(out_made, 1)
                    pe.wait_ge(out_made, 1 + s * nb + (e + 1) * TG)
                    pe.sem_inc(rest_used[e], 1)
            steps(pe, body)

        @block.scalar
        def _(act):
            def body(pr, g, s):
                for e in range(pair):
                    act.wait_ge(rest_used[e], 1 + s)
                    act.wait_ge(rest_in[e], 1 + pr * (16 * n_rest) + 16 * n_rest)
                    for c in range(hc):
                        n = e * hc + c
                        act.wait_ge(made, 1 + s * na + n + 1)
                        act.activation(H[e][:, c, :, :], psA[:, n % 2, :, 0:HALF], func, bias=B1[e][:, c:c + 1])\
                           .then_inc(active, 1)
                for e in range(pair if mid is not None else 0):
                    for c in range(mc):
                        n = pair * hc + e * mc + c
                        act.wait_ge(made, 1 + s * na + n + 1)
                        act.activation(HM[e][:, c, :, :], psA[:, n % 2, :, 0:HALF], func, bias=BM[e][:, c:c + 1])\
                           .then_inc(active, 1)
            steps(act, body)

        @block.vector
        def _(dve):
            def body(pr, g, s):
                for e in range(pair):
                    for j in range(TG):
                        n = e * TG + j
                        x = k.X[:, ds(g * TG + j, 1), :].squeeze(1)
                        gate = gates.rearrange("p e t -> p (e t)")[:, ds(pr * (pair * NT) + e * NT + g * TG + j, 1)]
                        dve.wait_ge(kept, 1 + s * nb + n)
                        dve.scalar_tensor_tensor(out=x, in0=B2[:, ds(pr * pair + e, 1), :].squeeze(1), scalar=gate,
                                                 in1=x, op0=ALU.mult, op1=ALU.add).then_inc(biased, 1)
                        dve.wait_ge(out_made, 1 + s * nb + n + 1)
                        dve.wait_ge(biased, 1 + s * nb + n + 1)
                        dve.scalar_tensor_tensor(out=x, in0=psB[:, n % 4, 0:D], scalar=gate, in1=x,
                                                 op0=ALU.mult, op1=ALU.add).then_inc(kept, 1)
            dve.wait_ge(b2_in, 1 + 16)
            steps(dve, body)
            dve.wait_ge(kept, 1 + nb * NTG * (ne // pair))


def place_tokens(nc, k, tag, gates, slot, weight, expert_of, rows):
    ne = gates.shape[1]
    n_groups = expert_of.shape[1]
    per_part = rows.shape[0] // P - 1
    parts = 4
    with stage(nc, tag) as st:
        member = st.sb("member", [P, ne, NT])
        rank = st.sb("rank", [P, ne, NT])
        here = st.sb("here", [P, ne, NT])
        ones_t = st.sb("ones_t", [P, NT])
        ones_e = st.sb("ones_e", [P, ne])
        count = st.sb("count", [P, ne])
        tot_i = st.sb("tot_i", [P, ne], I32)
        tot_j = st.sb("tot_j", [P, ne], I32)
        n_grp = st.sb("n_grp", [P, ne])
        end_g = st.sb("end_g", [P, ne])
        start = st.sb("start", [P, ne])
        best = st.sb("best", [P, NT])
        g_i = st.sb("g_i", [1, n_groups], I32)
        g_f = st.sb("g_f", [1, n_groups])
        past = st.sb("past", [1, n_groups, ne])
        expert_r = st.sb("expert_r", [1, n_groups])
        zeros = st.sb("zeros", [P, per_part // parts, D])
        psum = st.ps("psum", [P, 2, 512])
        order, summed, iota_made, zeroed, cleared, ranked = (
            st.sem(s) for s in ("order", "summed", "iota_made", "zeroed", "cleared", "ranked"))
        block = st.block()

        @block.gpsimd
        def _(pool):
            pool.memset(zeros[:], 0.0).then_inc(zeroed, 1)
            pool.iota(g_i[:], pattern=[[1, n_groups]], base=0, channel_multiplier=0).then_inc(iota_made, 1)

        @block.sync
        def _(sp):
            sp.wait_ge(zeroed, 1 + 1)
            by_part = rows[0:per_part * P, :].rearrange("(p c) d -> p c d", p=P)
            w = per_part // parts
            for q in range(parts):
                sp.dma_start(by_part[:, q * w:(q + 1) * w, :], zeros[:]).then_inc(cleared, 16)
            sp.wait_ge(cleared, 1 + 16 * parts)

        @block.tensor
        def _(pe):
            pe.wait_ge(order, 1 + 4)
            pe.matmul(psum[:, 0, 0:ne], k.tri[:], count[:], start=True, stop=True).then_inc(summed, 1)
            pe.matmul(psum[:, 1, 0:ne], k.ones[:], count[:], start=True, stop=True).then_inc(summed, 1)

        @block.vector
        def _(dve):
            at = [0]

            def then(ins):
                at[0] += 1
                ins.then_inc(order, 1)
                dve.wait_ge(order, 1 + at[0])

            then(dve.memset(ones_t[:], 1.0))
            then(dve.memset(ones_e[:], 1.0))
            then(dve.tensor_scalar(member[:], gates, 0.0, None, ALU.is_gt))
            then(dve.tensor_reduce(count[:], member[:], AX.X, ALU.add))
            dve.wait_ge(summed, 1 + 2)
            then(dve.tensor_scalar(tot_i[:], psum[:, 1, 0:ne], float(SG - 1), None, ALU.add))
            then(dve.tensor_scalar(tot_j[:], tot_i[:], SG.bit_length() - 1, None, ALU.arith_shift_right))
            then(dve.tensor_copy(n_grp[:], tot_j[:]))
            then(dve.tensor_tensor_scan(end_g[:], ones_e[:], n_grp[:], 0.0, ALU.mult, ALU.add))
            then(dve.tensor_tensor(start[:], end_g[:], n_grp[:], ALU.subtract))
            then(dve.tensor_scalar(start[:], start[:], float(SG), None, ALU.mult))
            then(dve.tensor_tensor(start[:], psum[:, 0, 0:ne], start[:], ALU.add))
            dve.wait_ge(iota_made, 1 + 1)
            then(dve.tensor_copy(g_f[:], g_i[:]))
            then(dve.tensor_tensor(past[:], g_f[:].unsqueeze(2).broadcast_to([1, n_groups, ne]),
                                   end_g[0:1, :].unsqueeze(1).broadcast_to([1, n_groups, ne]), ALU.is_ge))
            then(dve.tensor_reduce(expert_r[:], past[:], AX.X, ALU.add))
            then(dve.tensor_scalar(expert_of, expert_r[:], float(ne - 1), None, ALU.min))
            for e in range(ne):
                dve.tensor_tensor_scan(rank[:, e, :], ones_t[:], member[:, e, :], start[:, e:e + 1],
                                       ALU.mult, ALU.add).then_inc(ranked, 1)
            dve.wait_ge(ranked, 1 + ne)
            then(dve.tensor_tensor(rank[:], rank[:], member[:], ALU.mult))
            for i in range(2):
                then(dve.tensor_reduce(best[:], rank[:].rearrange("p e t -> p t e"), AX.X, ALU.max))
                last = best[:].unsqueeze(1).broadcast_to([P, ne, NT])
                then(dve.tensor_tensor(here[:], rank[:], last, ALU.is_equal))
                then(dve.tensor_tensor(here[:], here[:], gates, ALU.mult))
                then(dve.tensor_reduce(weight[:, i, :], here[:].rearrange("p e t -> p t e"), AX.X, ALU.add))
                then(dve.tensor_scalar(slot[:, i, :], best[:], -1.0, 0.0, ALU.add, ALU.max))
                if i == 0:
                    then(dve.tensor_tensor(here[:], rank[:], last, ALU.not_equal))
                    then(dve.tensor_tensor(rank[:], rank[:], here[:], ALU.mult))


def send_tokens(nc, tag, XR, slot, weight, rows):
    with stage(nc, tag) as st:
        out = st.sb("out", [P, TG, D])
        no_slot = st.sb("no_slot", [P, 2, NT])
        to_f = st.sb("to_f", [P, 2, NT])
        to = st.sb("to", [P, 2, NT], I32)
        idx = st.sb("idx", [P, TG, 2], I32)
        order, copied = st.sem("order"), st.sem("copied")
        sent = [st.gather_sem(f"sent{u}") for u in range(TG)]
        block = st.block()

        @block.vector
        def _(dve):
            spare = float(rows.shape[0] - P)
            dve.tensor_copy(to_f[:], slot).then_inc(order, 1)
            dve.tensor_scalar(no_slot[:], weight, 0.0, spare, ALU.is_equal, ALU.mult).then_inc(order, 1)
            dve.wait_ge(order, 1 + 2)
            dve.tensor_tensor(to[:], to_f[:], no_slot[:], ALU.max).then_inc(order, 1)
            dve.wait_ge(order, 1 + 3)

            def copy(it):
                for u in range(TG):
                    t = it * TG + u
                    if not isinstance(it, int):
                        dve.wait_ge(sent[u], it * 32)
                    dve.tensor_scalar(out[:, u, :], XR[:, ds(t, 1), :].squeeze(1), 0.0, None, ALU.add).then_inc(copied, 1)
                    dve.tensor_scalar(idx[:, u, :], to[:, :, ds(t, 1)].squeeze(2), 0, None, ALU.add).then_inc(copied, 1)

            copy(0)
            with dve.Fori(1, NTG) as it:
                copy(it)

        @block.gpsimd
        def _(pool):
            with pool.Fori(0, NTG) as it:
                for u in range(TG):
                    pool.wait_ge(copied, 1 + it * (2 * TG) + 2 * u + 2)
                    pool.nop(nofuse=True)
                    for i in range(2):
                        pool.indirect_dma_start(
                            out=rows, out_offset=bass.IndirectOffsetOnAxis(ap=idx[:, u, i:i + 1], axis=0),
                            in_=out[:, u, :], in_offset=None).then_inc(sent[u], 16)
            for u in range(TG):
                pool.wait_ge(sent[u], 32 * NTG)


def expert_groups(nc, k, tag, rows, results, expert_of, w1, b1, w2, b2, affine, func, jobs=()):
    ne, _, h1 = w1.shape
    kc = D // P
    hc = h1 // P
    sc = SG // P
    n_groups = (rows.shape[0] - P) // SG
    half = n_groups // 2
    with stage(nc, tag) as st:
        XR = st.sb("XR", [P, 2, sc, D])
        XE = st.sb("XE", [P, 2, kc, SG])
        AF = st.sb("AF", [P, 2, 2, kc])
        W1 = st.sb("W1", [P, 2, kc, h1])
        B1 = st.sb("B1", [P, 2, hc])
        W2 = st.sb("W2", [P, 2, hc, D])
        B2 = st.sb("B2", [P, 2, D])
        H = st.sb("H", [P, 2, hc, SG])
        Y = st.sb("Y", [P, 2, sc, D])
        psT = st.ps("psT", [P, 2, 512])
        psA = st.ps("psA", [P, 4, 512])
        psB = st.ps("psB", [P, sc, 512])

        def both(name):
            return [st.sem(f"{name}{s}") for s in range(2)]
        rows_in, first_in, rest_in, stored = both("rows_in"), both("first_in"), both("rest_in"), both("stored")
        turned, scaled, first_used, rest_used = both("turned"), both("scaled"), both("first_used"), both("rest_used")
        active = [st.sem(f"active{b}") for b in range(4)]
        kept = [st.sem(f"kept{j}") for j in range(sc)]
        made, out_made = st.sem("made"), st.sem("out_made")
        scatters = [Scatter(st, f"job{n}", *job) for n, job in enumerate(jobs)]
        block = st.block()

        @block.gpsimd
        def _(pool):
            for scatter in scatters:
                scatter.run(pool)

        def place(it, j):
            return it * 2 + j, j % 2, it + j // 2, not isinstance(it, int) or 0 <= it * 2 + j < n_groups

        def again(eng, sem, n, per=1):
            if not isinstance(n, int) or n > 0:
                eng.wait_ge(sem, 1 + n * per)

        def steps(eng, body):
            for j in range(-2, 2):
                body(0, j, None)
            with eng.Fori(1, half - 1) as it:
                for j in range(2):
                    body(it, j, None)
            for j in range(2):
                body(half - 1, j, None)

        @block.sync
        def _(sp):
            def load_rows(it, j, expert):
                g, s, n, there = place(it, j)
                if there:
                    again(sp, turned[s], n)
                    sp.nop(nofuse=True)
                    again(sp, scaled[s], n, kc)
                    sp.nop(nofuse=True)
                    sp.dma_start(XR[:, s, :, :], rows[ds(g * SG, SG), :].rearrange("(c p) d -> p c d", p=P))\
                      .then_inc(rows_in[s], 16)
                    sp.dma_start(AF[:, s, :, :], affine[ds(expert, 1)].squeeze(0)).then_inc(rows_in[s], 16)

            def load_first(it, j, expert):
                g, s, n, there = place(it, j)
                if there:
                    again(sp, first_used[s], n)
                    if not isinstance(it, int) or g >= 2:
                        sp.nop(nofuse=True)
                        sp.wait_ge(active[3], 1 + (g - 1) * (hc // 4))
                    sp.nop(nofuse=True)
                    sp.dma_start(W1[:, s, :, :], w1[ds(expert, 1), :, :].rearrange("o (k p) h -> p (o k) h", p=P))\
                      .then_inc(first_in[s], 16)
                    sp.dma_start(B1[:, s, :], b1[ds(expert, 1)].squeeze(0)).then_inc(first_in[s], 16)

            def load_rest(it, j, expert):
                g, s, n, there = place(it, j)
                if there:
                    again(sp, rest_used[s], n)
                    again(sp, stored[s], n, 16)
                    sp.nop(nofuse=True)
                    sp.dma_start(W2[:, s, :, :], w2[ds(expert, 1), :, :].rearrange("o (k p) h -> p (o k) h", p=P))\
                      .then_inc(rest_in[s], 16)
                    sp.dma_start(B2[:, s, :], b2[ds(expert, 1), :].squeeze(0).partition_broadcast(P))\
                      .then_inc(rest_in[s], 16)

            def store(it, j):
                g, s, n, there = place(it, j)
                if there:
                    for b in range(sc):
                        sp.nop(nofuse=True)
                        sp.wait_ge(kept[b], 1 + g + 1)
                    sp.nop(nofuse=True)
                    sp.dma_start(results[ds(g * SG, SG), :].rearrange("(c p) d -> p c d", p=P), Y[:, s, :, :])\
                      .then_inc(stored[s], 16)

            def experts(it):
                return nc.values_load_multi_w_load_instructions(
                    expert_of[:, ds(it * 2, 3)], engines=(mybir.EngineType.SP,), min_val=0, max_val=ne - 1,
                    skip_runtime_bounds_check_because="place_tokens makes only experts 0 .. ne - 1")[1]

            def pair(it):
                e = experts(it)
                for j in range(2):
                    load_first(it, j, e[j])
                    load_rows(it, j + 1, e[j + 1])
                    if not isinstance(it, int) or it > 0:
                        store(it, j - 2)
                    load_rest(it, j, e[j])

            load_rows(0, 0, experts(0)[0])
            pair(0)
            with sp.Fori(1, half - 1) as it:
                pair(it)
            pair(half - 1)
            store(half - 1, 0)
            store(half - 1, 1)
            for s in range(2):
                sp.wait_ge(stored[s], 1 + 16 * half)

        @block.tensor
        def _(pe):
            def turn(it, j):
                g, s, n, there = place(it, j)
                if there:
                    pe.wait_ge(rows_in[s], 1 + (n + 1) * 32)
                    again(pe, scaled[s], n, kc)
                    for i in range(kc):
                        for c in range(sc):
                            ins = pe.transpose(psT[:, s, i * SG + c * P:i * SG + (c + 1) * P],
                                               XR[:, s, c, i * P:(i + 1) * P], k.ident[:])
                    ins.then_inc(turned[s], 1)

            def first(it, j):
                g, s, n, there = place(it, j)
                if there:
                    pe.wait_ge(first_in[s], 1 + (n + 1) * 32)
                    pe.wait_ge(scaled[s], 1 + (n + 1) * kc)
                    for c in range(hc):
                        pe.wait_ge(active[c % 4], 1 + g * (hc // 4) + c // 4)
                        for i in range(kc):
                            ins = pe.matmul(psA[:, c % 4, 0:SG], W1[:, s, i, c * P:(c + 1) * P], XE[:, s, i, :],
                                            start=(i == 0), stop=(i == kc - 1))
                        ins.then_inc(made, 1)
                    pe.wait_ge(made, 1 + (g + 1) * hc)
                    pe.sem_inc(first_used[s], 1)

            def second(it, j):
                g, s, n, there = place(it, j)
                if there:
                    pe.wait_ge(rest_in[s], 1 + (n + 1) * 32)
                    for b in range(4):
                        pe.wait_ge(active[b], 1 + (g + 1) * (hc // 4))
                    for b in range(sc):
                        pe.wait_ge(kept[b], 1 + g)
                        for c in range(hc):
                            ins = pe.matmul(psB[:, b, 0:D], H[:, s, c, b * P:(b + 1) * P], W2[:, s, c, :],
                                            start=(c == 0), stop=(c == hc - 1))
                        ins.then_inc(out_made, 1)
                    pe.wait_ge(out_made, 1 + (g + 1) * sc)
                    pe.sem_inc(rest_used[s], 1)

            def body(it, j, _):
                turn(it, j + 2)
                first(it, j + 1)
                second(it, j)
            steps(pe, body)

        @block.scalar
        def _(act):
            def body(it, j, _):
                g, s, n, there = place(it, j)
                if there:
                    act.wait_ge(first_in[s], 1 + (n + 1) * 32)
                    again(act, rest_used[s], n)
                    for c in range(hc):
                        act.wait_ge(made, 1 + g * hc + c + 1)
                        act.activation(H[:, s, c, :], psA[:, c % 4, 0:SG], func, bias=B1[:, s, c:c + 1])\
                           .then_inc(active[c % 4], 1)
            steps(act, body)

        @block.vector
        def _(dve):
            def scale(it, j):
                g, s, n, there = place(it, j)
                if there:
                    dve.wait_ge(turned[s], 1 + n + 1)
                    dve.wait_ge(rows_in[s], 1 + (n + 1) * 32)
                    again(dve, first_used[s], n)
                    for i in range(kc):
                        dve.tensor_scalar(XE[:, s, i, :], psT[:, s, i * SG:(i + 1) * SG], AF[:, s, 0, i:i + 1],
                                          AF[:, s, 1, i:i + 1], ALU.mult, ALU.add).then_inc(scaled[s], 1)

            def keep(it, j):
                g, s, n, there = place(it, j)
                if there:
                    again(dve, stored[s], n, 16)
                    dve.wait_ge(rest_in[s], 1 + (n + 1) * 32)
                    for b in range(sc):
                        dve.wait_ge(out_made, 1 + g * sc + b + 1)
                        dve.tensor_tensor(Y[:, s, b, :], psB[:, b, 0:D], B2[:, s, :], ALU.add).then_inc(kept[b], 1)

            def body(it, j, _):
                scale(it, j + 2)
                keep(it, j)
            steps(dve, body)


def take_results(nc, k, tag, results, slot, weight):
    with stage(nc, tag) as st:
        idx = st.sb("idx", [P, TG, 2], I32)
        Y = st.sb("Y", [P, TG, 2, D])
        noted, first, kept = st.sem("noted"), st.sem("first"), st.sem("kept")
        fetched = [[st.gather_sem(f"fetched{u}_{i}") for i in range(2)] for u in range(TG)]
        block = st.block()

        @block.gpsimd
        def _(pool):
            with pool.Fori(0, NTG) as it:
                for u in range(TG):
                    pool.wait_ge(noted, 1 + it * TG + u + 1)
                    pool.wait_ge(kept, 1 + it * TG)
                    pool.nop(nofuse=True)
                    for i in range(2):
                        pool.indirect_dma_start(out=Y[:, u, i, :], out_offset=None, in_=results,
                                                in_offset=bass.IndirectOffsetOnAxis(ap=idx[:, u, i:i + 1], axis=0))\
                            .then_inc(fetched[u][i], 16)

        @block.vector
        def _(dve):
            def note(it):
                for u in range(TG):
                    dve.tensor_scalar(idx[:, u, :], slot[:, :, ds(it * TG + u, 1)].squeeze(2), 0, None, ALU.add)\
                       .then_inc(noted, 1)

            def add(it):
                for u in range(TG):
                    t = it * TG + u
                    x = k.X[:, ds(t, 1), :].squeeze(1)
                    for i, sem in ((0, first), (1, kept)):
                        dve.wait_ge(fetched[u][i], (it + 1) * 16)
                        if i == 1:
                            dve.wait_ge(first, 1 + t + 1)
                        dve.scalar_tensor_tensor(out=x, in0=Y[:, u, i, :], scalar=weight[:, i, ds(t, 1)], in1=x,
                                                 op0=ALU.mult, op1=ALU.add).then_inc(sem, 1)

            note(0)
            with dve.Fori(0, NTG - 1) as it:
                add(it)
                note(it + 1)
            add(NTG - 1)
            dve.wait_ge(kept, 1 + NT)


def pick_tokens(nc, k, tag, scores, gates, n_best):
    flat = nc.dram_tensor(f"{tag}_scores", (NT, P), F32, kind="Internal").ap()
    with stage(nc, tag) as st:
        sc = st.sb("sc", [P, NT])
        row = st.sb("row", [P, NP])
        cmp = st.sb("cmp", [P, 2, NP])
        low = st.sb("low", [P, P])
        cnt = st.sb("cnt", [P, NT, 3])
        rank = st.sb("rank", [P, NT])
        order, lows, moved, counted = (st.sem(s) for s in ("order", "lows", "moved", "counted"))
        block = st.block()

        @block.gpsimd
        def _(pool):
            pool.memset(low[:], 1.0).then_inc(lows, 1)
            pool.wait_ge(lows, 1 + 1)
            pool.affine_select(out=low[:], in_=low[:], compare_op=ALU.is_gt, fill=0.0, base=0,
                               pattern=[[-1, P]], channel_multiplier=1).then_inc(lows, 1)

        @block.sync
        def _(sp):
            sp.wait_ge(order, 1 + 3)
            sp.dma_start(flat.rearrange("t p -> p t"), sc[:], allow_slow_non_contiguous=True).then_inc(moved, 16)
            sp.wait_ge(moved, 1 + 16)
            sp.dma_start(row[:], flat.rearrange("t p -> (t p)").partition_broadcast(P)).then_inc(moved, 16)

        @block.vector
        def _(dve):
            at = [0]

            def then(ins):
                at[0] += 1
                ins.then_inc(order, 1)
                dve.wait_ge(order, 1 + at[0])

            then(dve.tensor_scalar(sc[:], scores, 0.0, None, ALU.add))
            then(dve.scalar_tensor_tensor(out=sc[:, NT - 1:NT], in0=k.past_end[:], scalar=-BIG, in1=sc[:, NT - 1:NT],
                                          op0=ALU.mult, op1=ALU.add))
            then(dve.memset(cnt[:], 0.0))
            dve.wait_ge(moved, 1 + 32)
            dve.wait_ge(lows, 1 + 2)
            n = 0
            for t in range(NT):
                own = sc[:, t:t + 1]
                steps = [
                    lambda o: dve.tensor_scalar(o[:, t * P:NP], row[:, t * P:NP], own, 0.0, ALU.is_gt, ALU.add,
                                                accum_out=cnt[:, t, 0:1]),
                    lambda o: dve.scalar_tensor_tensor(out=o[:, 0:P], in0=row[:, t * P:(t + 1) * P], scalar=own,
                                                       in1=low[:], op0=ALU.is_equal, op1=ALU.mult,
                                                       accum_out=cnt[:, t, 1:2]),
                ]
                if t:
                    steps.append(lambda o: dve.tensor_scalar(o[:, 0:t * P], row[:, 0:t * P], own, 0.0, ALU.is_ge,
                                                             ALU.add, accum_out=cnt[:, t, 2:3]))
                for step in steps:
                    if n >= 2:
                        dve.wait_ge(counted, 1 + n - 1)
                    step(cmp[:, n % 2, :]).then_inc(counted, 1)
                    n += 1
            dve.wait_ge(counted, 1 + n)
            then(dve.tensor_reduce(rank[:], cnt[:], AX.X, ALU.add))
            then(dve.scalar_tensor_tensor(out=gates, in0=rank[:], scalar=float(n_best), in1=scores,
                                          op0=ALU.is_lt, op1=ALU.mult))


class Softplus:

    def __init__(self, st, name, shape):
        self.ab, self.ex = st.sb(f"{name}_ab", shape), st.sb(f"{name}_ex", shape)
        self.has_abs, self.has_exp, self.has_log, self.done = (
            st.sem(f"{name}_{s}") for s in ("abs", "exp", "log", "done"))

    def dve_first(self, dve, src):
        dve.scalar_tensor_tensor(out=self.ab[:], in0=src, scalar=-1.0, in1=src, op0=ALU.mult, op1=ALU.max)\
           .then_inc(self.has_abs, 1)

    def act_part(self, act, n):
        act.wait_ge(self.has_abs, 1 + n + 1)
        act.activation(self.ex[:], self.ab[:], ACT.Exp, scale=-1.0).then_inc(self.has_exp, 1)
        act.wait_ge(self.has_exp, 1 + n + 1)
        act.activation(self.ex[:], self.ex[:], ACT.Ln, bias=1.0).then_inc(self.has_log, 1)

    def dve_last(self, dve, src, ex, dst):
        return dve.scalar_tensor_tensor(out=dst, in0=src, scalar=0.0, in1=ex, op0=ALU.max, op1=ALU.add)


def atom_tables(nc, k, tag, w, b, table, acc):
    kc = D // P
    wide = 2 * D
    with stage(nc, tag) as st:
        W = st.sb("W", [P, kc, wide])
        B = st.sb("B", [1, wide])
        XN = st.sb("XN", [P, TG, D])
        XP = st.sb("XP", [P, TG, D])
        XS = st.sb("XS", [P, TG, kc, P])
        PRE = st.sb("PRE", [P, TG, wide])
        ROW = st.sb("ROW", [P, TG, D])
        norm = Norm(st, "n")
        sp1 = Softplus(st, "s1", [P, TG, D])
        sp2 = Softplus(st, "s2", [P, TG, wide])
        psT = st.ps("psT", [P, 2, 512])
        psH = st.ps("psH", [P, 2, 512])
        w_in, turned, turned_out, made, pre_out, ready, stored, own = (
            st.sem(s) for s in ("w_in", "turned", "turned_out", "made", "pre_out", "ready", "stored", "own"))
        block = st.block()

        @block.sync
        def _(sp):
            sp.dma_start(W[:], w.rearrange("(k p) c -> p k c", p=P)).then_inc(w_in, 16)
            sp.dma_start(B[:], b.unsqueeze(0)).then_inc(w_in, 16)
            with sp.Fori(0, NTG) as it:
                sp.wait_ge(sp2.done, 1 + it * 2 + 2)
                sp.dma_start(table[ds(it * TOK, TOK), :].rearrange("(t p) d -> p t d", p=P), ROW[:]).then_inc(stored, 16)
            sp.wait_ge(stored, 1 + 16 * NTG)

        @block.vector
        def _(dve):
            def features(it):
                def x_tile(u):
                    return k.X[:, ds(it * TG + u, 1), :].squeeze(1)
                norm.dve_first(dve, it, x_tile)
                norm.dve_apply(dve, it, x_tile, lambda u: XN[:, u, :])
                dve.wait_ge(norm.applied, 1 + it * TG + TG)
                sp1.dve_first(dve, XN[:])
                dve.wait_ge(sp1.has_log, 1 + it + 1)
                dve.wait_ge(turned, 1 + it * TG)
                sp1.dve_last(dve, XN[:], sp1.ex[:], XP[:]).then_inc(own, 1)
                dve.wait_ge(own, 1 + it + 1)
                dve.tensor_scalar(XP[:], XP[:], -LN2, None, ALU.add).then_inc(sp1.done, 1)

            def rows(it):
                dve.wait_ge(pre_out, 1 + it * TG + TG)
                sp2.dve_first(dve, PRE[:])
                dve.wait_ge(sp2.has_log, 1 + it + 1)
                sp2.dve_last(dve, PRE[:, :, 0:D], sp2.ex[:, :, 0:D], acc[:, ds(it * TG, TG), :]).then_inc(sp2.done, 1)
                dve.wait_ge(stored, 1 + it * 16)
                sp2.dve_last(dve, PRE[:, :, D:wide], sp2.ex[:, :, D:wide], ROW[:]).then_inc(sp2.done, 1)

            features(0)
            with dve.Fori(0, NTG - 1) as it:
                features(it + 1)
                rows(it)
            rows(NTG - 1)

        @block.tensor
        def _(pe):
            pe.wait_ge(w_in, 1 + 32)
            with pe.Fori(0, NTG) as it:
                def free(u):
                    return it * TG if u < 2 else it * TG + u - 1
                for u in range(TG):
                    pe.wait_ge(sp1.done, 1 + it + 1)
                    pe.wait_ge(turned_out, 1 + free(u))
                    for s in range(kc):
                        ins = pe.transpose(psT[:, u % 2, s * P:(s + 1) * P], XP[:, u, s * P:(s + 1) * P], k.ident[:])
                    ins.then_inc(turned, 1)
                for u in range(TG):
                    pe.wait_ge(turned_out, 1 + it * TG + u + 1)
                    pe.wait_ge(pre_out, 1 + free(u))
                    for s in range(kc):
                        pe.matmul(psH[:, u % 2, :], XS[:, u, s, :], W[:, s, :], start=(s == 0), stop=False)
                    pe.matmul(psH[:, u % 2, :], k.ones[0:1, :], B[:], start=False, stop=True).then_inc(made, 1)

        @block.scalar
        def _(act):
            def turn(it):
                for u in range(TG):
                    act.wait_ge(turned, 1 + it * TG + u + 1)
                    act.wait_ge(made, 1 + it * TG)
                    act.activation(XS[:, u, :, :], psT[:, u % 2, 0:D].rearrange("p (k q) -> p k q", q=P), ACT.Copy)\
                       .then_inc(turned_out, 1)

            def rows(it):
                act.wait_ge(sp2.done, 1 + it * 2)
                for u in range(TG):
                    act.wait_ge(made, 1 + it * TG + u + 1)
                    act.activation(PRE[:, u, :], psH[:, u % 2, :], ACT.Copy).then_inc(pre_out, 1)
                sp2.act_part(act, it)

            norm.act_root(act, 0)
            sp1.act_part(act, 0)
            with act.Fori(0, NTG - 1) as it:
                norm.act_root(act, it + 1)
                turn(it)
                sp1.act_part(act, it + 1)
                rows(it)
            turn(NTG - 1)
            rows(NTG - 1)


def edge_filter(nc, k, tag, table, records, gt, other, local, tile_of, acc):
    nf = gt.shape[0]
    n_loop = tile_of.shape[1] // U - 1
    by_part = records.rearrange("(p c) w -> p c w", p=P)
    with stage(nc, tag) as st:
        IDX = st.sb("IDX", [P, U, G], I32)
        ROWS = st.sb("ROWS", [P, U, G, D])
        S = st.sb("S", [P, U, G, P])
        FE = st.sb("FE", [P, U, G, nf], I32)
        FT = st.sb("FT", [nf, U, G, P])
        GT = st.sb("GT", [nf, D])
        psF = st.ps("psF", [P, 2, 512])
        psM = st.ps("psM", [P, 2, 512])
        psO = st.ps("psO", [P, 2, 512])
        q = {s: st.sem(s) for s in ("g_in", "idx_made", "sel", "attr_t", "attr_out", "filtered", "scaled",
                                    "summed", "kept")}
        gathered = [[st.gather_sem(f"gathered{u}_{i}") for i in range(G)] for u in range(U)]
        attr_in = [st.sem(f"attr_in{u}") for u in range(U)]
        block = st.block()

        @block.sync
        def _(sp):
            sp.dma_start(GT[:], gt).then_inc(q["g_in"], 16)

            def load(it, j):
                g, v = it * U + j, j % U
                need(sp, q["attr_t"], it, j - (U - 1))
                sp.dma_start(FE[:, v, :, :], by_part[:, ds(g * G, G), 2:2 + nf]).then_inc(attr_in[v], 16)

            for j in range(U):
                load(0, j)
            with sp.Fori(0, n_loop) as it:
                for j in range(U):
                    load(it, j + U)
            for v in range(U):
                sp.wait_ge(attr_in[v], 1 + 16 * (n_loop + 1))

        @block.gpsimd
        def _(pool):
            def gather(it, j):
                g, v = it * U + j, j % U
                pool.wait_ge(q["idx_made"], 1 + g + 1)
                need(pool, q["summed"], it, j - (U - 1))
                pool.nop(nofuse=True)
                for i in range(G):
                    pool.indirect_dma_start(out=ROWS[:, v, i, :], out_offset=None, in_=table,
                                            in_offset=bass.IndirectOffsetOnAxis(ap=IDX[:, v, i:i + 1], axis=0))\
                        .then_inc(gathered[v][i], 16)

            for j in range(U):
                gather(0, j)
            with pool.Fori(0, n_loop) as it:
                for j in range(U):
                    gather(it, j + U)

        @block.scalar
        def _(act):
            def index(it, j):
                g, v, n = it * U + j, j % U, it + j // U
                for i in range(G):
                    if not isinstance(n, int) or n > 0:
                        act.wait_ge(gathered[v][i], n * 16)
                act.activation(IDX[:, v, :], other[:, ds(g * G, G)], ACT.Copy).then_inc(q["idx_made"], 1)

            def turn(it, j):
                g, v = it * U + j, j % U
                act.wait_ge(q["attr_t"], 1 + g + 1)
                need(act, q["filtered"], it, j - (U - 1))
                act.activation(FT[:, v, :, :], psF[0:nf, v % 2, 0:G * P].rearrange("p (i n) -> p i n", n=P), ACT.Copy)\
                   .then_inc(q["attr_out"], 1)

            def body(it, j):
                ahead(turn, it, j + 4)
                ahead(index, it, j + U)

            for j in range(-U, 0):
                body(0, j)
            with act.Fori(0, n_loop) as it:
                for j in range(U):
                    body(it, j)

        @block.tensor
        def _(pe):
            pe.wait_ge(q["g_in"], 1 + 16)

            def add_up(it, j):
                g, v = it * U + j, j % U
                pe.wait_ge(q["scaled"], 1 + g + 1)
                need(pe, q["kept"], it, j - 1)
                for i in range(G):
                    ins = pe.matmul(psO[:, v % 2, 0:D], S[:, v, i, :], ROWS[:, v, i, :],
                                    start=(i == 0), stop=(i == G - 1))
                ins.then_inc(q["summed"], 1)

            def filt(it, j):
                g, v = it * U + j, j % U
                pe.wait_ge(q["attr_out"], 1 + g + 1)
                need(pe, q["scaled"], it, j - 1)
                for i in range(G):
                    ins = pe.matmul(psM[:, v % 2, i * D:(i + 1) * D], FT[:, v, i, :], GT[:], start=True, stop=True)
                ins.then_inc(q["filtered"], 1)

            def turn(it, j):
                g, v, n = it * U + j, j % U, it + j // U + 1
                pe.wait_ge(attr_in[v], 1 + n * 16)
                need(pe, q["attr_out"], it, j - 1)
                pe.nop(nofuse=True)
                for i in range(G):
                    ins = pe.transpose(psF[0:nf, v % 2, i * P:(i + 1) * P], FE[:, v, i, :].bitcast(F32), k.ident[:])
                ins.then_inc(q["attr_t"], 1)

            def body(it, j):
                ahead(turn, it, j + 4)
                ahead(filt, it, j + 2)
                ahead(add_up, it, j + 1)

            for j in range(-U, 0):
                body(0, j)
            with pe.Fori(0, n_loop) as it:
                for j in range(U):
                    body(it, j)

        @block.vector
        def _(dve):
            def scale_rows(it, j):
                g, v, n = it * U + j, j % U, it + j // U + 1
                dve.wait_ge(q["filtered"], 1 + g + 1)
                for i in range(G):
                    dve.wait_ge(gathered[v][i], n * 16)
                r = ROWS[:, v, :, :].rearrange("p i d -> p (i d)")
                dve.tensor_tensor(r, psM[:, v % 2, :], r, ALU.mult).then_inc(q["scaled"], 1)

            def keep_sum(it, j, tile):
                g, v = it * U + j, j % U
                dve.wait_ge(q["summed"], 1 + g + 1)
                need(dve, q["kept"], it, j)
                a = acc[:, ds(tile, 1), :].squeeze(1)
                dve.tensor_tensor(a, psO[:, v % 2, 0:D], a, ALU.add).then_inc(q["kept"], 1)

            def select(it, j):
                g, v = it * U + j, j % U
                need(dve, q["summed"], it, j - (U - 1))
                dve.tensor_tensor(S[:, v, :, :], k.iota[:].unsqueeze(1).broadcast_to([P, G, P]),
                                  local[:, ds(g * G, G)].unsqueeze(2).broadcast_to([P, G, P]), ALU.is_equal)\
                   .then_inc(q["sel"], 1)

            def body(it, j, tile):
                ahead(scale_rows, it, j + 1)
                ahead(keep_sum, it, j, tile)
                ahead(select, it, j + 5)

            for j in range(-U, 0):
                body(0, j, None)
            with dve.Fori(0, n_loop) as it:
                tiles = tile_ids(nc, mybir.EngineType.DVE, tile_of, it * U)
                for j in range(U):
                    body(it, j, tiles[j])
            for v in range(U):
                for i in range(G):
                    dve.wait_ge(gathered[v][i], 16 * (n_loop + 1))


def residual_blocks(nc, k, tag, acc, VT, r1, b1, r2, b2):
    kc = D // P
    nb = r1.shape[0]
    with stage(nc, tag) as st:
        R1, R2 = st.sb("R1", [P, nb, kc, D]), st.sb("R2", [P, nb, kc, D])
        B1, B2 = st.sb("B1", [P, nb, kc]), st.sb("B2", [P, nb, kc])
        PRE = st.sb("PRE", [P, kc, TOK])
        HS = st.sb("HS", [P, kc, TOK])
        soft = Softplus(st, "s", [P, kc, TOK])
        w_in, turned, turned_out, made, pre_out, out_made, updated = (
            st.sem(s) for s in ("w_in", "turned", "turned_out", "made", "pre_out", "out_made", "updated"))
        psA = st.ps("psA", [P, kc, 2, 512])
        psB = st.ps("psB", [P, kc, 2, 512])
        block = st.block()

        @block.sync
        def _(sp):
            sp.dma_start(R1[:], r1.rearrange("b (k p) c -> p b k c", p=P)).then_inc(w_in, 16)
            sp.dma_start(R2[:], r2.rearrange("b (k p) c -> p b k c", p=P)).then_inc(w_in, 16)
            sp.dma_start(B1[:], b1.rearrange("b p k -> p b k")).then_inc(w_in, 16)
            sp.dma_start(B2[:], b2.rearrange("b p k -> p b k")).then_inc(w_in, 16)
            sp.wait_ge(w_in, 1 + 64)

        @block.tensor
        def _(pe):
            for t in range(NT):
                if t >= 4:
                    pe.wait_ge(turned_out, 1 + t - 3)
                for s in range(kc):
                    ins = pe.transpose(psA[:, (t // 2) % 2, t % 2, s * P:(s + 1) * P], acc[:, t, s * P:(s + 1) * P],
                                       k.ident[:])
                ins.then_inc(turned, 1)
            pe.wait_ge(w_in, 1 + 64)
            pe.wait_ge(turned_out, 1 + NT)

            def first(b, g):
                n = b * NTG + g
                if b:
                    pe.wait_ge(updated, 1 + (n - NTG) * kc + kc)
                for c in range(kc):
                    if b or not isinstance(g, int) or g:
                        pe.wait_ge(pre_out, 1 + (n - 1) * kc + c + 1)
                    for half in range(2):
                        for i in range(kc):
                            ins = pe.matmul(psA[:, c, half, 0:HALF], R1[:, b, i, c * P:(c + 1) * P],
                                            VT[:, i, ds(g * TOK + half * HALF, HALF)],
                                            start=(i == 0), stop=(i == kc - 1))
                    ins.then_inc(made, 1)

            def second(b, g):
                n = b * NTG + g
                pe.wait_ge(soft.done, 1 + n + 1)
                if b or not isinstance(g, int):
                    pe.wait_ge(updated, 1 + n * kc)
                for c in range(kc):
                    for half in range(2):
                        for i in range(kc):
                            ins = pe.matmul(psB[:, c, half, 0:HALF], R2[:, b, i, c * P:(c + 1) * P],
                                            HS[:, i, half * HALF:(half + 1) * HALF], start=(i == 0), stop=(i == kc - 1))
                    ins.then_inc(out_made, 1)

            for b in range(nb):
                first(b, 0)
                with pe.Fori(0, NTG - 1) as g:
                    first(b, g + 1)
                    second(b, g)
                second(b, NTG - 1)

        @block.scalar
        def _(act):
            for t in range(NT):
                act.wait_ge(turned, 1 + t + 1)
                act.activation(VT[:, :, t * P:(t + 1) * P],
                               psA[:, (t // 2) % 2, t % 2, 0:D].rearrange("p (k q) -> p k q", q=P), ACT.Copy)\
                   .then_inc(turned_out, 1)
            act.wait_ge(w_in, 1 + 64)

            def part(b, g):
                n = b * NTG + g
                for c in range(kc):
                    act.wait_ge(made, 1 + n * kc + c + 1)
                    if b or not isinstance(g, int) or g:
                        act.wait_ge(soft.done, 1 + n)
                    act.activation(PRE[:, c, :].rearrange("p (a t) -> p a t", a=2), psA[:, c, :, 0:HALF],
                                   ACT.Identity, bias=B1[:, b, c:c + 1]).then_inc(pre_out, 1)
                soft.act_part(act, n)

            for b in range(nb):
                part(b, 0)
                with act.Fori(0, NTG - 1) as g:
                    part(b, g + 1)

        @block.vector
        def _(dve):
            dve.wait_ge(turned_out, 1 + NT)

            def first(b, g):
                n = b * NTG + g
                dve.wait_ge(pre_out, 1 + n * kc + kc)
                soft.dve_first(dve, PRE[:, :, :])

            def last(b, g):
                n = b * NTG + g
                dve.wait_ge(soft.has_log, 1 + n + 1)
                soft.dve_last(dve, PRE[:, :, :], soft.ex[:], HS[:, :, :]).then_inc(soft.done, 1)

            def update(b, g):
                n = b * NTG + g
                for c in range(kc):
                    dve.wait_ge(out_made, 1 + n * kc + c + 1)
                    v = VT[:, c, ds(g * TOK, TOK)].rearrange("p (a t) -> p a t", a=2)
                    dve.scalar_tensor_tensor(out=v, in0=psB[:, c, :, 0:HALF], scalar=B2[:, b, c:c + 1], in1=v,
                                             op0=ALU.add, op1=ALU.add).then_inc(updated, 1)

            for b in range(nb):
                first(b, 0)
                last(b, 0)
                with dve.Fori(0, NTG - 1) as g:
                    first(b, g + 1)
                    update(b, g)
                    last(b, g + 1)
                update(b, NTG - 1)
            dve.wait_ge(updated, 1 + nb * NTG * kc)


def project_out(nc, k, tag, VT, w, b):
    kc = D // P
    with stage(nc, tag) as st:
        W = st.sb("W", [P, kc, D])
        B = st.sb("B", [1, D])
        Z = [st.sb(f"Z{s}", [P, kc, TOK]) for s in range(2)]
        soft = [Softplus(st, f"s{s}", [P, kc, TOK]) for s in range(2)]
        psO = st.ps("psO", [P, 4, 512])
        w_in, made, kept = (st.sem(s) for s in ("w_in", "made", "kept"))
        block = st.block()

        @block.sync
        def _(sp):
            sp.dma_start(W[:], w.rearrange("(k p) c -> p k c", p=P)).then_inc(w_in, 16)
            sp.dma_start(B[:], b.unsqueeze(0)).then_inc(w_in, 16)

        @block.scalar
        def _(act):
            for g in range(NTG):
                soft[g % 2].act_part(act, g // 2)

        @block.vector
        def _(dve):
            def first(g):
                if g >= 2:
                    dve.wait_ge(soft[g % 2].has_exp, 1 + g // 2)
                soft[g % 2].dve_first(dve, VT[:, :, g * TOK:(g + 1) * TOK])

            def last(g):
                s = soft[g % 2]
                dve.wait_ge(s.has_log, 1 + g // 2 + 1)
                if g >= 2:
                    dve.wait_ge(made, 1 + (g - 1) * TG)
                s.dve_last(dve, VT[:, :, g * TOK:(g + 1) * TOK], s.ex[:], Z[g % 2][:]).then_inc(s.done, 1)

            def add(g):
                for t in range(g * TG, (g + 1) * TG):
                    dve.wait_ge(made, 1 + t + 1)
                    dve.tensor_tensor(k.X[:, t, :], k.X[:, t, :], psO[:, t % 4, 0:D], ALU.add).then_inc(kept, 1)

            first(0)
            first(1)
            for g in range(NTG):
                last(g)
                if g + 2 < NTG:
                    first(g + 2)
                if g:
                    add(g - 1)
            add(NTG - 1)
            dve.wait_ge(kept, 1 + NT)

        @block.tensor
        def _(pe):
            pe.wait_ge(w_in, 1 + 32)
            for g in range(NTG):
                pe.wait_ge(soft[g % 2].done, 1 + g // 2 + 1)
                for u in range(TG):
                    t = g * TG + u
                    if t >= 4:
                        pe.wait_ge(kept, 1 + t - 3)
                    for i in range(kc):
                        pe.matmul(psO[:, t % 4, 0:D], Z[g % 2][:, i, u * P:(u + 1) * P], W[:, i, :],
                                  start=(i == 0), stop=False)
                    pe.matmul(psO[:, t % 4, 0:D], k.ones[0:1, :], B[:], start=False, stop=True).then_inc(made, 1)


def expert_scores(nc, k, tag, acc, na, bias, gamma, beta, scores):
    f1 = acc.shape[2] // na
    hd = f1 - 1
    nf = na * hd
    whole = [P, NT, nf]
    with stage(nc, tag) as st:
        rows = st.sb("rows", [P, 3, nf])
        rec, m, v, sd, rs = (st.sb(n, [P, NT]) for n in ("rec", "m", "v", "sd", "rs"))
        den = st.sb("den", [P, NT, na])
        h, c2 = st.sb("h", whole), st.sb("c2", whole)
        in_, order, root = (st.sem(s) for s in ("in", "order", "root"))
        at_var = []
        block = st.block()

        @block.sync
        def _(sp):
            for n, r in enumerate((bias, gamma, beta)):
                sp.dma_start(rows[:, n, :], r.partition_broadcast(P)).then_inc(in_, 16)

        @block.vector
        def _(dve):
            at = [0]

            def then(ins):
                at[0] += 1
                ins.then_inc(order, 1)
                dve.wait_ge(order, 1 + at[0])

            view = acc.rearrange("p t (h f) -> p t h f", f=f1)
            h4 = h[:].rearrange("p t (h f) -> p t h f", f=hd)
            dve.wait_ge(in_, 1 + 48)
            then(dve.tensor_scalar(den[:], view[:, :, :, hd], 1e-16, None, ALU.add))
            then(dve.reciprocal(den[:], den[:]))
            for a in range(na):
                ins = dve.tensor_tensor(h4[:, :, a, :], view[:, :, a, 0:hd],
                                        den[:, :, a:a + 1].broadcast_to([P, NT, hd]), ALU.mult)
            then(ins)
            then(dve.tensor_tensor(h[:], h[:], rows[:, 0:1, :].broadcast_to(whole), ALU.add))
            then(dve.tensor_reduce(m[:], h[:], AX.X, ALU.add))
            then(dve.scalar_tensor_tensor(out=h[:], in0=m[:].unsqueeze(2).broadcast_to(whole), scalar=-1.0 / nf,
                                          in1=h[:], op0=ALU.mult, op1=ALU.add))
            then(dve.tensor_tensor(c2[:], h[:], h[:], ALU.mult))
            then(dve.tensor_reduce(rec[:], c2[:], AX.X, ALU.add))
            then(dve.tensor_scalar(v[:], rec[:], 1.0 / nf, LN_EPS, ALU.mult, ALU.add))
            at_var.append(at[0])
            dve.wait_ge(root, 1 + 1)
            then(dve.reciprocal(rs[:], sd[:]))
            then(dve.tensor_tensor(h[:], h[:], rs[:].unsqueeze(2).broadcast_to(whole), ALU.mult))
            then(dve.tensor_tensor(h[:], h[:], rows[:, 1:2, :].broadcast_to(whole), ALU.mult))
            then(dve.tensor_tensor(h[:], h[:], rows[:, 2:3, :].broadcast_to(whole), ALU.add))
            then(dve.tensor_reduce(scores, h[:].rearrange("p t (h f) -> p t f h", f=hd), AX.X, ALU.add))
            then(dve.tensor_scalar(scores, scores, 1.0 / na, None, ALU.mult))

        @block.scalar
        def _(act):
            act.wait_ge(order, 1 + at_var[0])
            act.activation(sd[:], v[:], ACT.Sqrt).then_inc(root, 1)


def program(nc, a, out, upto=99):
    with ExitStack() as ctx:
        k = Consts()

        def sb(name, shape, dt=F32):
            return ctx.enter_context(nc.sbuf_tensor(name, shape, dt))

        k.X = sb("X", [P, NT, D])
        k.ident = sb("ident", [P, P])
        k.tri = sb("tri", [P, P])
        k.ones = sb("ones", [P, P])
        k.iota = sb("iota", [P, P])
        k.past_end = sb("past_end", [P, 1])
        setup(nc, k, a["x"])
        n_groups = groups_of(a["src"].shape[0] * a["src"].shape[1])
        cols = n_groups * G
        rw = 2 + a["attr"].shape[2]
        by_src = [sb("src_other", [P, cols], I32), sb("src_local", [P, cols]), sb("src_tile", [1, n_groups], I32)]
        by_dst = [sb("dst_other", [P, cols], I32), sb("dst_local", [P, cols]), sb("dst_tile", [1, n_groups], I32)]
        rg = groups_of(a["rdst"].shape[0] * a["rdst"].shape[1])
        rcols = rg * G
        r_tile = sb("r_tile", [1, rg], I32)
        src_table = nc.dram_tensor("src_table", (P * cols, rw), I32, kind="Internal").ap()
        dst_table = nc.dram_tensor("dst_table", (P * cols, 2), I32, kind="Internal").ap()
        rtable = nc.dram_tensor("router_table", (P * rcols, 2), I32, kind="Internal").ap()
        pb, m = a["src"].shape
        rb, rm = a["rdst"].shape
        S = [t[:] for t in by_src]
        late = ExitStack()
        dst_row, r_row = (late.enter_context(nc.sbuf_tensor(n, s, I32)) for n, s in
                          (("dst_row", [pb, m]), ("r_row", [rb, rm])))
        dst_rec, r_rec = (late.enter_context(nc.sbuf_tensor(n, s, I32)) for n, s in
                          (("dst_rec", [pb, m, 2]), ("r_rec", [rb, rm, 2])))
        table0 = nc.dram_tensor("table0", (NP, 260), F32, kind="Internal").ap()
        with nc.sbuf_tensor("near0", [P, NT, 4], F32) as near, ExitStack() as acc_at:
            with nc.sbuf_tensor("src_row", [pb, m], I32) as row, nc.sbuf_tensor("src_rec", [pb, m, rw], I32) as rec:
                place_edges(nc, k, "os", a["src"], a["dst"], a["attr"], src_table, row[:], rec[:], by_src[2][:])
                def part(start, end):
                    return [(row[:], rec[:], src_table, start, end)]
                cuts = [0, 80, 144, 224, m]
                place_edges(nc, k, "od", a["dst"], a["src"], None, dst_table, dst_row[:], dst_rec[:], by_dst[2][:],
                            jobs=part(cuts[0], cuts[1]))
                place_edges(nc, k, "or", a["rdst"], a["rsrc"], None, rtable, r_row[:], r_rec[:], r_tile[:],
                            jobs=part(cuts[1], cuts[2]))
                make_table(nc, k, "t0", a["W0"], a["a0f"], a["a0n"], table0, near[:], guard=True,
                           jobs=part(cuts[2], cuts[3]))
                scatter_edges(nc, "os_rest", part(cuts[3], cuts[4]))
            read_slots(nc, "os_read", src_table, *S[0:2])
            if upto >= 1:
                acc = acc_at.enter_context(nc.sbuf_tensor("acc0", [P, NT, 260], F32))
                edge_pass(nc, k, "e0", table0, *S, near[:], acc[:], guard=True)
                finish_attention(nc, k, "f0", acc[:], 4, 64, 2, True)
        late_jobs = [(dst_row[:], dst_rec[:], dst_table, 0, m), (r_row[:], r_rec[:], rtable, 0, rm)]
        if upto >= 2:
            with (nc.sbuf_tensor("XT1", [P, D // P, NP], F32) as XT, nc.sbuf_tensor("logits1", [P, NT, 6], F32) as lg,
                  nc.sbuf_tensor("gates1", [P, 6, NT], F32) as gates):
                tokens(nc, k, "k1", XT[:], lg[:], a["rw2"], a["rb2"], hidden=(a["rw1"], a["rb1"]))
                choose(nc, k, "c1", lg[:], gates[:], probs=True, renorm=False)
                feed_forward(nc, k, "m1", XT[:], a["ew1"], a["eb1"], a["ew3"], a["eb3"], gates[:], ACT.Relu,
                             mid=(a["ew2"], a["eb2"]), jobs=late_jobs[:1])
        else:
            scatter_edges(nc, "late_dst", late_jobs[:1])
        if upto >= 3:
            with nc.sbuf_tensor("acc2", [P, NT, 258], F32) as acc, nc.sbuf_tensor("near2", [P, NT, 2], F32) as near:
                table = nc.dram_tensor("table2", (NP, 258), F32, kind="Internal").ap()
                make_table(nc, k, "t2", a["W1"], a["a1f"], a["a1n"], table, near[:], bias=a["b1"])
                edge_pass(nc, k, "e2", table, *S, near[:], acc[:])
                finish_attention(nc, k, "f2", acc[:], 2, 128, 1, False)
        if upto >= 4:
            ne = a["mW1"].shape[0]
            n_groups = -(-((2 * NP + ne * (SG - 1)) // SG) // 2) * 2
            rows3 = nc.dram_tensor("rows3", (n_groups * SG + P, D), F32, kind="Internal").ap()
            results3 = nc.dram_tensor("results3", (n_groups * SG, D), F32, kind="Internal").ap()
            with (nc.sbuf_tensor("gates3", [P, 8, NT], F32) as gates, nc.sbuf_tensor("slot3", [P, 2, NT], I32) as slot,
                  nc.sbuf_tensor("weight3", [P, 2, NT], F32) as weight,
                  nc.sbuf_tensor("expert3", [1, n_groups + 2], I32) as expert_of):
                with (nc.sbuf_tensor("XR3", [P, NT, D], F32) as XR, nc.sbuf_tensor("logits3", [P, NT, 8], F32) as lg):
                    tokens(nc, k, "k3", None, lg[:], a["Wr"], a["br"], rows=XR[:])
                    choose(nc, k, "c3", lg[:], gates[:], probs=True, renorm=True)
                    place_tokens(nc, k, "pt3", gates[:], slot[:], weight[:], expert_of[:], rows3)
                    send_tokens(nc, "st3", XR[:], slot[:], weight[:], rows3)
                expert_groups(nc, k, "m3", rows3, results3, expert_of[:], a["mW1"], a["mb1"], a["mW2"], a["mb2"],
                              a["affine"],
                              ACT.Gelu, jobs=late_jobs[1:])
                take_results(nc, k, "tr3", results3, slot[:], weight[:])
        else:
            scatter_edges(nc, "late_r", late_jobs[1:])
        late.close()
        if upto >= 5:
            with (nc.sbuf_tensor("acc4", [P, NT, D + 1], F32) as acc, nc.sbuf_tensor("near4", [P, NT, 1], F32) as near,
                  nc.sbuf_tensor("shift4", [P, 1], F32) as shift,
                  nc.sbuf_tensor("base4", [P, NT, 1], F32) as base, nc.sbuf_tensor("h4", [P, NT, D], F32) as h4):
                read_slots(nc, "od_read", dst_table, by_dst[0][:], by_dst[1][:])
                soft = (shift[:], base[:])
                for r in range(2):
                    table = nc.dram_tensor(f"table4_{r}", (NP, D + 1), F32, kind="Internal").ap()
                    make_table(nc, k, f"t4{r}", a["W2"][r], a["a2f"][r], a["a2n"][r], table, near[:], acc[:],
                               softmax=soft, plain=h4[:] if r else None)
                    edge_pass(nc, k, f"e4{r}", table, *(t[:] for t in by_dst), near[:], acc[:], softmax=soft)
                    finish_conv(nc, k, f"f4{r}", acc[:], a["b2"][r], h4[:] if r == 0 else k.X[:], r == 0, r == 1)
        if upto >= 6:
            with (nc.sbuf_tensor("XT5", [P, D // P, NP], F32) as XT, nc.sbuf_tensor("score5", [P, NT, 1], F32) as sc,
                  nc.sbuf_tensor("gates5", [P, 1, NT], F32) as gates):
                tokens(nc, k, "k5", XT[:], sc[:], a["wr"], a["br5"], keep=True)
                pick_tokens(nc, k, "p5", sc[:].squeeze(2), gates[:].squeeze(1), N // 2 - 1)
                feed_forward(nc, k, "m5", XT[:], a["fw1"], a["fb1"], a["fw2"], a["fb2"], gates[:], ACT.Gelu_apprx_tanh)
        if upto >= 7:
            with nc.sbuf_tensor("acc6", [P, NT, D], F32) as acc, nc.sbuf_tensor("VT6", [P, D // P, NP], F32) as VT:
                table = nc.dram_tensor("table6", (NP, D), F32, kind="Internal").ap()
                atom_tables(nc, k, "t6", a["Wij"], a["bij"], table, acc[:])
                edge_filter(nc, k, "e6", table, src_table, a["GT"], *S, acc[:])
                residual_blocks(nc, k, "r6", acc[:], VT[:], a["res1"], a["resb1"], a["res2"], a["resb2"])
                project_out(nc, k, "o6", VT[:], a["Wv"], a["bv"])
        if upto >= 8:
            with (nc.sbuf_tensor("sc7", [P, NT, 4], F32) as scores, nc.sbuf_tensor("gates7", [P, 4, NT], F32) as gates):
                with (nc.sbuf_tensor("acc7", [P, NT, 20], F32) as acc, nc.sbuf_tensor("near7", [P, NT, 4], F32) as near,
                      nc.sbuf_tensor("shift7", [P, 4], F32) as shift,
                      nc.sbuf_tensor("base7", [P, NT, 4], F32) as base, nc.sbuf_tensor("r_other", [P, rcols], I32) as ro,
                      nc.sbuf_tensor("r_local", [P, rcols], F32) as rl):
                    read_slots(nc, "or_read", rtable, ro[:], rl[:])
                    soft = (shift[:], base[:])
                    table = nc.dram_tensor("table7", (NP, 20), F32, kind="Internal").ap()
                    make_table(nc, k, "t7", a["W3"], a["a3f"], a["a3n"], table, near[:], acc[:], softmax=soft)
                    edge_pass(nc, k, "e7", table, ro[:], rl[:], r_tile[:], near[:], acc[:], softmax=soft)
                    expert_scores(nc, k, "s7", acc[:], 4, a["gb"], a["lg"], a["lb"], scores[:])
                choose(nc, k, "c7", scores[:], gates[:], probs=False, renorm=False)
                with nc.sbuf_tensor("XT7", [P, D // P, NP], F32) as XT:
                    tokens(nc, k, "k7", XT[:])
                    feed_forward(nc, k, "m7", XT[:], a["xw1"], a["xb1"], a["xw2"], a["xb2"], gates[:], ACT.Gelu)
        with stage(nc, "out") as st:
            stored = st.sem("stored")
            block = st.block()

            @block.sync
            def _(sp):
                full = (NT - 1) * P
                sp.dma_start(out[0:full, :].rearrange("(t p) d -> p t d", p=P), k.X[:, 0:NT - 1, :]).then_inc(stored, 16)
                sp.dma_start(out[full:N, :], k.X[0:REST, NT - 1, :]).then_inc(stored, 16)
                sp.wait_ge(stored, 1 + 32)


def layout(inputs):
    import numpy as np

    def arr(x):
        return np.ascontiguousarray(x)

    def chunks(x):
        return np.ascontiguousarray(x.reshape(x.shape[0], -1, P).transpose(0, 2, 1))

    i = {n: np.asarray(v) for n, v in inputs.items()}
    e = i["src"].shape[0]
    m = e // 125
    a0, a1 = i["L0_gnn_a"], i["L1_gnn_a"]
    return {
        "x": arr(i["x"]),
        "src": arr(i["src"].reshape(125, m)),
        "dst": arr(i["dst"].reshape(125, m)),
        "attr": arr(i["edge_attr_64"].reshape(125, m, 64).view(np.int32)),
        "W0": arr(i["L0_gnn_W"].transpose(1, 0, 2).reshape(D, D)),
        "a0n": arr(a0[:, 0, :64].reshape(-1)),
        "a0f": arr(a0[:, 0, 64:].reshape(-1)),
        "rw1": arr(i["L0_ffn_router_w1"]),
        "rb1": arr(i["L0_ffn_router_b1"]),
        "rw2": arr(i["L0_ffn_router_w2"]),
        "rb2": arr(i["L0_ffn_router_b2"]),
        "ew1": arr(i["L0_ffn_expert_w1"]),
        "eb1": chunks(i["L0_ffn_expert_b1"]),
        "ew2": arr(i["L0_ffn_expert_w2"]),
        "eb2": chunks(i["L0_ffn_expert_b2"]),
        "ew3": arr(i["L0_ffn_expert_w3"]),
        "eb3": arr(i["L0_ffn_expert_b3"]),
        "W1": arr(i["L1_gnn_W"].transpose(2, 0, 1).reshape(D, D)),
        "b1": arr(i["L1_gnn_b"].reshape(-1)),
        "a1n": arr(a1[:, :128].reshape(-1)),
        "a1f": arr(a1[:, 128:].reshape(-1)),
        "Wr": arr(i["L1_ffn_Wr"]),
        "br": arr(i["L1_ffn_br"]),
        "affine": arr(np.stack([chunks(i["L1_ffn_ln_g"]), chunks(i["L1_ffn_ln_b"])], 2)),
        "mW1": arr(i["L1_ffn_W1"]),
        "mb1": chunks(i["L1_ffn_b1"]),
        "mW2": arr(i["L1_ffn_W2"]),
        "mb2": arr(i["L1_ffn_b2"]),
        "W2": arr(i["L2_gnn_W"]),
        "a2f": arr(i["L2_gnn_attn_l"]),
        "a2n": arr(i["L2_gnn_attn_r"]),
        "b2": arr(i["L2_gnn_bias"]),
        "wr": arr(i["L2_ffn_wr"]),
        "br5": arr(i["L2_ffn_br"]),
        "fw1": arr(i["L2_ffn_w1"][None]),
        "fb1": chunks(i["L2_ffn_b1"][None]),
        "fw2": arr(i["L2_ffn_w2"][None]),
        "fb2": arr(i["L2_ffn_b2"][None]),
        "Wij": arr(np.concatenate([i["L3_gnn_Wi"].T, i["L3_gnn_Wj"].T], 1)),
        "bij": arr(np.concatenate([i["L3_gnn_bi"], i["L3_gnn_bj"]])),
        "GT": arr(i["L3_gnn_G"].T),
        "res1": arr(i["L3_gnn_res_w1"].transpose(0, 2, 1)),
        "resb1": chunks(i["L3_gnn_res_b1"]),
        "res2": arr(i["L3_gnn_res_w2"].transpose(0, 2, 1)),
        "resb2": chunks(i["L3_gnn_res_b2"]),
        "Wv": arr(i["L3_gnn_Wv"].T),
        "bv": arr(i["L3_gnn_bv"]),
        "rsrc": arr(i["L3_ffn_edge_index"][0].reshape(128, -1)),
        "rdst": arr(i["L3_ffn_edge_index"][1].reshape(128, -1)),
        "W3": arr(i["L3_ffn_W_gat"]),
        "a3f": arr(i["L3_ffn_att_src"].reshape(-1)),
        "a3n": arr(i["L3_ffn_att_dst"].reshape(-1)),
        "gb": arr(i["L3_ffn_b_gat"]),
        "lg": arr(i["L3_ffn_ln_gamma"]),
        "lb": arr(i["L3_ffn_ln_beta"]),
        "xw1": arr(i["L3_ffn_W1"]),
        "xb1": chunks(i["L3_ffn_b1"]),
        "xw2": arr(i["L3_ffn_W2"]),
        "xb2": arr(i["L3_ffn_b2"]),
    }


def kernel(**inputs):
    import concourse.bacc as bacc
    from concourse.bass_utils import run_bass_kernel_spmd

    nc = bacc.Bacc("TRN2", target_bir_lowering=False, num_devices=1)
    arrays = {f"in_{name}": v for name, v in layout(inputs).items()}
    args = {name[3:]: nc.dram_tensor(name, v.shape, mybir.dt.from_np(v.dtype), kind="ExternalInput").ap()
            for name, v in arrays.items()}
    out = nc.dram_tensor("out", (N, D), F32, kind="ExternalOutput").ap()
    program(nc, args, out)
    return run_bass_kernel_spmd(nc, [arrays], core_ids=[0]).results[0]["out"]
```
